# Optimizing a Trainium2 kernel written in Bass

```python
import numpy as np
import jax
import jax.numpy as jnp

def _softmax(x, axis=-1):
    return jax.nn.softmax(x, axis=axis)

def _gelu(x):
    return jax.nn.gelu(x, approximate=True)

def _silu(x):
    return jax.nn.silu(x)

def _sigmoid(x):
    return jax.nn.sigmoid(x)

def _layernorm(x, axis=-1, eps=1e-05):
    m = jnp.mean(x, axis=axis, keepdims=True)
    v = jnp.var(x, axis=axis, keepdims=True)
    return (x - m) / jnp.sqrt(v + eps)

def _scatter_add(tgt, idx, src, axis=0):
    return tgt.at[idx].add(src)

def _segment_sum(src, seg, n):
    return jax.ops.segment_sum(src, seg, n)
kernel_name = 'mk_pixart_resid_d2_seqx_r8_7837e1'

def setup_inputs(seed: int=0):
    np.random.seed(seed)
    _w = jnp.asarray

    def _rec_inputs():
        import jax
        import jax.numpy as jnp
        _rk = jax.random.key(seed)
        x = -0.0002928 + 1 * jax.random.normal(jax.random.fold_in(_rk, 1), (16, 128, 128), jnp.float32)
        _lenS = 128 - jax.random.randint(jax.random.fold_in(_rk, 7), (16,), 0, max(1, 128 // 4) + 1, jnp.int32)
        _lenS2 = 77 - jax.random.randint(jax.random.fold_in(_rk, 8), (16,), 0, max(1, 77 // 4) + 1, jnp.int32)
        cond_1024 = 0.000887014 + 1.03683 * jax.random.normal(jax.random.fold_in(_rk, 11), (16, 128), jnp.float32)
        _ctx_1024P = jax.random.normal(jax.random.fold_in(_rk, 12), (16, 16, 128), jnp.float32)
        _ctx_1024c = jax.random.dirichlet(jax.random.fold_in(_rk, 512), 0.3 * jnp.ones((16,), jnp.float32), (16, 77))
        _ctx_1024t = jnp.einsum('bsk,bkd->bsd', _ctx_1024c, _ctx_1024P)
        _ctx_1024t = _ctx_1024t * jax.lax.rsqrt(jnp.mean(jnp.square(_ctx_1024t)) + 1e-12) * 0.953939
        ctx_1024 = -0.000761806 + 0.999296 * (_ctx_1024t + 0.3 * jax.random.normal(jax.random.fold_in(_rk, 612), (16, 77, 128), jnp.float32))
        return (x, cond_1024, ctx_1024)
    x, cond_1024, ctx_1024 = _rec_inputs()

    def _L0_xcond_setup():
        import jax, jax.numpy as jnp
        import numpy as np
        import math
        B, S, CTX, D, H, DH = (2, 256, 32, 128, 16, 64)
        INNER = H * DH
        DFF = 4 * D

        def layernorm(x, eps=1e-05):
            m = jnp.mean(x, axis=-1, keepdims=True)
            v = jnp.var(x, axis=-1, keepdims=True)
            return (x - m) * jax.lax.rsqrt(v + eps)

        def adaln(x, t, w, b):
            emb = t @ w + b
            scale, shift = jnp.split(emb, 2, axis=-1)
            return layernorm(x) * (1.0 + scale) + shift

        def mha(xq, ctx, wq, wk, wv, wo, bo):
            b, sq, _ = xq.shape
            sk = ctx.shape[1]
            q = (xq @ wq).reshape(b, sq, H, DH).transpose(0, 2, 1, 3)
            k = (ctx @ wk).reshape(b, sk, H, DH).transpose(0, 2, 1, 3)
            v = (ctx @ wv).reshape(b, sk, H, DH).transpose(0, 2, 1, 3)
            scores = jnp.einsum('bhqd,bhkd->bhqk', q, k) / math.sqrt(DH)
            attn = jax.nn.softmax(scores, axis=-1)
            out = jnp.einsum('bhqk,bhkd->bhqd', attn, v)
            out = out.transpose(0, 2, 1, 3).reshape(b, sq, INNER)
            return out @ wo + bo

        def glu_ff(x, w1, b1, w2, b2):
            u = x @ w1 + b1
            a, gate = jnp.split(u, 2, axis=-1)
            return a * jax.nn.gelu(gate, approximate=False) @ w2 + b2
        key = jax.random.key(seed)
        ks = jax.random.split(key, 24)
        s = 1.0 / math.sqrt(D)

        def n(k, shape, scale=1.0):
            return jax.random.normal(k, shape, dtype=jnp.float32) * scale
        return {'x': n(ks[0], (B, S, D)), 't': n(ks[1], (B, 1, D)), 'context': n(ks[2], (B, CTX, D)), 'attn1_wq': n(ks[3], (D, INNER), s), 'attn1_wk': n(ks[4], (D, INNER), s), 'attn1_wv': n(ks[5], (D, INNER), s), 'attn1_wo': n(ks[6], (INNER, D), s), 'attn1_bo': n(ks[7], (D,), 0.01), 'attn2_wq': n(ks[8], (D, INNER), s), 'attn2_wk': n(ks[9], (D, INNER), s), 'attn2_wv': n(ks[10], (D, INNER), s), 'attn2_wo': n(ks[11], (INNER, D), s), 'attn2_bo': n(ks[12], (D,), 0.01), 'ff_w1': n(ks[13], (D, 2 * DFF), s), 'ff_b1': n(ks[14], (2 * DFF,), 0.01), 'ff_w2': n(ks[15], (DFF, D), 1.0 / math.sqrt(DFF)), 'ff_b2': n(ks[16], (D,), 0.01), 'norm1_w': n(ks[17], (D, 2 * D), s), 'norm1_b': n(ks[18], (2 * D,), 0.01), 'norm2_w': n(ks[19], (D, 2 * D), s), 'norm2_b': n(ks[20], (2 * D,), 0.01), 'norm3_w': n(ks[21], (D, 2 * D), s), 'norm3_b': n(ks[22], (2 * D,), 0.01)}
    _L0_xcond_all = _L0_xcond_setup()
    _L0_xcond_in = {k: v for k, v in _L0_xcond_all.items() if k in ('attn1_wq', 'attn1_wk', 'attn1_wv', 'attn1_wo', 'attn1_bo', 'attn2_wq', 'attn2_wk', 'attn2_wv', 'attn2_wo', 'attn2_bo', 'ff_w1', 'ff_b1', 'ff_w2', 'ff_b2', 'norm1_w', 'norm1_b', 'norm2_w', 'norm2_b', 'norm3_w', 'norm3_b')}
    del _L0_xcond_all

    def _L0_ffn_setup():
        import jax, jax.numpy as jnp
        import numpy as np
        H, I, E_ROUTED, TOP_K = (128, 352, 7, 2)
        B, S = (4, 256)

        def _expert(h, g, u, d):
            return jnp.einsum('...i,hi->...h', jax.nn.silu(h @ g.T) * (h @ u.T), d)
        key = jax.random.key(seed)
        ks = jax.random.split(key, 10)
        sc = 0.02
        return {'x': jax.random.normal(ks[0], (B, S, H), dtype=jnp.float32), 'sg': jax.random.normal(ks[1], (I, H), dtype=jnp.float32) * sc, 'su': jax.random.normal(ks[2], (I, H), dtype=jnp.float32) * sc, 'sd': jax.random.normal(ks[3], (H, I), dtype=jnp.float32) * sc, 'rg': jax.random.normal(ks[4], (E_ROUTED, I, H), dtype=jnp.float32) * sc, 'ru': jax.random.normal(ks[5], (E_ROUTED, I, H), dtype=jnp.float32) * sc, 'rd': jax.random.normal(ks[6], (E_ROUTED, H, I), dtype=jnp.float32) * sc, 'wr': jax.random.normal(ks[7], (E_ROUTED, H), dtype=jnp.float32) * sc, 'rb': jnp.zeros((E_ROUTED,), dtype=jnp.float32)}
    _L0_ffn_all = _L0_ffn_setup()
    _L0_ffn_in = {k: v for k, v in _L0_ffn_all.items() if k in ('sg', 'su', 'sd', 'rg', 'ru', 'rd', 'wr', 'rb')}
    del _L0_ffn_all

    def _L1_xcond_setup():
        import jax, jax.numpy as jnp
        import numpy as np
        B, N, K, D, T = (16, 512, 16, 128, 3)
        EPS_ATTN = 1e-08
        LN_EPS = 1e-05

        def _ln(x, g, b):
            mu = jnp.mean(x, axis=-1, keepdims=True)
            var = jnp.mean(jnp.square(x - mu), axis=-1, keepdims=True)
            return (x - mu) * jax.lax.rsqrt(var + LN_EPS) * g + b
        key = jax.random.key(seed)
        ks = jax.random.split(key, 16)
        w = lambda k, i, o: jax.random.normal(k, (i, o), jnp.float32) * 0.02
        inp = {'x_cls': jax.random.normal(ks[0], (B, D), jnp.float32), 'x': jax.random.normal(ks[1], (B, N, D), jnp.float32), 'noise': jax.random.normal(ks[2], (B, K, D), jnp.float32), 'q_mu': jax.random.normal(ks[3], (1, 1, D), jnp.float32), 'q_logsig': jax.random.normal(ks[4], (1, 1, D), jnp.float32) * 0.02, 'lnkv_g': jnp.ones((D,), jnp.float32), 'lnkv_b': jnp.zeros((D,), jnp.float32), 'lnq_g': jnp.ones((D,), jnp.float32), 'lnq_b': jnp.zeros((D,), jnp.float32), 'lnm_g': jnp.ones((D,), jnp.float32), 'lnm_b': jnp.zeros((D,), jnp.float32), 'lnp_g': jnp.ones((D,), jnp.float32), 'lnp_b': jnp.zeros((D,), jnp.float32), 'wk': w(ks[5], D, D), 'bk': jnp.zeros((D,), jnp.float32), 'wv': w(ks[6], D, D), 'bv': jnp.zeros((D,), jnp.float32), 'wq': w(ks[7], D, D), 'bq': jnp.zeros((D,), jnp.float32), 'wu': w(ks[8], D, D), 'bu': jnp.zeros((D,), jnp.float32), 'w1': w(ks[9], D, D), 'b1': jnp.zeros((D,), jnp.float32), 'w2': w(ks[10], D, D), 'b2': jnp.zeros((D,), jnp.float32)}
        return inp
    _L1_xcond_all = _L1_xcond_setup()
    _L1_xcond_in = {k: v for k, v in _L1_xcond_all.items() if k in ('q_mu', 'q_logsig', 'lnkv_g', 'lnkv_b', 'lnq_g', 'lnq_b', 'lnm_g', 'lnm_b', 'lnp_g', 'lnp_b', 'wk', 'bk', 'wv', 'bv', 'wq', 'bq', 'wu', 'bu', 'w1', 'b1', 'w2', 'b2')}
    del _L1_xcond_all

    def _L1_ffn_setup():
        import jax, jax.numpy as jnp
        import numpy as np
        D_MODEL = 128
        MLP_DIM = 512
        N_EXPERTS = 8
        B, T = (4, 128)
        key = jax.random.key(seed)
        ks = jax.random.split(key, 7)
        scale_in = (1.0 / D_MODEL) ** 0.5
        scale_out = (1.0 / MLP_DIM) ** 0.5
        bound_g = (1.0 / D_MODEL) ** 0.5
        w_gate = jax.random.uniform(ks[0], (D_MODEL, N_EXPERTS), minval=-bound_g, maxval=bound_g, dtype=jnp.float32)
        b_gate = jax.random.uniform(ks[1], (N_EXPERTS,), minval=-bound_g, maxval=bound_g, dtype=jnp.float32)
        W1 = jax.random.uniform(ks[2], (N_EXPERTS, D_MODEL, MLP_DIM), minval=-scale_in, maxval=scale_in, dtype=jnp.float32)
        b1 = jnp.zeros((N_EXPERTS, MLP_DIM), dtype=jnp.float32)
        W2 = jax.random.uniform(ks[3], (N_EXPERTS, MLP_DIM, D_MODEL), minval=-scale_out, maxval=scale_out, dtype=jnp.float32)
        b2 = jnp.zeros((N_EXPERTS, D_MODEL), dtype=jnp.float32)
        x = jax.random.normal(ks[4], (B, T, D_MODEL), dtype=jnp.float32)
        return {'x': x, 'w_gate': w_gate, 'b_gate': b_gate, 'W1': W1, 'b1': b1, 'W2': W2, 'b2': b2}
    _L1_ffn_all = _L1_ffn_setup()
    _L1_ffn_in = {k: v for k, v in _L1_ffn_all.items() if k in ('w_gate', 'b_gate', 'W1', 'b1', 'W2', 'b2')}
    del _L1_ffn_all
    return {'x': x, 'cond_1024': cond_1024, 'ctx_1024': ctx_1024, 'L0_xcond_attn1_wq': _L0_xcond_in['attn1_wq'], 'L0_xcond_attn1_wk': _L0_xcond_in['attn1_wk'], 'L0_xcond_attn1_wv': _L0_xcond_in['attn1_wv'], 'L0_xcond_attn1_wo': _L0_xcond_in['attn1_wo'], 'L0_xcond_attn1_bo': _L0_xcond_in['attn1_bo'], 'L0_xcond_attn2_wq': _L0_xcond_in['attn2_wq'], 'L0_xcond_attn2_wk': _L0_xcond_in['attn2_wk'], 'L0_xcond_attn2_wv': _L0_xcond_in['attn2_wv'], 'L0_xcond_attn2_wo': _L0_xcond_in['attn2_wo'], 'L0_xcond_attn2_bo': _L0_xcond_in['attn2_bo'], 'L0_xcond_ff_w1': _L0_xcond_in['ff_w1'], 'L0_xcond_ff_b1': _L0_xcond_in['ff_b1'], 'L0_xcond_ff_w2': _L0_xcond_in['ff_w2'], 'L0_xcond_ff_b2': _L0_xcond_in['ff_b2'], 'L0_xcond_norm1_w': _L0_xcond_in['norm1_w'], 'L0_xcond_norm1_b': _L0_xcond_in['norm1_b'], 'L0_xcond_norm2_w': _L0_xcond_in['norm2_w'], 'L0_xcond_norm2_b': _L0_xcond_in['norm2_b'], 'L0_xcond_norm3_w': _L0_xcond_in['norm3_w'], 'L0_xcond_norm3_b': _L0_xcond_in['norm3_b'], 'L0_ffn_sg': _L0_ffn_in['sg'], 'L0_ffn_su': _L0_ffn_in['su'], 'L0_ffn_sd': _L0_ffn_in['sd'], 'L0_ffn_rg': _L0_ffn_in['rg'], 'L0_ffn_ru': _L0_ffn_in['ru'], 'L0_ffn_rd': _L0_ffn_in['rd'], 'L0_ffn_wr': _L0_ffn_in['wr'], 'L0_ffn_rb': _L0_ffn_in['rb'], 'L1_xcond_q_mu': _L1_xcond_in['q_mu'], 'L1_xcond_q_logsig': _L1_xcond_in['q_logsig'], 'L1_xcond_lnkv_g': _L1_xcond_in['lnkv_g'], 'L1_xcond_lnkv_b': _L1_xcond_in['lnkv_b'], 'L1_xcond_lnq_g': _L1_xcond_in['lnq_g'], 'L1_xcond_lnq_b': _L1_xcond_in['lnq_b'], 'L1_xcond_lnm_g': _L1_xcond_in['lnm_g'], 'L1_xcond_lnm_b': _L1_xcond_in['lnm_b'], 'L1_xcond_lnp_g': _L1_xcond_in['lnp_g'], 'L1_xcond_lnp_b': _L1_xcond_in['lnp_b'], 'L1_xcond_wk': _L1_xcond_in['wk'], 'L1_xcond_bk': _L1_xcond_in['bk'], 'L1_xcond_wv': _L1_xcond_in['wv'], 'L1_xcond_bv': _L1_xcond_in['bv'], 'L1_xcond_wq': _L1_xcond_in['wq'], 'L1_xcond_bq': _L1_xcond_in['bq'], 'L1_xcond_wu': _L1_xcond_in['wu'], 'L1_xcond_bu': _L1_xcond_in['bu'], 'L1_xcond_w1': _L1_xcond_in['w1'], 'L1_xcond_b1': _L1_xcond_in['b1'], 'L1_xcond_w2': _L1_xcond_in['w2'], 'L1_xcond_b2': _L1_xcond_in['b2'], 'L1_ffn_w_gate': _L1_ffn_in['w_gate'], 'L1_ffn_b_gate': _L1_ffn_in['b_gate'], 'L1_ffn_W1': _L1_ffn_in['W1'], 'L1_ffn_b1': _L1_ffn_in['b1'], 'L1_ffn_W2': _L1_ffn_in['W2'], 'L1_ffn_b2': _L1_ffn_in['b2']}

def reference(x, cond_1024, ctx_1024, L0_xcond_attn1_wq, L0_xcond_attn1_wk, L0_xcond_attn1_wv, L0_xcond_attn1_wo, L0_xcond_attn1_bo, L0_xcond_attn2_wq, L0_xcond_attn2_wk, L0_xcond_attn2_wv, L0_xcond_attn2_wo, L0_xcond_attn2_bo, L0_xcond_ff_w1, L0_xcond_ff_b1, L0_xcond_ff_w2, L0_xcond_ff_b2, L0_xcond_norm1_w, L0_xcond_norm1_b, L0_xcond_norm2_w, L0_xcond_norm2_b, L0_xcond_norm3_w, L0_xcond_norm3_b, L0_ffn_sg, L0_ffn_su, L0_ffn_sd, L0_ffn_rg, L0_ffn_ru, L0_ffn_rd, L0_ffn_wr, L0_ffn_rb, L1_xcond_q_mu, L1_xcond_q_logsig, L1_xcond_lnkv_g, L1_xcond_lnkv_b, L1_xcond_lnq_g, L1_xcond_lnq_b, L1_xcond_lnm_g, L1_xcond_lnm_b, L1_xcond_lnp_g, L1_xcond_lnp_b, L1_xcond_wk, L1_xcond_bk, L1_xcond_wv, L1_xcond_bv, L1_xcond_wq, L1_xcond_bq, L1_xcond_wu, L1_xcond_bu, L1_xcond_w1, L1_xcond_b1, L1_xcond_w2, L1_xcond_b2, L1_ffn_w_gate, L1_ffn_b_gate, L1_ffn_W1, L1_ffn_b1, L1_ffn_W2, L1_ffn_b2):
    import jax
    import jax.numpy as jnp

    def _L0_xcond_ref(x, t, context, attn1_wq, attn1_wk, attn1_wv, attn1_wo, attn1_bo, attn2_wq, attn2_wk, attn2_wv, attn2_wo, attn2_bo, ff_w1, ff_b1, ff_w2, ff_b2, norm1_w, norm1_b, norm2_w, norm2_b, norm3_w, norm3_b):
        import jax, jax.numpy as jnp
        import numpy as np
        import math
        B, S, CTX, D, H, DH = (2, 256, 32, 128, 16, 64)
        INNER = H * DH
        DFF = 4 * D

        def layernorm(x, eps=1e-05):
            m = jnp.mean(x, axis=-1, keepdims=True)
            v = jnp.var(x, axis=-1, keepdims=True)
            return (x - m) * jax.lax.rsqrt(v + eps)

        def adaln(x, t, w, b):
            emb = t @ w + b
            scale, shift = jnp.split(emb, 2, axis=-1)
            return layernorm(x) * (1.0 + scale) + shift

        def mha(xq, ctx, wq, wk, wv, wo, bo):
            b, sq, _ = xq.shape
            sk = ctx.shape[1]
            q = (xq @ wq).reshape(b, sq, H, DH).transpose(0, 2, 1, 3)
            k = (ctx @ wk).reshape(b, sk, H, DH).transpose(0, 2, 1, 3)
            v = (ctx @ wv).reshape(b, sk, H, DH).transpose(0, 2, 1, 3)
            scores = jnp.einsum('bhqd,bhkd->bhqk', q, k) / math.sqrt(DH)
            attn = jax.nn.softmax(scores, axis=-1)
            out = jnp.einsum('bhqk,bhkd->bhqd', attn, v)
            out = out.transpose(0, 2, 1, 3).reshape(b, sq, INNER)
            return out @ wo + bo

        def glu_ff(x, w1, b1, w2, b2):
            u = x @ w1 + b1
            a, gate = jnp.split(u, 2, axis=-1)
            return a * jax.nn.gelu(gate, approximate=False) @ w2 + b2
        h1 = adaln(x, t, norm1_w, norm1_b)
        x = mha(h1, h1, attn1_wq, attn1_wk, attn1_wv, attn1_wo, attn1_bo) + x
        h2 = adaln(x, t, norm2_w, norm2_b)
        x = mha(h2, context, attn2_wq, attn2_wk, attn2_wv, attn2_wo, attn2_bo) + x
        h3 = adaln(x, t, norm3_w, norm3_b)
        x = glu_ff(h3, ff_w1, ff_b1, ff_w2, ff_b2) + x
        return x

    def _L0_ffn_ref(x, sg, su, sd, rg, ru, rd, wr, rb):
        import jax, jax.numpy as jnp
        import numpy as np
        H, I, E_ROUTED, TOP_K = (128, 352, 7, 2)
        B, S = (4, 256)

        def _expert(h, g, u, d):
            return jnp.einsum('...i,hi->...h', jax.nn.silu(h @ g.T) * (h @ u.T), d)
        shared_out = _expert(x, sg, su, sd)
        logits = x @ wr.T + rb
        probs = jax.nn.softmax(logits, axis=-1)
        scores, idx = jax.lax.top_k(probs, TOP_K)
        scores = scores / scores.sum(axis=-1, keepdims=True)
        w = jnp.sum(scores[..., None] * jax.nn.one_hot(idx, E_ROUTED, dtype=x.dtype), axis=-2)
        out = shared_out
        for e in range(E_ROUTED):
            out = out + w[..., e:e + 1] * _expert(x, rg[e], ru[e], rd[e])
        return out

    def _L1_xcond_ref(x_cls, x, noise, q_mu, q_logsig, lnkv_g, lnkv_b, lnq_g, lnq_b, lnm_g, lnm_b, lnp_g, lnp_b, wk, bk, wv, bv, wq, bq, wu, bu, w1, b1, w2, b2):
        import jax, jax.numpy as jnp
        import numpy as np
        B, N, K, D, T = (16, 512, 16, 128, 3)
        EPS_ATTN = 1e-08
        LN_EPS = 1e-05

        def _ln(x, g, b):
            mu = jnp.mean(x, axis=-1, keepdims=True)
            var = jnp.mean(jnp.square(x - mu), axis=-1, keepdims=True)
            return (x - mu) * jax.lax.rsqrt(var + LN_EPS) * g + b
        scale = D ** (-0.5)
        x_in = _ln(x, lnkv_g, lnkv_b)
        k = x_in @ wk + bk
        v = x_in @ wv + bv
        slots = q_mu + jnp.exp(q_logsig) * noise
        for _ in range(T):
            prev = slots
            q = _ln(slots, lnq_g, lnq_b) @ wq + bq
            logits = jnp.einsum('bnd,bkd->bnk', k, q) / scale
            attn = jax.nn.softmax(logits, axis=-1) + EPS_ATTN
            attn = attn / jnp.sum(attn, axis=1, keepdims=True)
            upd = jnp.einsum('bnk,bnd->bkd', attn, v)
            slots = upd @ wu + bu + prev
            h = _ln(slots, lnm_g, lnm_b) @ w1 + b1
            slots = jax.nn.gelu(h, approximate=False) @ w2 + b2 + slots
            slots = _ln(slots + x_cls[:, None, :], lnp_g, lnp_b)
        return slots

    def _L1_ffn_ref(x, w_gate, b_gate, W1, b1, W2, b2):
        import jax, jax.numpy as jnp
        import numpy as np
        D_MODEL = 128
        MLP_DIM = 512
        N_EXPERTS = 8
        B, T = (4, 128)
        b, t, d = x.shape
        x_flat = x.reshape(b * t, d)
        logits = x_flat @ w_gate + b_gate
        probs = jax.nn.softmax(logits, axis=-1)
        route_p = jnp.max(probs, axis=-1)
        route_idx = jnp.argmax(probs, axis=-1)
        h = jnp.einsum('nd,edm->enm', x_flat, W1) + b1[:, None, :]
        h = jax.nn.relu(h)
        y = jnp.einsum('enm,emd->end', h, W2) + b2[:, None, :]
        n = b * t
        out = y[route_idx, jnp.arange(n)] * route_p[:, None]
        return out.reshape(b, t, d)
    x = x + _L0_xcond_ref(_layernorm(x, axis=-1), cond_1024[:, None, :], ctx_1024, L0_xcond_attn1_wq, L0_xcond_attn1_wk, L0_xcond_attn1_wv, L0_xcond_attn1_wo, L0_xcond_attn1_bo, L0_xcond_attn2_wq, L0_xcond_attn2_wk, L0_xcond_attn2_wv, L0_xcond_attn2_wo, L0_xcond_attn2_bo, L0_xcond_ff_w1, L0_xcond_ff_b1, L0_xcond_ff_w2, L0_xcond_ff_b2, L0_xcond_norm1_w, L0_xcond_norm1_b, L0_xcond_norm2_w, L0_xcond_norm2_b, L0_xcond_norm3_w, L0_xcond_norm3_b)
    x = x + _L0_ffn_ref(_layernorm(x, axis=-1), L0_ffn_sg, L0_ffn_su, L0_ffn_sd, L0_ffn_rg, L0_ffn_ru, L0_ffn_rd, L0_ffn_wr, L0_ffn_rb)
    x = x + _L1_xcond_ref(cond_1024, ctx_1024, _layernorm(x, axis=-1), L1_xcond_q_mu, L1_xcond_q_logsig, L1_xcond_lnkv_g, L1_xcond_lnkv_b, L1_xcond_lnq_g, L1_xcond_lnq_b, L1_xcond_lnm_g, L1_xcond_lnm_b, L1_xcond_lnp_g, L1_xcond_lnp_b, L1_xcond_wk, L1_xcond_bk, L1_xcond_wv, L1_xcond_bv, L1_xcond_wq, L1_xcond_bq, L1_xcond_wu, L1_xcond_bu, L1_xcond_w1, L1_xcond_b1, L1_xcond_w2, L1_xcond_b2)
    x = x + _L1_ffn_ref(_layernorm(x, axis=-1), L1_ffn_w_gate, L1_ffn_b_gate, L1_ffn_W1, L1_ffn_b1, L1_ffn_W2, L1_ffn_b2)
    return x

_drawn_inputs = setup_inputs


def setup_inputs(seed=0):
    import zlib

    import numpy as np

    out = dict(_drawn_inputs(seed))
    spreads = {'L0_ffn_rb': (0.0, 0.8),
     'L1_xcond_lnkv_g': (1.0, 0.6),
     'L1_xcond_lnkv_b': (0.0, 0.8),
     'L1_xcond_lnq_g': (1.0, 0.6),
     'L1_xcond_lnq_b': (0.0, 2.0),
     'L1_xcond_lnm_g': (1.0, 0.6),
     'L1_xcond_lnm_b': (0.0, 0.8),
     'L1_xcond_lnp_g': (1.0, 0.2),
     'L1_xcond_lnp_b': (0.0, 0.1),
     'L1_xcond_bk': (0.0, 2.0),
     'L1_xcond_bv': (0.0, 0.8),
     'L1_xcond_bq': (0.0, 2.0),
     'L1_xcond_bu': (0.0, 0.356),
     'L1_xcond_b1': (0.0, 0.8),
     'L1_xcond_b2': (0.0, 0.41),
     'L1_ffn_b1': (0.0, 0.8),
     'L1_ffn_b2': (0.0, 0.8)}
    factors = {'L0_xcond_attn1_bo': 8.0,
     'L0_xcond_attn2_bo': 8.0,
     'L0_xcond_ff_b1': 8.0,
     'L0_xcond_ff_b2': 8.0,
     'L0_xcond_norm1_b': 4.99,
     'L0_xcond_norm2_b': 8.0,
     'L0_xcond_norm3_b': 8.0,
     'L0_ffn_sg': 8.0,
     'L0_ffn_su': 8.0,
     'L0_ffn_sd': 8.0,
     'L0_ffn_rg': 8.0,
     'L0_ffn_ru': 8.0,
     'L0_ffn_rd': 8.0,
     'L0_ffn_wr': 8.0,
     'L1_xcond_q_logsig': 82.994,
     'L1_xcond_wk': 23.797,
     'L1_xcond_wv': 8.0,
     'L1_xcond_wq': 26.591,
     'L1_xcond_wu': 6.678,
     'L1_xcond_w1': 8.0,
     'L1_xcond_w2': 8.0,
     'L1_ffn_w_gate': 4.406,
     'L1_ffn_b_gate': 8.0,
     'L1_ffn_W1': 5.97,
     'L1_ffn_W2': 4.924,
     'L1_xcond_q_mu': 2.885}
    for name, (base, spread) in spreads.items():
        noise = np.random.default_rng([zlib.crc32(name.encode()), seed]).standard_normal(out[name].shape)
        drawn = base * np.exp(spread * noise) if base else spread * noise
        out[name] = jnp.asarray(drawn.astype(out[name].dtype))
    for name, factor in factors.items():
        out[name] = (out[name] * factor).astype(out[name].dtype)
    return out
```

```python
from contextlib import ExitStack

import concourse.bass as bass
from concourse import mybir

F32 = mybir.dt.float32
I32 = mybir.dt.int32
ALU = mybir.AluOpType
ACT = mybir.ActivationFunctionType
X = mybir.AxisListType.X

P = 128
B = 16
D = 128
C = 77
H = 16
DH = 64
INNER = H * DH
NCH = INNER // P
QH = 4
FF = 512
EPS = 1e-5
TOK = B * P
EA, IA = 7, 352
CA = -(-IA // P)
EB, FB = 8, 512
NR = (2 * TOK + EA * (P - 1)) // P
NA = B + NR
NB = (TOK + EB * (P - 1)) // P
SLOT_ITERS = 3

PROJ_USES = [
    ("q2_0", "B", "act"), ("q2_1", "B", "act"), ("gate", "C", "dve"), ("lin", "C", "dve"),
    ("ffout", "C", "dve"), ("zT", "C", "act"), ("k2_0", "A", "act"), ("k2_1", "A", "act"),
    ("o2T_0", "B", "act"), ("o2T_1", "B", "act"), ("logit", "C", "dve"),
    ("v2_0", "A", "act"), ("v2_1", "A", "act"), ("wo2", "B", "dve"),
    ("q1_0", "N", "act"), ("q1_1", "N", "act"), ("o1T_0", "A", "act"), ("o1T_1", "A", "act"),
    ("h3T", "B", "act"), ("k1_0", "N", "act"), ("wo1", "A", "dve"), ("k1_1", "N", "act"),
    ("v1_0", "N", "act"), ("v1_1", "N", "act"), ("h2T", "A", "act"),
]
NBANK = 3
RSQRT_STEPS = 13
FIRST_LOOPED = 2


def streams(i):
    return {s for s, b in (("A", i), ("B", i - 1), ("C", i - 2), ("N", i + 1)) if 0 <= b < B}


def proj_plan():
    full, done, last, plan = 0, {"act": 0, "dve": 0}, [None] * NBANK, {}
    for i in range(-1, B + 2):
        for n, (name, stream, eng) in enumerate(PROJ_USES):
            if stream not in streams(i):
                continue
            full += 1
            done[eng] += 1
            plan[i, name] = (n % NBANK, full, done[eng], last[n % NBANK])
            last[n % NBANK] = (eng, done[eng])
    return plan


def units_before(i):
    return sum(QH * (("A" in streams(j)) + ("B" in streams(j))) for j in range(-1, i))


def unit_heads(j):
    return slice(8 * (j // 2) + j % 2, 8 * (j // 2) + 8, 2)


def is_iteration(i, n):
    return isinstance(i, int) and i == n


def at(i, count):
    if isinstance(i, int):
        return count(i)
    a, b = count(FIRST_LOOPED), count(FIRST_LOOPED + 1)
    assert all(count(j) == a + (j - FIRST_LOOPED) * (b - a) for j in range(FIRST_LOOPED, B - 1))
    return i * (b - a) + (a - FIRST_LOOPED * (b - a))


def from_one(eng, sem, count):
    if not isinstance(count, int) or count >= 1:
        eng.wait_ge(sem, count)


def skewed(eng, nblk, step):
    pairs = (nblk - 4) // 2
    for n in range(-2, 2):
        step(n // 2, n % 2)
    with eng.Fori(1, 1 + pairs) as q:
        step(q, 0)
        step(q, 1)
    for n in range(2 + 2 * pairs, nblk + 1):
        step(n // 2, n % 2)


def exists(n, nblk):
    return not isinstance(n, int) or 0 <= n < nblk


def program(nc, A, row_names, out):
    PLAN = proj_plan()
    with ExitStack() as ctx:
        def sb(name, *shape, dt=F32):
            return ctx.enter_context(nc.sbuf_tensor("sb_" + name, list(shape), dt))

        phase1 = ctx.enter_context(ExitStack())

        def sb1(name, *shape, dt=F32):
            return phase1.enter_context(nc.sbuf_tensor("sb_" + name, list(shape), dt))

        def sem(name):
            return ctx.enter_context(nc.semaphore(name))

        eye = sb("eye", P, P)
        tri = sb("tri", P, P)
        ones = sb("ones", P, P)
        zeros = sb("zeros", P, P)
        cols = sb("cols", P, 24)
        rows = sb("rows", P, A["rows"].shape[0])
        x_sb = sb("x", P, B, D)
        z_all = sb("z_all", P, B, D)
        ctx_n = sb("ctx", C, B, D)
        logits = sb("logits", P, B, EB)
        gate_up = sb("gate_up", P, EA + 1, 2 * IA)
        down = sb("down", P, EA + 1, CA, D)
        wr = sb("wr", P, EA)
        wgate = sb("wgate", P, EB)
        slot_w = sb("slot_w", P, 6, D)
        st_all = sb("st_all", P, B, 6)
        mv_all = sb("mv_all", P, B, 2)
        rsq_all = sb("rsq_all", P, 2, B)
        rstd_all = sb("rstd_all", P, B)
        expert_a = sb("expert_a", 1, NA, dt=I32)
        expert_b = sb("expert_b", 1, NB, dt=I32)

        x0b = sb1("x0b", P, B, D)
        h1T = sb1("h1T", P, B, P)
        ctxT = sb1("ctxT", P, B * C)
        cond_t = sb1("cond_t", P, B)
        nw = sb1("norm_w", P, 3, 2 * D)
        ada = sb1("ada", P, 3, 2, B)
        watt = sb1("watt", P, 2, 4, INNER)
        w1 = sb1("ff_w1", P, 2 * FF)
        w2 = sb1("ff_w2", P, FF // P, D)
        q1T, k1T, q2T = (sb1(n, P, NCH, P) for n in ("q1T", "k1T", "q2T"))
        k2T = sb1("k2T", P, NCH, C)
        v1 = sb1("v1", P, H, DH + 1)
        v2 = sb1("v2", C, H, DH + 1)
        shifted = sb1("shifted", P, 2, QH, P)
        expd = sb1("expd", P, 2, QH, P)
        probT = sb1("probT", P, 2, QH, P)
        smax = sb1("smax", P, 2, QH)
        rden = sb1("rden", P, 2, QH)
        o_nat = {s: sb1("o" + s, P, H, DH) for s in "AB"}
        oT = {s: sb1("oT" + s, P, NCH, P) for s in "AB"}
        xa, xab, xb, xbx = (sb1(n, P, D) for n in ("xa", "xab", "xb", "xbx"))
        zA, zB, zC = (sb1("z" + s, P, D) for s in "ABC")
        hcur1, h2T, h3T, zT = (sb1(n, P, P) for n in ("hcur1", "h2T", "h3T", "zT"))
        ctxcur = sb1("ctxcur", P, C)
        gpre = sb1("gpre", P, FF // P, P)
        gact = sb1("gact", P, FF // P, P)
        glu = sb1("glu", P, FF // P, P)
        st = {s: sb1("st" + s, P, 6) for s in "ABC"}
        mv = {s: sb1("mv" + s, P, 2) for s in "ABC"}
        rsq = {s: sb1("rsq" + s, P, 2, 1) for s in "ABC"}
        rstd = {s: sb1("rstd" + s, P, 1) for s in "ABC"}
        phase1.close()

        w1b = sb("w1b", P, EB, FB)
        w2b = sb("w2b", P, EB, FB // P, D)
        spent = gate_up[:, :, :].rearrange("p e n -> p (e n)")
        b1b = spent[:, 0:EB * FB].rearrange("p (e n) -> p e n", e=EB)
        b2b = spent[:, EB * FB:EB * (FB + D)].rearrange("p (e n) -> p e n", e=EB)
        S = sb("S", P, B, D)
        s_rest = sb("s_rest", P, B, D)
        zs = z_all
        zsT = sb("zsT", P, B, P)
        hid = sb("hid", P, B, P)
        att = sb("att", C, B, P)
        cb2 = sb("cb2", P, B, D)
        kq = sb("kq", P, B, C)
        kqb = sb("kqb", 1, B, C)
        vu = sb("vu", C, B, D + 1)
        es_b = sb("es_b", P, D)
        picked = sb("picked", P, B, 2, D)
        xinT, kkT, vT = (picked[:, 5 * n:5 * n + 5, :, :].rearrange("p b k d -> p (b k d)")[:, 0:B * C].rearrange(
            "p (b c) -> p b c", b=B) for n in range(3))
        blk_x = sb("blk_x", P, 2, D)
        blk_xT = sb("blk_xT", P, 2, P)
        blk_act = sb("blk_act", P, 2, FB)
        blk_h = sb("blk_h", P, 2, FB)
        blk_hT = sb("blk_hT", P, 2, FB // P, P)
        blk_y = sb("blk_y", P, 2, D)
        hot1, hot2, hot, run, slot, rt = (sb(n, P, EB, B) for n in ("hot1", "hot2", "hot", "run", "slot", "rt"))
        top1, top2, idx, wgt1, wgt2, slot1f, slot2f = (
            sb(n, P, B) for n in ("top1", "top2", "idx", "wgt1", "wgt2", "slot1f", "slot2f"))
        slot1, slot2 = (sb(n, P, B, dt=I32) for n in ("slot1", "slot2"))
        cnt, nblk, cblk, base = (sb(n, P, EB) for n in ("cnt", "nblk", "cblk", "base"))
        bge = sb("bge", 1, NA, EB)
        bex = sb("bex", 1, NA)
        nmax, esum, rsum, rcol = (sb(n, P, B) for n in ("nmax", "esum", "rsum", "rcol"))

        rows_a = nc.dram_tensor("rows_a", (NR * P, D), F32, kind="Internal").ap()
        outs_a = nc.dram_tensor("outs_a", (NA * P, D), F32, kind="Internal").ap()
        rows_b = nc.dram_tensor("rows_b", (NB * P, D), F32, kind="Internal").ap()
        outs_b = nc.dram_tensor("outs_b", (NB * P, D), F32, kind="Internal").ap()

        wq, wk, wv = ([watt[:, a, j, :] for a in range(2)] for j in range(3))
        wo = [watt[:, a, 3, :].rearrange("p (c n) -> p c n", c=NCH) for a in range(2)]
        R = {}
        at_col = 0
        for name, n in row_names:
            R[name] = rows[:, at_col:at_col + n]
            at_col += n
        wks, wvs, wqTs, wus, w1s, w2s = (slot_w[:, n, :] for n in range(6))
        lnkv_g, lnkv_b, lnq_g, lnq_b, lnm_g, lnm_b, bk, bq, sb1_, bv = (cols[:, 14 + n:15 + n] for n in range(10))

        bank = [ctx.enter_context(nc.psum_tensor(f"bank{n}", [P, 512], F32)) for n in range(8)]
        proj = bank[0:NBANK]

        def quads(t):
            return t[:, :].rearrange("p (h n) -> p h n", h=QH)

        score = [quads(t) for t in bank[3:5]]
        trans = [quads(t) for t in bank[5:7]]
        pvo = bank[7][:, 0:QH * (DH + 1)].rearrange("p (h d) -> p h d", h=QH)

        ld_x, ld_small, ld_att1, ld_att2, ld_ff, ld_ctx = (
            sem(n) for n in ("ld_x", "ld_small", "ld_att1", "ld_att2", "ld_ff", "ld_ctx"))
        pre_dve = sem("pre_dve")
        pre_ada = sem("pre_ada")
        pre_T = sem("pre_T")
        pre_act = sem("pre_act")
        hcur_ready = sem("hcur_ready")
        ctxcur_ready = sem("ctxcur_ready")
        proj_full = sem("proj_full")
        emptied = {"act": sem("proj_act"), "dve": sem("proj_dve")}
        score_done, max_done, sub_done, exp_done = (
            sem(n) for n in ("score_done", "max_done", "sub_done", "exp_done"))
        T_done, probT_ready, pv_done, rden_done, norm_done = (
            sem(n) for n in ("T_done", "probT_ready", "pv_done", "rden_done", "norm_done"))
        gelu_done = sem("gelu_done")
        stats_done, mv_ready, ln_step = (
            {s: sem(n + s) for s in "ABC"} for n in ("stats_done", "mv_ready", "ln_step"))
        pre_rsqrt = sem("pre_rsqrt")
        z_ready = {s: sem("z_ready" + s) for s in "ABC"}
        xab_ready, xbx_ready, z_kept = (sem(n) for n in ("xab_ready", "xbx_ready", "z_kept"))
        out_sem = sem("out_sem")

        ld_moe, ld_slot, ld_cond, ld_moe_b, zeroed, consts_ready, filled_rows = (
            sem(n) for n in ("ld_moe", "ld_slot", "ld_cond", "ld_moe_b", "zeroed", "consts_ready", "filled_rows"))
        pre_slot_full, pre_slot_done = sem("pre_slot_full"), sem("pre_slot_done")
        ctx_step, ctx_rsqrt = sem("ctx_step"), sem("ctx_rsqrt")
        rt_step = {x: sem("rt_step_" + x) for x in "ab"}
        hot_ready, rank_done, exp_in, exp_out, routed, scattered, all_stored = (
            {x: sem(n + x) for x in "ab"} for n in (
                "hot_ready_", "rank_done_", "exp_in_", "exp_out_", "routed_", "scattered_", "all_stored_"))
        blk_in, stored = ({x: [sem(f"{n}_{x}{u}") for u in range(2)] for x in "ab"} for n in ("blk_in", "stored"))
        xT_done, xT_ready, up_done, act_done, h_ready, hT_done, hT_ready, y_done, y_ready = (
            {x: sem(n + x) for x in "ab"} for n in (
                "xT_done_", "xT_ready_", "up_done_", "act_done_", "h_ready_", "hT_done_", "hT_ready_", "y_done_", "y_ready_"))
        shared_in = sem("shared_in")
        picked_a, picked_b = ([sem(f"picked_{x}{g}") for g in range(4)] for x in "ab")
        mean_ready, x2_ready = sem("mean_ready"), sem("x2_ready")
        sl_step, sl_rsqrt = sem("sl_step"), sem("sl_rsqrt")
        zq_ready, zqT_done, zqT_ready, lg_done, nmax_ready, att_exp, att_ready, upd_done, mid_ready, mid_rest = (
            sem("sl_" + n) for n in ("zq_ready", "zqT_done", "zqT_ready", "lg_done", "nmax_ready", "att_exp",
                                     "att_ready", "upd_done", "mid_ready", "mid_rest"))
        zm_ready, zmT_done, zmT_ready, hid_done, hid_ready, mlp_done, sum_ready, zp_ready, S_ready, S_rest = (
            sem("sl_" + n) for n in ("zm_ready", "zmT_done", "zmT_ready", "hid_done", "hid_ready", "mlp_done",
                                     "sum_ready", "zp_ready", "S_ready", "S_rest"))
        x3_ready, z3_ready, z3T_done, z3T_ready, lgb_done = (
            sem(n) for n in ("x3_ready", "z3_ready", "z3T_done", "z3T_ready", "lgb_done"))
        fin_step, fin_rsqrt = sem("fin_step"), sem("fin_rsqrt")
        fence = sem("fence")
        out_ready, sum_ready2 = sem("out_ready"), sem("sl_scaled")
        G = 4

        NBLK = {"a": NA, "b": NB}
        RANK_BANK = {"a": 7, "b": 2}

        def first_phase_over(eng):
            eng.wait_ge(emptied["dve"], PLAN[B + 1, "logit"][2])
            eng.wait_ge(z_kept, B)

        N_SMALL = 6
        PRE_Z1 = 8
        block = ctx.enter_context(nc.Block())

        @block.sync
        def _(sp):
            for g in range(4):
                sp.dma_start(x_sb[:, 4 * g:4 * g + 4, :],
                             A["x"][4 * g:4 * g + 4].rearrange("b s d -> s b d")).then_inc(ld_x, 16)
            sp.dma_start(cond_t[:, :], A["cond_t"]).then_inc(ld_small, 16)
            sp.dma_start(nw[:, :, :], A["norm_w"].rearrange("n p d -> p n d")).then_inc(ld_small, 16)
            sp.dma_start(eye[:, :], A["eye"]).then_inc(ld_small, 16)
            sp.dma_start(cols[:, :], A["cols"]).then_inc(ld_small, 16)
            nrow = A["rows"].shape[0]
            sp.dma_start(rows[:, :], A["rows"].partition_broadcast(P)).then_inc(ld_small, 16)
            sp.dma_start(wr[:, 0:7], A["wr_t"]).then_inc(ld_small, 16)
            for j in range(3):
                sp.dma_start(watt[:, 0, j, :], A["att_w"][0, j]).then_inc(ld_att1, 16)
            sp.dma_start(ctx_n[:, :, :], A["ctx"].rearrange("b c d -> c b d")).then_inc(ld_ctx, 16)
            sp.dma_start(wo[0], A["att_wo"][0].rearrange("(c p) n -> p c n", p=P)).then_inc(ld_att1, 16)
            for j in range(3):
                sp.dma_start(watt[:, 1, j, :], A["att_w"][1, j]).then_inc(ld_att2, 16)
            sp.dma_start(wo[1], A["att_wo"][1].rearrange("(c p) n -> p c n", p=P)).then_inc(ld_att2, 16)
            sp.dma_start(w1[:, :], A["ff_w1"]).then_inc(ld_ff, 16)
            sp.dma_start(w2[:, :, :], A["ff_w2"].rearrange("(c p) n -> p c n", p=P)).then_inc(ld_ff, 16)
            sp.dma_start(gate_up[:, :, :], A["gate_up"]).then_inc(ld_moe, 16)
            sp.dma_start(down[:, :, :, :], A["down"]).then_inc(ld_moe, 16)
            sp.dma_start(tri[:, :], A["tri"]).then_inc(ld_moe, 16)
            sp.dma_start(wgate[:, :], A["wgate"]).then_inc(ld_slot, 16)
            sp.dma_start(slot_w[:, :, :], A["slot_w"].rearrange("n p d -> p n d")).then_inc(ld_slot, 16)
            sp.wait_ge(consts_ready, 1)
            for t, n in ((rows_a, NR), (rows_b, NB)):
                sp.dma_start(t.rearrange("(n p) d -> p n d", p=P),
                             zeros[:, :].unsqueeze(1).broadcast_to([P, n, D])).then_inc(zeroed, 16)
            first_phase_over(sp)
            sp.dma_start(cb2[:, :, :].rearrange("p b d -> p (b d)"),
                         A["cond"].rearrange("b d -> (b d)").partition_broadcast(P)).then_inc(ld_cond, 16)

            def load(x, m, u, src):
                from_one(sp, xT_done[x], m - 1)
                sp.dma_start(blk_x[:, u, :], src).then_inc(blk_in[x][u], 16)

            def store(x, m, u, dst, row):
                sp.wait_ge(y_ready[x], m + 1)
                sp.dma_start(dst[bass.ds(row * P, P), :], blk_y[:, u, :]).then_inc(stored[x][u], 16)

            def kept(m):
                return z_all[:, bass.ds(m, 1), :].rearrange("p a d -> p (a d)")

            def sorted_rows(t, m):
                return t[bass.ds(m * P, P), :]

            load("a", 0, 0, kept(0))
            load("a", 1, 1, kept(1))
            load("a", 2, 0, kept(2))
            with sp.Fori(1, B // 2 - 1) as q:
                for u in range(2):
                    load("a", 2 * q + u + 1, 1 - u, kept(2 * q + u + 1))
                    store("a", 2 * q + u - 2, u, outs_a, 2 * q + u - 2 + NR)
            load("a", B - 1, 1, kept(B - 1))
            store("a", B - 4, 0, outs_a, NR + B - 4)
            sp.wait_ge(scattered["a"], 16 * 2 * B)
            for m in range(B, B + 3):
                load("a", m, m % 2, sorted_rows(rows_a, m - B))
                store("a", m - 3, (m - 3) % 2, outs_a, NR + m - 3)
            with sp.Fori(0, (NR - 4) // 2) as q:
                for u in range(2):
                    load("a", 2 * q + u + B + 3, 1 - u, sorted_rows(rows_a, 2 * q + u + 3))
                    store("a", 2 * q + u + B, u, outs_a, 2 * q + u)
            load("a", NA - 1, (NA - 1) % 2, sorted_rows(rows_a, NR - 1))
            for m in range(NA - 4, NA):
                store("a", m, m % 2, outs_a, m - B)
            for u in range(2):
                sp.wait_ge(stored["a"][u], 16 * (NA // 2))
            sp.dma_start(z_all[:, :, :], outs_a[NR * P:NA * P, :].rearrange("(b s) d -> s b d", s=P)).then_inc(shared_in, 16)
            sp.dma_start(w1b[:, :, :], A["w1b"].rearrange("e p n -> p e n")).then_inc(ld_moe_b, 16)
            sp.dma_start(w2b[:, :, :, :], A["w2b"].rearrange("e (c p) d -> p e c d", p=P)).then_inc(ld_moe_b, 16)
            sp.dma_start(spent[:, 0:EB * (FB + D)], A["b12"].partition_broadcast(P)).then_inc(ld_moe_b, 16)
            sp.wait_ge(scattered["b"], 16 * B)
            load("b", 0, 0, sorted_rows(rows_b, 0))
            load("b", 1, 1, sorted_rows(rows_b, 1))
            load("b", 2, 0, sorted_rows(rows_b, 2))
            odd = (NB - 3) % 2
            with sp.Fori(0, (NB - 3 - odd) // 2) as q:
                for u in range(2):
                    load("b", 2 * q + u + 3, 1 - u, sorted_rows(rows_b, 2 * q + u + 3))
                    store("b", 2 * q + u, u, outs_b, 2 * q + u)
            for m in range(NB - odd, NB):
                load("b", m, m % 2, sorted_rows(rows_b, m))
            for m in range(NB - 3 - odd, NB):
                store("b", m, m % 2, outs_b, m)
            for g in range(G):
                sp.wait_ge(out_ready, g + 1)
                sp.dma_start(out[4 * g:4 * g + 4].rearrange("b s d -> s b d"),
                             x_sb[:, 4 * g:4 * g + 4, :]).then_inc(out_sem, 16)
            sp.wait_ge(out_sem, 16 * G)

        @block.tensor
        def _(pe):
            pe.wait_ge(ld_small, 16 * N_SMALL)
            for n in range(3):
                for j in range(2):
                    mm = pe.matmul(proj[0][:, (2 * n + j) * B:(2 * n + j + 1) * B], nw[:, n, j * D:(j + 1) * D],
                                   cond_t[:, :], start=True, stop=True)
            mm.then_inc(pre_ada, 1)
            pe.wait_ge(pre_dve, PRE_Z1)
            for g in range(8):
                if g == 4:
                    pe.wait_ge(ld_ctx, 16)
                if g >= 2:
                    pe.wait_ge(pre_act, g - 1)
                for n in range(4):
                    b = 4 * (g % 4) + n
                    if g < 4:
                        mm = pe.transpose(trans[g % 2][:, n, :], z_all[:, b, :], eye[:, :])
                    else:
                        mm = pe.transpose(trans[g % 2][:, n, 0:C], ctx_n[:, b, :], eye[0:C, 0:C])
                mm.then_inc(pre_T, 1)

            def use(i, name):
                bank, _, _, free = PLAN[FIRST_LOOPED if not isinstance(i, int) else i, name]
                if free is not None:
                    pe.wait_ge(emptied[free[0]], at(i, lambda j: PLAN[j, name][3][1]))
                return proj[bank]

            def qk_proj(i, name, w, src, half, n):
                t = use(i, name)
                for c in range(4):
                    mm = pe.matmul(t[:, c * n:(c + 1) * n], w[:, (4 * half + c) * P:(4 * half + c + 1) * P], src,
                                   start=True, stop=True)
                mm.then_inc(proj_full, 1)

            def v_proj(i, name, w, src, half, n):
                t = use(i, name)
                pe.matmul(t[0:n, :], src, w[:, half * 512:(half + 1) * 512],
                          start=True, stop=True).then_inc(proj_full, 1)

            def turn(i, name, src):
                pe.transpose(use(i, name)[:, 0:P], src[:, :], eye[:, :]).then_inc(proj_full, 1)

            def o_turn(i, name, o, half):
                t = use(i, name)
                for c in range(4):
                    mm = pe.transpose(t[:, c * P:(c + 1) * P],
                                      o[:, 2 * (4 * half + c):2 * (4 * half + c) + 2, :].rearrange("p h d -> p (h d)"),
                                      eye[:, :])
                mm.then_inc(proj_full, 1)

            def o_proj(i, name, s, w):
                t = use(i, name)
                for c in range(NCH):
                    mm = pe.matmul(t[:, 0:D], oT[s][:, c, :], w[:, c, :], start=(c == 0), stop=(c == NCH - 1))
                mm.then_inc(proj_full, 1)

            def score_unit(i, u, s, j):
                q, k, n = (q1T, k1T, P) if s == "A" else (q2T, k2T, C)
                if not (isinstance(i, int) and units_before(i) + u < 2):
                    pe.wait_ge(sub_done, at(i, lambda t: units_before(t) + u - 1))
                p = slice(DH * (j % 2), DH * (j % 2) + DH)
                for h in range(QH):
                    mm = pe.matmul(score[u % 2][:, h, 0:n], q[p, 4 * (j // 2) + h, :],
                                   k[p, 4 * (j // 2) + h, 0:n], start=True, stop=True)
                mm.then_inc(score_done, 1)

            def prob_turn(i, u, s):
                n = P if s == "A" else C
                pe.wait_ge(exp_done, at(i, lambda t: units_before(t) + u + 1))
                if not (isinstance(i, int) and units_before(i) + u < 2):
                    pe.wait_ge(probT_ready, at(i, lambda t: units_before(t) + u - 1))
                for h in range(QH):
                    mm = pe.transpose(trans[u % 2][0:n, h, :], expd[:, u % 2, h, 0:n], eye[:, :])
                mm.then_inc(T_done, 1)

            def pv_unit(i, u, s, j):
                n, v = (P, v1) if s == "A" else (C, v2)
                pe.wait_ge(probT_ready, at(i, lambda t: units_before(t) + u + 1))
                if not (isinstance(i, int) and units_before(i) + u < 1):
                    pe.wait_ge(norm_done, at(i, lambda t: units_before(t) + u))
                for h in range(QH):
                    mm = pe.matmul(pvo[:, h, :], probT[0:n, u % 2, h, :], v[:, unit_heads(j), :][:, h, :],
                                   start=True, stop=True)
                mm.then_inc(pv_done, 1)

            def emptied_by(i, name, ago=0):
                eng = [e for n, _, e in PROJ_USES if n == name][0]
                pe.wait_ge(emptied[eng], at(i, lambda j: PLAN[j - ago, name][2]))

            def iteration(i, S):
                units = [("B", j) for j in range(4) if "B" in S] + [("A", j) for j in range(4) if "A" in S]
                if "B" in S:
                    emptied_by(i, "h2T", 1)
                    qk_proj(i, "q2_0", wq[1], h2T[:, :], 0, P)
                    qk_proj(i, "q2_1", wq[1], h2T[:, :], 1, P)
                if "C" in S:
                    pe.wait_ge(ld_ff, 32)
                    emptied_by(i, "h3T", 1)
                    qk_proj(i, "gate", w1[:, FF:2 * FF], h3T[:, :], 0, P)
                    qk_proj(i, "lin", w1[:, 0:FF], h3T[:, :], 0, P)
                for k in range(10):
                    if k < len(units):
                        s, j = units[k]
                        if j == 0:
                            if s == "A":
                                emptied_by(i, "k1_1", 1)
                            else:
                                emptied_by(i, "q2_1")
                        score_unit(i, k, s, j)
                    if 0 <= k - 2 < len(units):
                        s, j = units[k - 2]
                        if j == 0:
                            emptied_by(i, "v1_1" if s == "A" else "v2_1", 1)
                        pv_unit(i, k - 2, s, j)
                    if 0 <= k - 1 < len(units):
                        prob_turn(i, k - 1, units[k - 1][0])
                    if k == 2 and "C" in S:
                        t = use(i, "ffout")
                        emptied_by(i, "lin")
                        for c in range(FF // P):
                            mm = pe.matmul(t[:, 0:D], glu[:, c, :], w2[:, c, :], start=(c == 0), stop=(c == FF // P - 1))
                        mm.then_inc(proj_full, 1)
                    if k == 4 and "C" in S:
                        pe.wait_ge(z_ready["C"], i - 2 + 1)
                        turn(i, "zT", zC)
                    if k in (4, 5) and "A" in S:
                        if k == 4:
                            if is_iteration(i, 0):
                                pe.wait_ge(ld_att2, 64)
                            pe.wait_ge(ctxcur_ready, i + 1)
                        qk_proj(i, f"k2_{k - 4}", wk[1], ctxcur[:, :], k - 4, C)
                    if k == 6 and "B" in S:
                        pe.wait_ge(norm_done, at(i, lambda t: units_before(t) + 4))
                        o_turn(i, "o2T_0", o_nat["B"], 0)
                        o_turn(i, "o2T_1", o_nat["B"], 1)
                    if k == 6 and "C" in S:
                        t = use(i, "logit")
                        emptied_by(i, "zT")
                        pe.matmul(t[:, 0:7], zT[:, :], wr[:, 0:7], start=True, stop=True).then_inc(proj_full, 1)
                    if k == 7 and "A" in S:
                        v_proj(i, "v2_0", wv[1], ctxcur[:, :], 0, C)
                        v_proj(i, "v2_1", wv[1], ctxcur[:, :], 1, C)
                    if k == 7 and "B" in S:
                        emptied_by(i, "o2T_1")
                        o_proj(i, "wo2", "B", wo[1])
                if "N" in S:
                    pe.wait_ge(hcur_ready, i + 2)
                    qk_proj(i, "q1_0", wq[0], hcur1[:, :], 0, P)
                    qk_proj(i, "q1_1", wq[0], hcur1[:, :], 1, P)
                if "A" in S:
                    pe.wait_ge(norm_done, at(i, lambda t: units_before(t + 1)))
                    o_turn(i, "o1T_0", o_nat["A"], 0)
                    o_turn(i, "o1T_1", o_nat["A"], 1)
                if "B" in S:
                    pe.wait_ge(z_ready["B"], i)
                    turn(i, "h3T", zB)
                if "N" in S:
                    qk_proj(i, "k1_0", wk[0], hcur1[:, :], 0, P)
                if "A" in S:
                    emptied_by(i, "o1T_1")
                    o_proj(i, "wo1", "A", wo[0])
                if "N" in S:
                    qk_proj(i, "k1_1", wk[0], hcur1[:, :], 1, P)
                    v_proj(i, "v1_0", wv[0], hcur1[:, :], 0, P)
                    v_proj(i, "v1_1", wv[0], hcur1[:, :], 1, P)
                if "A" in S:
                    pe.wait_ge(z_ready["A"], i + 1)
                    turn(i, "h2T", zA)


            def rank_sums(x, n_exp):
                pe.wait_ge(hot_ready[x], 1)
                pe.wait_ge(ld_moe, 48)
                src = hot[:, 0:n_exp, :].rearrange("p e t -> p (e t)")
                w = n_exp * B
                t = bank[RANK_BANK[x]]
                pe.matmul(t[:, 0:w], tri[:, :], src, start=True, stop=True)
                mm = pe.matmul(t[:, P:P + w], ones[:, :], src, start=True, stop=True)
                mm.then_inc(rank_done[x], 1)

            pe.wait_ge(ld_att1, 64)
            for i in (-1, 0, 1):
                iteration(i, streams(i))
            with pe.Fori(FIRST_LOOPED, B - 1) as i:
                iteration(i, set("ABCN"))
            for i in (B - 1, B, B + 1):
                iteration(i, streams(i))

            first_phase_over(pe)
            pe.wait_ge(ld_slot, 32)
            uses = [0]

            def slot_bank():
                from_one(pe, pre_slot_done, uses[0] - 6)
                uses[0] += 1
                return bank[(uses[0] - 1) % 7]

            def flat(t, g):
                return t[:, 4 * g:4 * g + 4, :].rearrange("p b c -> p (b c)")

            for g in range(G):
                t = slot_bank()
                pe.wait_ge(ctx_step, 3)
                for n in range(4):
                    mm = pe.transpose(t[:, n * C:(n + 1) * C], ctx_n[:, 4 * g + n, :], eye[0:C, 0:C])
                mm.then_inc(pre_slot_full, 1)
            for stage, (w, src, rowsn) in enumerate(((wks, xinT, P), (wvs, xinT, P), (wqTs, kkT, P), (bq, kkT, 1))):
                for g in range(G):
                    t = slot_bank()
                    pe.wait_ge(pre_slot_done, (g + 1) if src is xinT else G + g + 1)
                    pe.matmul(t[0:rowsn, 0:4 * C], w, flat(src, g), start=True, stop=True).then_inc(pre_slot_full, 1)
                if stage == 1:
                    rank_sums("a", EA)
            for g in range(G):
                t = slot_bank()
                pe.wait_ge(pre_slot_done, 2 * G + g + 1)
                for n in range(4):
                    mm = pe.matmul(t[0:C, n * D:(n + 1) * D], vT[:, 4 * g + n, :], wus, start=True, stop=True)
                mm.then_inc(pre_slot_full, 1)

            pe.wait_ge(ld_moe, 48)
            pe.wait_ge(pre_slot_done, 6 * G)

            def turn_rows(x, q, u):
                m = 2 * q + u + 2
                if exists(m, NBLK[x]):
                    pe.wait_ge(blk_in[x][u], 16 * (q + 2))
                    from_one(pe, xT_ready[x], m)
                    pe.transpose(bank[0][:, 0:P], blk_x[:, u, :], eye[:, :]).then_inc(xT_done[x], 1)

            def expert_of(table, m, n_exp):
                return pe.value_load(table[0:1, bass.ds(m, 1)], min_val=0, max_val=n_exp - 1)

            def step_a(q, u):
                n, v = 2 * q + u, 1 - u
                turn_rows("a", q, u)
                m = n + 1
                if exists(m, NA):
                    pe.wait_ge(xT_ready["a"], m + 1)
                    from_one(pe, h_ready["a"], m - 1)
                    e = expert_of(expert_a, m, EA + 1)
                    for j in range(2):
                        mm = pe.matmul(bank[1 + 2 * j + v][:, 0:IA], blk_xT[:, v, :],
                                       gate_up[:, bass.ds(e, 1), j * IA:(j + 1) * IA].rearrange("p a n -> p (a n)"),
                                       start=True, stop=True)
                    mm.then_inc(up_done["a"], 1)
                if exists(n, NA):
                    pe.wait_ge(h_ready["a"], n + 1)
                    from_one(pe, hT_ready["a"], n)
                    for c in range(CA):
                        w = min(P, IA - c * P)
                        mm = pe.transpose(bank[5][0:w, c * P:(c + 1) * P], blk_h[:, u, c * P:c * P + w], eye[:, :])
                    mm.then_inc(hT_done["a"], 1)
                m = n - 1
                if exists(m, NA):
                    pe.wait_ge(hT_ready["a"], m + 1)
                    from_one(pe, y_ready["a"], m - 1)
                    e = expert_of(expert_a, m, EA + 1)
                    for c in range(CA):
                        w = min(P, IA - c * P)
                        mm = pe.matmul(bank[6 + v][:, 0:D], blk_hT[0:w, v, c, :],
                                       down[0:w, bass.ds(e, 1), c, :].rearrange("p a n -> p (a n)"),
                                       start=(c == 0), stop=(c == CA - 1))
                    mm.then_inc(y_done["a"], 1)

            skewed(pe, NA, step_a)

            def turn_group(g, ready, count, done):
                pe.wait_ge(ready, count)
                for n in range(4):
                    mm = pe.transpose(quads(bank[2 * g])[:, n, :], zs[:, 4 * g + n, :], eye[:, :])
                mm.then_inc(done, 1)

            pe.wait_ge(y_ready["a"], NA)
            with pe.Fori(0, SLOT_ITERS) as it:
                for g in range(G):
                    turn_group(g, zq_ready, it * G + g + 1, zqT_done)
                for g in range(G):
                    pe.wait_ge(zqT_ready, it * G + g + 1)
                    for n in range(4):
                        b = 4 * g + n
                        pe.matmul(quads(bank[2 * g + 1])[0:C, n, :], kqb[0:1, b, :], ones[0:1, :], start=True, stop=False)
                        mm = pe.matmul(quads(bank[2 * g + 1])[0:C, n, :], kq[:, b, :], zsT[:, b, :], start=False, stop=True)
                    mm.then_inc(lg_done, 1)
                for g in range(G):
                    pe.wait_ge(att_ready, it * G + g + 1)
                    for n in range(4):
                        b = 4 * g + n
                        mm = pe.matmul(bank[2 * g + n // 2][:, (n % 2) * (D + 1):(n % 2 + 1) * (D + 1)],
                                       att[:, b, :], vu[:, b, :], start=True, stop=True)
                    mm.then_inc(upd_done, 1)
                for g in range(G):
                    turn_group(g, zm_ready, it * G + g + 1, zmT_done)
                for g in range(G):
                    pe.wait_ge(zmT_ready, it * G + g + 1)
                    pe.matmul(bank[2 * g + 1][:, :], w1s, flat(zsT, g), start=True, stop=True).then_inc(hid_done, 1)
                for g in range(G):
                    pe.wait_ge(hid_ready, it * G + g + 1)
                    for n in range(4):
                        mm = pe.matmul(quads(bank[2 * g])[:, n, :], hid[:, 4 * g + n, :], w2s, start=True, stop=True)
                    mm.then_inc(mlp_done, 1)

            for g in range(G):
                turn_group(g, z3_ready, g + 1, z3T_done)
            for g in range(G):
                pe.wait_ge(z3T_ready, g + 1)
                for n in range(4):
                    b = 4 * g + n
                    mm = pe.matmul(bank[1][:, b * EB:(b + 1) * EB], zsT[:, b, :], wgate[:, :], start=True, stop=True)
            mm.then_inc(lgb_done, 1)
            rank_sums("b", EB)
            pe.wait_ge(ld_moe_b, 48)

            def step_b(q, u):
                n, v = 2 * q + u, 1 - u
                turn_rows("b", q, u)
                m = n + 1
                if exists(m, NB):
                    pe.wait_ge(xT_ready["b"], m + 1)
                    from_one(pe, h_ready["b"], m - 1)
                    e = expert_of(expert_b, m, EB)
                    pe.matmul(bank[1 + v][:, :], blk_xT[:, v, :], w1b[:, bass.ds(e, 1), :].rearrange("p a n -> p (a n)"),
                              start=True, stop=True).then_inc(up_done["b"], 1)
                if exists(n, NB):
                    pe.wait_ge(h_ready["b"], n + 1)
                    from_one(pe, hT_ready["b"], n - 1)
                    for c in range(FB // P):
                        mm = pe.transpose(bank[3 + u][:, c * P:(c + 1) * P], blk_h[:, u, c * P:(c + 1) * P], eye[:, :])
                    mm.then_inc(hT_done["b"], 1)
                m = n - 1
                if exists(m, NB):
                    pe.wait_ge(hT_ready["b"], m + 1)
                    from_one(pe, y_ready["b"], m - 1)
                    e = expert_of(expert_b, m, EB)
                    for c in range(FB // P):
                        mm = pe.matmul(bank[5 + v][:, 0:D], blk_hT[:, v, c, :],
                                       w2b[:, bass.ds(e, 1), c, :].rearrange("p a n -> p (a n)"),
                                       start=(c == 0), stop=(c == FB // P - 1))
                    mm.then_inc(y_done["b"], 1)

            skewed(pe, NB, step_b)

        @block.scalar
        def _(act):
            act.wait_ge(pre_dve, 2)
            for g in range(8):
                act.wait_ge(pre_T, g + 1)
                for n in range(4):
                    b = 4 * (g % 4) + n
                    if g < 4:
                        ins = act.activation(h1T[:, b, :], trans[g % 2][:, n, :], ACT.Identity,
                                             bias=ada[:, 0, 1, b:b + 1], scale=ada[:, 0, 0, b:b + 1])
                    elif n == 0:
                        ins = act.activation(ctxT[:, 4 * (g - 4) * C:4 * (g - 3) * C].rearrange("p (n c) -> p n c", n=4),
                                             trans[g % 2][:, :, 0:C], ACT.Copy)
                ins.then_inc(pre_act, 1)

            def empty(i, name, dst, src=None, **kw):
                bank = PLAN[FIRST_LOOPED if not isinstance(i, int) else i, name][0]
                act.wait_ge(proj_full, at(i, lambda j: PLAN[j, name][1]))
                act.activation(dst, src(proj[bank]), kw.pop("f", ACT.Copy), **kw).then_inc(emptied["act"], 1)

            def chunks(t, n):
                return t[:, 0:4 * n].rearrange("p (c n) -> p c n", c=4)

            def heads(t, n):
                return t[0:n, :].rearrange("p (h d) -> p h d", d=DH)

            def modulated(i, name, dst, norm, b):
                empty(i, name, dst[:, :], lambda t: t[:, 0:P], f=ACT.Identity,
                      bias=ada[:, norm, 1, bass.ds(b, 1)], scale=ada[:, norm, 0, bass.ds(b, 1)])

            def iteration(i, S):
                units = [("B", j) for j in range(4) if "B" in S] + [("A", j) for j in range(4) if "A" in S]
                if "B" in S:
                    empty(i, "q2_0", q2T[:, 0:4, :], lambda t: chunks(t, P))
                    empty(i, "q2_1", q2T[:, 4:8, :], lambda t: chunks(t, P))
                if "C" in S:
                    act.wait_ge(emptied["dve"], at(i, lambda j: PLAN[j, "gate"][2]))
                    act.activation(gact[:, :, :], gpre[:, :, :], ACT.Gelu).then_inc(gelu_done, 1)
                for k in range(10):
                    if 0 <= k - 1 < len(units):
                        n = P if units[k - 1][0] == "A" else C
                        act.wait_ge(T_done, at(i, lambda t: units_before(t) + k))
                        act.activation(probT[0:n, (k - 1) % 2, :, :], trans[(k - 1) % 2][0:n, :, :],
                                       ACT.Copy).then_inc(probT_ready, 1)
                    if k < len(units):
                        n = P if units[k][0] == "A" else C
                        act.wait_ge(sub_done, at(i, lambda t: units_before(t) + k + 1))
                        act.activation(expd[:, k % 2, :, 0:n], shifted[:, k % 2, :, 0:n], ACT.Exp,
                                       scale=DH ** -0.5).then_inc(exp_done, 1)
                    if k == 4 and "C" in S:
                        empty(i, "zT", zT[:, :], lambda t: t[:, 0:P])
                    if k in (4, 5) and "A" in S:
                        empty(i, f"k2_{k - 4}", k2T[:, 4 * (k - 4):4 * (k - 3), :], lambda t: chunks(t, C))
                    if k == 6 and "B" in S:
                        for half in range(2):
                            empty(i, f"o2T_{half}", oT["B"][:, 4 * half:4 * half + 4, :], lambda t: chunks(t, P))
                    if k == 7 and "A" in S:
                        for half in range(2):
                            empty(i, f"v2_{half}", v2[:, 8 * half:8 * half + 8, 0:DH], lambda t: heads(t, C))
                if "N" in S:
                    empty(i, "q1_0", q1T[:, 0:4, :], lambda t: chunks(t, P))
                    empty(i, "q1_1", q1T[:, 4:8, :], lambda t: chunks(t, P))
                if "A" in S:
                    for half in range(2):
                        empty(i, f"o1T_{half}", oT["A"][:, 4 * half:4 * half + 4, :], lambda t: chunks(t, P))
                if "B" in S:
                    modulated(i, "h3T", h3T, 2, i - 1)
                if "N" in S:
                    empty(i, "k1_0", k1T[:, 0:4, :], lambda t: chunks(t, P))
                    empty(i, "k1_1", k1T[:, 4:8, :], lambda t: chunks(t, P))
                    for half in range(2):
                        empty(i, f"v1_{half}", v1[:, 8 * half:8 * half + 8, 0:DH], lambda t: heads(t, P))
                if "A" in S:
                    modulated(i, "h2T", h2T, 1, i)

            for i in (-1, 0, 1):
                iteration(i, streams(i))
            with act.Fori(FIRST_LOOPED, B - 1) as i:
                iteration(i, set("ABCN"))
            for i in (B - 1, B, B + 1):
                iteration(i, streams(i))

            first_phase_over(act)
            seen = [0]

            def from_slot_bank(dst, view, f=ACT.Copy, **kw):
                t = bank[seen[0] % 7]
                seen[0] += 1
                act.wait_ge(pre_slot_full, seen[0])
                act.activation(dst, view(t), f, **kw).then_inc(pre_slot_done, 1)

            def group_of(t, g):
                return t[:, 4 * g:4 * g + 4, :].rearrange("p b c -> p (b c)")

            wide = lambda t: t[:, 0:4 * C]
            for g in range(G):
                from_slot_bank(group_of(xinT, g), wide, ACT.Identity, scale=lnkv_g, bias=lnkv_b)
            for g in range(G):
                from_slot_bank(group_of(kkT, g), wide, ACT.Identity, bias=bk)
            for g in range(G):
                from_slot_bank(group_of(vT, g), wide, ACT.Identity, bias=bv)
            for g in range(G):
                from_slot_bank(group_of(kq, g), wide, scale=D ** 0.5)
            for g in range(G):
                from_slot_bank(group_of(kqb, g), lambda t: t[0:1, 0:4 * C], scale=D ** 0.5)
            for g in range(G):
                from_slot_bank(vu[:, 4 * g:4 * g + 4, 0:D], lambda t: quads(t)[0:C, :, :])
            act.wait_ge(exp_in["a"], 1)
            act.activation(wgt2[:, :], top2[:, :], ACT.Exp).then_inc(exp_out["a"], 1)

            def turned_rows(x, q, u, nblk):
                m = 2 * q + u + 2
                if exists(m, nblk):
                    act.wait_ge(xT_done[x], m + 1)
                    act.activation(blk_xT[:, u, :], bank[0][:, 0:P], ACT.Copy).then_inc(xT_ready[x], 1)

            def step_a(q, u):
                n, v = 2 * q + u, 1 - u
                turned_rows("a", q, u, NA)
                if exists(n + 1, NA):
                    act.wait_ge(up_done["a"], n + 2)
                    act.activation(blk_act[:, v, 0:IA], bank[1 + v][:, 0:IA], ACT.Silu).then_inc(act_done["a"], 1)
                if exists(n, NA):
                    act.wait_ge(hT_done["a"], n + 1)
                    full = IA // P
                    act.activation(blk_hT[:, u, 0:full, :],
                                   bank[5][:, 0:full * P].rearrange("p (c n) -> p c n", n=P), ACT.Copy)
                    act.activation(blk_hT[0:IA - full * P, u, full, :], bank[5][0:IA - full * P, full * P:(full + 1) * P],
                                   ACT.Copy).then_inc(hT_ready["a"], 1)

            skewed(act, NA, step_a)

            act.wait_ge(ld_slot, 32)
            act.activation(es_b[:, :], R["q_logsig"], ACT.Exp).then_inc(exp_out["a"], 1)

            def modulated_group(g, done, count, ready, scale, bias):
                act.wait_ge(done, count)
                act.activation(group_of(zsT, g), bank[2 * g][:, :], ACT.Identity, scale=scale, bias=bias).then_inc(ready, 1)

            with act.Fori(0, SLOT_ITERS) as it:
                for g in range(G):
                    modulated_group(g, zqT_done, it * G + g + 1, zqT_ready, lnq_g, lnq_b)
                for g in range(G):
                    act.wait_ge(nmax_ready, it * G + g + 1)
                    for n in range(4):
                        b = 4 * g + n
                        ins = act.activation(att[:, b, :], quads(bank[2 * g + 1])[0:C, n, :], ACT.Exp,
                                             bias=nmax[0:C, b:b + 1], accum_out=esum[0:C, b:b + 1])
                    ins.then_inc(att_exp, 1)
                for g in range(G):
                    modulated_group(g, zmT_done, it * G + g + 1, zmT_ready, lnm_g, lnm_b)
                for g in range(G):
                    act.wait_ge(hid_done, it * G + g + 1)
                    act.activation(group_of(hid, g), bank[2 * g + 1][:, :], ACT.Gelu, bias=sb1_).then_inc(hid_ready, 1)

            for g in range(G):
                act.wait_ge(z3T_done, g + 1)
                act.activation(group_of(zsT, g), bank[2 * g][:, :], ACT.Copy).then_inc(z3T_ready, 1)
            act.wait_ge(exp_in["b"], 1)
            act.activation(hot1[:, :, :].rearrange("p e t -> p t e"), hot2[:, :, :].rearrange("p e t -> p t e"),
                           ACT.Exp).then_inc(exp_out["b"], 1)

            def step_b(q, u):
                n, v = 2 * q + u, 1 - u
                turned_rows("b", q, u, NB)
                if exists(n, NB):
                    act.wait_ge(hT_done["b"], n + 1)
                    act.activation(blk_hT[:, u, :, :], bank[3 + u][:, :].rearrange("p (c n) -> p c n", n=P),
                                   ACT.Relu).then_inc(hT_ready["b"], 1)

            skewed(act, NB, step_b)

        @block.vector
        def _(dve):
            count, roots = [0], [0]

            def step(ins):
                count[0] += 1
                ins.then_inc(pre_dve, 1)

            def settle():
                dve.wait_ge(pre_dve, count[0])

            def rsqrt_steps(y, var, tmp, done, base):
                v, t = tmp[:, 0, :], tmp[:, 1, :]
                yi, vi = y.bitcast(I32), v.bitcast(I32)
                steps = [lambda: dve.tensor_scalar(v, var, EPS, None, ALU.add),
                         lambda: dve.tensor_scalar(yi, vi, 1, None, ALU.logical_shift_right),
                         lambda: dve.tensor_scalar(yi, yi, -1, 0x5F3759DF, ALU.mult, ALU.add)]
                for square in (1.0, 4.0, 256.0):
                    steps += [lambda: dve.tensor_tensor(t, y, y, ALU.mult),
                              lambda: dve.tensor_tensor(t, t, v, ALU.mult),
                              lambda q=square: dve.scalar_tensor_tensor(y, t, -3.0 * q, y, ALU.add, ALU.mult)]
                steps += [lambda: dve.tensor_scalar(y, y, -1.0 / 8192.0, None, ALU.mult)]
                assert len(steps) == RSQRT_STEPS
                for n, ins in enumerate(steps):
                    ins().then_inc(done, 1)
                    dve.wait_ge(done, base + n + 1)

            def norm_all(src, dst, n):
                for b in range(B):
                    ins = dve.bn_stats(st_all[0:n, b, :], src[:, b, :])
                step(ins)
                settle()
                for b in range(B):
                    ins = dve.bn_aggr(mv_all[0:n, b, :], st_all[0:n, b, :])
                step(ins)
                settle()
                settle()
                rsqrt_steps(rstd_all[0:n, :], mv_all[0:n, :, 1], rsq_all[0:n], pre_rsqrt, RSQRT_STEPS * roots[0])
                roots[0] += 1
                for b in range(B):
                    ins = dve.tensor_scalar(dst[:, b, :], src[:, b, :], mv_all[0:n, b, 0:1], rstd_all[0:n, b:b + 1],
                                            ALU.subtract, ALU.mult)
                step(ins)
                settle()

            dve.memset(v1[:, :, DH:DH + 1], 1.0)
            step(dve.memset(v2[:, :, DH:DH + 1], 1.0))
            dve.wait_ge(ld_small, 16 * N_SMALL)
            dve.wait_ge(pre_ada, 1)
            adaP = proj[0][:, 0:6 * B].rearrange("p (n j b) -> p n j b", n=3, j=2)
            for n in range(3):
                dve.tensor_scalar(ada[:, n, 0, :], adaP[:, n, 0, :], cols[:, 2 * n:2 * n + 1], 1.0, ALU.add, ALU.add)
                ins = dve.tensor_scalar(ada[:, n, 1, :], adaP[:, n, 1, :], cols[:, 2 * n + 1:2 * n + 2], None, ALU.add)
            step(ins)
            dve.wait_ge(ld_x, 64)
            norm_all(x_sb, x0b, P)
            norm_all(x0b, z_all, P)
            assert count[0] == PRE_Z1
            dve.tensor_tensor(x0b[:, :, :], x0b[:, :, :], R["bo1"].unsqueeze(1).broadcast_to([P, B, D]), ALU.add)
            step(dve.tensor_tensor(x_sb[:, :, :], x_sb[:, :, :], R["ffb2"].unsqueeze(1).broadcast_to([P, B, D]), ALU.add))

            dve.wait_ge(pre_T, 8)
            for b in range(B):
                ins = dve.bn_stats(st_all[0:C, b, :], ctx_n[:, b, :])
            ins.then_inc(ctx_step, 1)
            dve.wait_ge(ctx_step, 1)
            for b in range(B):
                ins = dve.bn_aggr(mv_all[0:C, b, :], st_all[0:C, b, :])
            ins.then_inc(ctx_step, 1)
            dve.wait_ge(ctx_step, 2)
            rsqrt_steps(rstd_all[0:C, :], mv_all[0:C, :, 1], rsq_all[0:C], ctx_rsqrt, 0)
            for b in range(B):
                ins = dve.tensor_scalar(ctx_n[:, b, :], ctx_n[:, b, :], mv_all[0:C, b, 0:1], rstd_all[0:C, b:b + 1],
                                        ALU.subtract, ALU.mult)
            ins.then_inc(ctx_step, 1)

            def bank_of(i, name):
                return proj[PLAN[FIRST_LOOPED if not isinstance(i, int) else i, name][0]]

            def filled(i, name):
                dve.wait_ge(proj_full, at(i, lambda j: PLAN[j, name][1]))

            def stand():
                dve.sem_inc(fence, 1)

            def layernorm(s, b, src, dst):
                stand()
                dve.bn_stats(st[s][:, :], src).then_inc(stats_done[s], 1)
                dve.wait_ge(stats_done[s], b + 1)
                stand()
                dve.bn_aggr(mv[s][:, :], st[s][:, :]).then_inc(mv_ready[s], 1)
                dve.wait_ge(mv_ready[s], b + 1)
                rsqrt_steps(rstd[s][:, :], mv[s][:, 1:2], rsq[s], ln_step[s], RSQRT_STEPS * b)
                if s == "C" and not (isinstance(b, int) and b == 0):
                    dve.wait_ge(z_kept, b)
                dve.tensor_scalar(dst[:, :], src, mv[s][:, 0:1], rstd[s][:, 0:1],
                                  ALU.subtract, ALU.mult).then_inc(z_ready[s], 1)

            def residual(i, name, dst, rest):
                filled(i, name)
                dve.tensor_tensor(dst, bank_of(i, name)[:, 0:D], rest, ALU.add).then_inc(emptied["dve"], 1)
                dve.wait_ge(emptied["dve"], at(i, lambda j: PLAN[j, name][2]))

            def iteration(i, S):
                units = [("B", j) for j in range(4) if "B" in S] + [("A", j) for j in range(4) if "A" in S]
                b, c = i - 1, i - 2
                if "C" in S:
                    filled(i, "gate")
                    dve.tensor_tensor(gpre[:, :, :], bank_of(i, "gate")[:, :].rearrange("p (c n) -> p c n", c=4),
                                      cols[:, 10:14].unsqueeze(2).broadcast_to([P, 4, P]),
                                      ALU.add).then_inc(emptied["dve"], 1)
                for k in range(10):
                    if k < len(units):
                        n = P if units[k][0] == "A" else C
                        s_in = score[k % 2][:, :, 0:n]
                        dve.wait_ge(score_done, at(i, lambda t: units_before(t) + k + 1))
                        dve.tensor_reduce(smax[:, k % 2, :], s_in, X,
                                          ALU.max).then_inc(max_done, 1)
                        dve.wait_ge(max_done, at(i, lambda t: units_before(t) + k + 1))
                        dve.tensor_tensor(shifted[:, k % 2, :, 0:n], s_in,
                                          smax[:, k % 2, :].unsqueeze(2).broadcast_to([P, QH, n]),
                                          ALU.subtract).then_inc(sub_done, 1)
                    if 0 <= k - 2 < len(units):
                        u = k - 2
                        s, j = units[u]
                        dve.wait_ge(pv_done, at(i, lambda t: units_before(t) + u + 1))
                        dve.reciprocal(rden[:, u % 2, :], pvo[:, :, DH]).then_inc(rden_done, 1)
                        dve.wait_ge(rden_done, at(i, lambda t: units_before(t) + u + 1))
                        dve.tensor_tensor(o_nat[s][:, unit_heads(j), :], pvo[:, :, 0:DH],
                                          rden[:, u % 2, :].unsqueeze(2).broadcast_to([P, QH, DH]),
                                          ALU.mult).then_inc(norm_done, 1)
                    if k == 0 and "C" in S:
                        filled(i, "lin")
                        dve.wait_ge(gelu_done, c + 1)
                        for n in range(FF // P):
                            ins = dve.scalar_tensor_tensor(glu[:, n, :], bank_of(i, "lin")[:, n * P:(n + 1) * P],
                                                           cols[:, 6 + n:7 + n], gact[:, n, :], ALU.add, ALU.mult)
                        ins.then_inc(emptied["dve"], 1)
                    if k == 3 and "C" in S:
                        x1 = x_sb[:, bass.ds(c, 1), :].rearrange("p a d -> p (a d)")
                        dve.wait_ge(xbx_ready, c + 1)
                        residual(i, "ffout", x1, xbx[:, :])
                        layernorm("C", c, x1, zC)
                    if k == 7 and "C" in S:
                        filled(i, "logit")
                        dve.tensor_tensor(logits[:, bass.ds(c, 1), 0:7].rearrange("p a e -> p (a e)"),
                                          bank_of(i, "logit")[:, 0:7], R["rb"], ALU.add).then_inc(emptied["dve"], 1)
                    if k == 8 and "B" in S:
                        dve.wait_ge(xab_ready, b + 1)
                        residual(i, "wo2", xb[:, :], xab[:, :])
                        layernorm("B", b, xb[:, :], zB)
                if "A" in S:
                    residual(i, "wo1", xa[:, :], x0b[:, bass.ds(i, 1), :].rearrange("p a d -> p (a d)"))
                    layernorm("A", i, xa[:, :], zA)

            for i in (-1, 0, 1):
                iteration(i, streams(i))
            with dve.Fori(FIRST_LOOPED, B - 1) as i:
                iteration(i, set("ABCN"))
            for i in (B - 1, B, B + 1):
                iteration(i, streams(i))

            def routing(x, n_exp, picks, table, first_block, n_blk):
                done, at_step = rt_step[x], [0]

                def link(ins):
                    at_step[0] += 1
                    ins.then_inc(done, 1)
                    dve.wait_ge(done, at_step[0])

                lg = logits[:, :, 0:n_exp]
                by_e = lambda t: t[:, 0:n_exp, :]
                by_t = lambda t: by_e(t).rearrange("p e t -> p t e")
                flat = lambda t: by_e(t).rearrange("p e t -> p (e t)")
                per_t = lambda t: t.unsqueeze(2).broadcast_to([P, B, n_exp])
                per_e = lambda t: t.unsqueeze(1).broadcast_to([P, B, n_exp])
                iota, iota100 = (per_e(R[n][:, 0:n_exp]) for n in ("iota", "iota100"))

                def first_best(vals, best, one_hot):
                    link(dve.tensor_reduce(best[:, :], vals, X, ALU.max))
                    link(dve.tensor_tensor(by_t(rt), vals, per_t(best[:, :]), ALU.is_equal))
                    link(dve.scalar_tensor_tensor(by_t(rt), by_t(rt), -100.0, iota100, ALU.mult, ALU.add))
                    link(dve.tensor_reduce(idx[:, :], by_t(rt), X, ALU.min))
                    link(dve.tensor_tensor(by_t(one_hot), iota, per_t(idx[:, :]), ALU.is_equal))

                if picks == 2:
                    first_best(lg, top1, hot1)
                    link(dve.scalar_tensor_tensor(by_t(slot), by_t(hot1), -3e38, lg, ALU.mult, ALU.add))
                    first_best(by_t(slot), top2, hot2)
                    link(dve.tensor_tensor(flat(hot), flat(hot1), flat(hot2), ALU.add))
                    dve.sem_inc(hot_ready[x], 1)
                    link(dve.tensor_tensor(top2[:, :], top2[:, :], top1[:, :], ALU.subtract))
                    dve.sem_inc(exp_in[x], 1)
                else:
                    first_best(lg, top1, hot)
                    dve.sem_inc(hot_ready[x], 1)
                    link(dve.tensor_tensor(by_t(hot2), lg, per_t(top1[:, :]), ALU.subtract))
                    dve.sem_inc(exp_in[x], 1)
                dve.wait_ge(rank_done[x], 1)
                t = bank[RANK_BANK[x]]
                w = n_exp * B
                link(dve.tensor_copy(flat(rt), t[:, P:P + w]))
                link(dve.tensor_tensor_scan(flat(run), flat(rt), zeros[:, 0:w], 0.0, ALU.add, ALU.add))
                link(dve.tensor_reduce(cnt[:, 0:n_exp], by_e(rt), X, ALU.add))
                link(dve.tensor_tensor(by_e(slot), cnt[:, 0:n_exp].unsqueeze(2).broadcast_to([P, n_exp, B]),
                                       R["edges"].unsqueeze(1).broadcast_to([P, n_exp, B]), ALU.is_gt))
                link(dve.tensor_reduce(nblk[:, 0:n_exp], by_e(slot), X, ALU.add))
                link(dve.tensor_tensor_scan(cblk[:, 0:n_exp], nblk[:, 0:n_exp], zeros[:, 0:n_exp], 0.0, ALU.add, ALU.add))
                link(dve.tensor_tensor(base[:, 0:n_exp], cblk[:, 0:n_exp], nblk[:, 0:n_exp], ALU.subtract))
                link(dve.scalar_tensor_tensor(base[:, 0:n_exp], base[:, 0:n_exp], float(P), cnt[:, 0:n_exp], ALU.mult, ALU.add))
                link(dve.tensor_tensor(base[:, 0:n_exp], base[:, 0:n_exp], run[:, 0:n_exp, B - 1], ALU.subtract))
                link(dve.tensor_tensor(flat(slot), flat(run), flat(rt), ALU.subtract))
                link(dve.tensor_tensor(flat(slot), flat(slot), t[:, 0:w], ALU.add))
                link(dve.tensor_tensor(by_e(slot), by_e(slot), base[:, 0:n_exp].unsqueeze(2).broadcast_to([P, n_exp, B]), ALU.add))
                for one_hot, f, i in (((hot1, slot1f, slot1), (hot2, slot2f, slot2)) if picks == 2 else ((hot, slot1f, slot1),)):
                    link(dve.tensor_tensor(flat(rt), flat(one_hot), flat(slot), ALU.mult))
                    link(dve.tensor_reduce(f[:, :], by_t(rt), X, ALU.add))
                    link(dve.tensor_copy(i[:, :], f[:, :]))
                nb = n_blk - first_block
                link(dve.tensor_tensor(bge[0:1, 0:nb, 0:n_exp], R["blocks"][0:1, 0:nb].unsqueeze(2).broadcast_to([1, nb, n_exp]),
                                       cblk[0:1, 0:n_exp].unsqueeze(1).broadcast_to([1, nb, n_exp]), ALU.is_ge))
                link(dve.tensor_reduce(bex[0:1, 0:nb], bge[0:1, 0:nb, 0:n_exp], X, ALU.add))
                link(dve.tensor_scalar(table[0:1, first_block:n_blk], bex[0:1, 0:nb], float(n_exp - 1), None, ALU.min))
                dve.sem_inc(routed[x], 1)
                dve.wait_ge(exp_out[x], 1)
                if picks == 2:
                    link(dve.tensor_scalar(top1[:, :], wgt2[:, :], 1.0, None, ALU.add))
                    link(dve.reciprocal(wgt1[:, :], top1[:, :]))
                    link(dve.tensor_tensor(wgt2[:, :], wgt2[:, :], wgt1[:, :], ALU.mult))
                else:
                    link(dve.tensor_reduce(top1[:, :], by_t(hot1), X, ALU.add))
                    link(dve.reciprocal(wgt1[:, :], top1[:, :]))

            first_phase_over(dve)
            dve.memset(vu[:, :, D:D + 1], 1.0)
            routing("a", EA, 2, expert_a, B, NA)

            def step_a(q, u):
                n, v = 2 * q + u, 1 - u
                if exists(n + 1, NA):
                    dve.wait_ge(act_done["a"], n + 2)
                    dve.tensor_tensor(blk_h[:, v, 0:IA], bank[3 + v][:, 0:IA], blk_act[:, v, 0:IA],
                                      ALU.mult).then_inc(h_ready["a"], 1)
                if exists(n - 1, NA):
                    leave("a", q, u, bank[6 + v])

            def leave(x, q, u, t, add=None):
                m, v = 2 * q + u - 1, 1 - u
                dve.wait_ge(y_done[x], m + 1)
                from_one(dve, stored[x][v], 16 * (q - (u == 0)))
                if add is None:
                    dve.tensor_copy(blk_y[:, v, :], t[:, 0:D]).then_inc(y_ready[x], 1)
                else:
                    dve.tensor_tensor(blk_y[:, v, :], t[:, 0:D], add, ALU.add).then_inc(y_ready[x], 1)

            skewed(dve, NA, step_a)

            def group(t, g):
                return t[:, 4 * g:4 * g + 4, :]

            dve.wait_ge(shared_in, 16)
            for g in range(G):
                dve.tensor_tensor(group(x_sb, g), group(x_sb, g), group(z_all, g), ALU.add).then_inc(mean_ready, 1)
                dve.wait_ge(mean_ready, 3 * g + 1)
                dve.wait_ge(picked_a[g], 16 * 8)
                for k, wgt in ((0, wgt1), (1, wgt2)):
                    for n in range(4):
                        b = 4 * g + n
                        ins = dve.scalar_tensor_tensor(x_sb[:, b, :], picked[:, b, k, :], wgt[:, b:b + 1], x_sb[:, b, :],
                                                       ALU.mult, ALU.add)
                    ins.then_inc(mean_ready, 1)
                    dve.wait_ge(mean_ready, 3 * g + 2 + k)
                dve.sem_inc(x2_ready, 1)

            def norm_groups(src, link, done, base, ready, count):
                stand()
                for b in range(B):
                    ins = dve.bn_stats(st_all[:, b, :], src[:, b, :])
                link(ins)
                stand()
                for b in range(B):
                    ins = dve.bn_aggr(mv_all[:, b, :], st_all[:, b, :])
                link(ins)
                rsqrt_steps(rstd_all[:, :], mv_all[:, :, 1], rsq_all, done, base)
                for g in range(G):
                    for b in range(4 * g, 4 * g + 4):
                        ins = dve.tensor_scalar(zs[:, b, :], src[:, b, :], mv_all[:, b, 0:1], rstd_all[:, b:b + 1],
                                                ALU.subtract, ALU.mult)
                    ins.then_inc(ready, 1)
                dve.wait_ge(ready, count)

            def chain(sem_, start):
                at_step = [0]

                def link(ins):
                    at_step[0] += 1
                    ins.then_inc(sem_, 1)
                    dve.wait_ge(sem_, start + at_step[0])
                return link, at_step

            link, _ = chain(sl_step, 0)
            norm_groups(x_sb, link, sl_rsqrt, 0, zp_ready, G)
            dve.wait_ge(exp_out["a"], 2)
            for g in range(G):
                ins = dve.tensor_tensor(group(S, g), group(zs, g), es_b[:, :].unsqueeze(1).broadcast_to([P, 4, D]), ALU.mult)
            link(ins)
            for g in range(G):
                ins = dve.tensor_tensor(group(S, g), group(S, g), R["q_mu"].unsqueeze(1).broadcast_to([P, 4, D]), ALU.add)
                ins.then_inc(S_ready, 1)
            dve.wait_ge(S_ready, G)
            SETUP, STEPS = 3, 6 + 2 * G

            with dve.Fori(0, SLOT_ITERS) as it:
                link, n_steps = chain(sl_step, it * STEPS + SETUP)
                per_round = 3 * RSQRT_STEPS
                at_rsqrt = it * per_round + RSQRT_STEPS
                norm_groups(S, link, sl_rsqrt, at_rsqrt, zq_ready, it * G + G)
                for g in range(G):
                    dve.wait_ge(lg_done, it * G + g + 1)
                    dve.tensor_reduce(nmax[0:C, 4 * g:4 * g + 4], quads(bank[2 * g + 1])[0:C, :, :], X, ALU.max,
                                      negate=True).then_inc(nmax_ready, 1)
                for g in range(G):
                    dve.wait_ge(att_exp, it * G + g + 1)
                    link(dve.reciprocal(rsum[0:C, 4 * g:4 * g + 4], esum[0:C, 4 * g:4 * g + 4]))
                    for b in range(4 * g, 4 * g + 4):
                        ins = dve.tensor_scalar(att[:, b, :], att[:, b, :], rsum[0:C, b:b + 1], 1e-8, ALU.mult, ALU.add)
                    ins.then_inc(att_ready, 1)
                for g in range(G):
                    dve.wait_ge(upd_done, it * G + g + 1)
                    for j in range(2):
                        ins = dve.reciprocal(rcol[:, 4 * g + 2 * j:4 * g + 2 * j + 2],
                                             bank[2 * g + j][:, D:2 * (D + 1):D + 1])
                    link(ins)
                    dve.wait_ge(S_rest, it * G + g + 1)
                    for n in range(4):
                        b = 4 * g + n
                        ins = dve.scalar_tensor_tensor(S[:, b, :], bank[2 * g + n // 2][:, (n % 2) * (D + 1):(n % 2) * (D + 1) + D],
                                                       rcol[:, b:b + 1], s_rest[:, b, :], ALU.mult, ALU.add)
                    ins.then_inc(mid_ready, 1)
                dve.wait_ge(mid_ready, it * G + G)
                norm_groups(S, link, sl_rsqrt, at_rsqrt + RSQRT_STEPS, zm_ready, it * G + G)
                for g in range(G):
                    dve.wait_ge(mlp_done, it * G + g + 1)
                    dve.wait_ge(mid_rest, it * G + g + 1)
                    dve.tensor_tensor(group(S, g), quads(bank[2 * g])[:, :, :], group(s_rest, g), ALU.add).then_inc(sum_ready, 1)
                dve.wait_ge(sum_ready, it * G + G)
                norm_groups(S, link, sl_rsqrt, at_rsqrt + 2 * RSQRT_STEPS, zp_ready, it * G + 2 * G)
                for g in range(G):
                    dve.tensor_tensor(group(S, g), group(zs, g), R["lnp_g"].unsqueeze(1).broadcast_to([P, 4, D]),
                                      ALU.mult).then_inc(sum_ready2, 1)
                    dve.wait_ge(sum_ready2, it * G + g + 1)
                    dve.tensor_tensor(group(S, g), group(S, g), R["lnp_b"].unsqueeze(1).broadcast_to([P, 4, D]),
                                      ALU.add).then_inc(S_ready, 1)
                dve.wait_ge(S_ready, it * G + 2 * G)
                assert n_steps[0] == STEPS, n_steps

            for g in range(G):
                dve.tensor_tensor(group(x_sb, g), group(x_sb, g), group(S, g), ALU.add).then_inc(x3_ready, 1)
            dve.wait_ge(x3_ready, G)

            link, _ = chain(fin_step, 0)
            norm_groups(x_sb, link, fin_rsqrt, 0, z3_ready, G)
            dve.wait_ge(lgb_done, 1)
            link(dve.tensor_tensor(logits[:, :, :], bank[1][:, 0:B * EB].rearrange("p (b e) -> p b e", b=B),
                                   R["b_gate"].unsqueeze(1).broadcast_to([P, B, EB]), ALU.add))
            routing("b", EB, 1, expert_b, 0, NB)

            def expert_of(m):
                return dve.value_load(expert_b[0:1, bass.ds(m, 1)], min_val=0, max_val=EB - 1)

            def step_b(q, u):
                n, v = 2 * q + u, 1 - u
                if exists(n + 1, NB):
                    dve.wait_ge(up_done["b"], n + 2)
                    e = expert_of(n + 1)
                    dve.tensor_tensor(blk_h[:, v, :], bank[1 + v][:, :], b1b[:, bass.ds(e, 1), :].rearrange("p a n -> p (a n)"),
                                      ALU.add).then_inc(h_ready["b"], 1)
                if exists(n - 1, NB):
                    e = expert_of(n - 1)
                    leave("b", q, u, bank[5 + v], b2b[:, bass.ds(e, 1), :].rearrange("p a n -> p (a n)"))

            dve.wait_ge(ld_moe_b, 48)
            skewed(dve, NB, step_b)
            for g in range(G):
                dve.wait_ge(picked_b[g], 16 * 4)
                for b in range(4 * g, 4 * g + 4):
                    ins = dve.scalar_tensor_tensor(x_sb[:, b, :], picked[:, b, 0, :], wgt1[:, b:b + 1], x_sb[:, b, :],
                                                   ALU.mult, ALU.add)
                ins.then_inc(out_ready, 1)

        @block.gpsimd
        def _(pool):
            pool.memset(ones[:, :], 1.0)
            pool.memset(expert_a[:, 0:B], EA)
            pool.memset(zeros[:, :], 0.0).then_inc(consts_ready, 1)

            def tile(t, b):
                return t[:, bass.ds(b, 1), :].rearrange("p a d -> p (a d)")

            def iteration(i, S):
                if "N" in S:
                    if is_iteration(i, -1):
                        pool.wait_ge(pre_act, 4)
                    else:
                        pool.wait_ge(proj_full, at(i, lambda j: PLAN[j - 1, "v1_1"][1]))
                    pool.tensor_copy(hcur1[:, :], tile(h1T, i + 1)).then_inc(hcur_ready, 1)
                if "A" in S:
                    if is_iteration(i, 0):
                        pool.wait_ge(pre_act, 8)
                    else:
                        pool.wait_ge(proj_full, at(i, lambda j: PLAN[j - 1, "v2_1"][1]))
                    pool.tensor_copy(ctxcur[:, :], ctxT[:, bass.ds(i * C, C)]).then_inc(ctxcur_ready, 1)
                if "C" in S:
                    pool.wait_ge(z_ready["C"], i - 1)
                    pool.tensor_copy(tile(z_all, i - 2), zC[:, :]).then_inc(z_kept, 1)
                if "B" in S:
                    pool.wait_ge(emptied["dve"], at(i, lambda j: PLAN[j, "wo2"][2]))
                    pool.tensor_tensor(xbx[:, :], xb[:, :], tile(x_sb, i - 1), ALU.add).then_inc(xbx_ready, 1)
                if "A" in S:
                    pool.wait_ge(emptied["dve"], at(i, lambda j: PLAN[j, "wo1"][2]))
                    pool.tensor_tensor(xab[:, :], xa[:, :], R["bo2"], ALU.add).then_inc(xab_ready, 1)

            for i in (-1, 0, 1):
                iteration(i, streams(i))
            with pool.Fori(FIRST_LOOPED, B - 1) as i:
                iteration(i, set("ABCN"))
            for i in (B - 1, B, B + 1):
                iteration(i, streams(i))

            def scatter(x, picks, dst):
                pool.wait_ge(zeroed, 32)
                pool.wait_ge(routed[x], 1)
                for b in range(B):
                    for slots in picks:
                        pool.indirect_dma_start(dst, bass.IndirectOffsetOnAxis(ap=slots[:, b:b + 1], axis=0),
                                                z_all[:, b, :], None).then_inc(scattered[x], 16)

            def pick(x, picks, src, n_blk, groups):
                for u in range(2):
                    pool.wait_ge(stored[x][u], 16 * ((n_blk + 1 - u) // 2))
                for b in range(B):
                    for k, slots in enumerate(picks):
                        pool.indirect_dma_start(picked[:, b, k, :], None, src,
                                                bass.IndirectOffsetOnAxis(ap=slots[:, b:b + 1], axis=0)).then_inc(groups[b // 4], 16)

            scatter("a", (slot1, slot2), rows_a)
            pool.wait_ge(pre_slot_done, 6 * G)
            pick("a", (slot1, slot2), outs_a, NA, picked_a)

            def group(t, g):
                return t[:, 4 * g:4 * g + 4, :]

            pool.wait_ge(ld_cond, 16)
            for g in range(G):
                ins = pool.tensor_tensor(group(cb2, g), group(cb2, g), R["b2"].unsqueeze(1).broadcast_to([P, 4, D]), ALU.add)
            ins.then_inc(filled_rows, 1)
            pool.wait_ge(filled_rows, 1)
            with pool.Fori(0, SLOT_ITERS) as it:
                for g in range(G):
                    pool.wait_ge(S_ready, it * G + g + 1)
                    pool.tensor_tensor(group(s_rest, g), group(S, g), R["bu"].unsqueeze(1).broadcast_to([P, 4, D]),
                                       ALU.add).then_inc(S_rest, 1)
                for g in range(G):
                    pool.wait_ge(mid_ready, it * G + g + 1)
                    pool.tensor_tensor(group(s_rest, g), group(S, g), group(cb2, g), ALU.add).then_inc(mid_rest, 1)
            pool.wait_ge(z3_ready, G)
            scatter("b", (slot1,), rows_b)
            pick("b", (slot1,), outs_b, NB, picked_b)


def layout(I):
    import numpy as np

    arr = {
        "x": I["x"], "ctx": I["ctx_1024"], "cond_t": I["cond_1024"].T,
        "norm_w": np.stack([I[f"L0_xcond_norm{n}_w"] for n in (1, 2, 3)]),
        "eye": np.eye(P, dtype=np.float32),
        "att_w": np.stack([[I[f"L0_xcond_attn{a}_w{j}"] for j in "qkv"] for a in (1, 2)]),
        "att_wo": np.stack([I[f"L0_xcond_attn{a}_wo"] for a in (1, 2)]),
        "ff_w1": I["L0_xcond_ff_w1"], "ff_w2": I["L0_xcond_ff_w2"],
        "wr_t": I["L0_ffn_wr"].T,
    }
    col_list = [I[f"L0_xcond_norm{n}_b"].reshape(2, D) for n in (1, 2, 3)]
    col_list += [I["L0_xcond_ff_b1"].reshape(2 * FF // P, P)]
    col_list += [I[f"L1_xcond_{n}"].reshape(1, D) for n in ("lnkv_g", "lnkv_b", "lnq_g", "lnq_b", "lnm_g", "lnm_b", "bk", "bq", "b1", "bv")]
    arr["cols"] = np.concatenate(col_list).T
    arr["gate_up"] = np.concatenate([np.concatenate([I["L0_ffn_rg"], I["L0_ffn_ru"]], 1),
                                     np.concatenate([I["L0_ffn_sg"], I["L0_ffn_su"]], 0)[None]]).transpose(2, 0, 1)
    downs = np.concatenate([I["L0_ffn_rd"], I["L0_ffn_sd"][None]]).transpose(0, 2, 1)
    downs = np.concatenate([downs, np.zeros((EA + 1, CA * P - IA, D), np.float32)], 1)
    arr["down"] = downs.reshape(EA + 1, CA, P, D).transpose(2, 0, 1, 3)
    arr["tri"] = np.triu(np.ones((P, P), np.float32), 1)
    arr["wgate"] = I["L1_ffn_w_gate"]
    arr["slot_w"] = np.stack([I["L1_xcond_wk"], I["L1_xcond_wv"], I["L1_xcond_wq"].T, I["L1_xcond_wu"],
                              I["L1_xcond_w1"], I["L1_xcond_w2"]])
    arr["cond"] = I["cond_1024"]
    arr["w1b"], arr["w2b"] = I["L1_ffn_W1"], I["L1_ffn_W2"]
    arr["b12"] = np.concatenate([I["L1_ffn_b1"].reshape(-1), I["L1_ffn_b2"].reshape(-1)])
    shape_rows = {"iota": np.arange(EB), "iota100": np.arange(EB) + 100, "edges": np.arange(B) * P, "blocks": np.arange(NR)}
    rows = [("bo1", "L0_xcond_attn1_bo"), ("bo2", "L0_xcond_attn2_bo"), ("ffb2", "L0_xcond_ff_b2"), ("rb", "L0_ffn_rb")]
    rows += [(n, "L1_xcond_" + n) for n in ("q_mu", "q_logsig", "bu", "b2", "lnp_g", "lnp_b")] + [("b_gate", "L1_ffn_b_gate")]
    arr["rows"] = np.concatenate([I[k].reshape(-1) for _, k in rows] + [v.astype(np.float32) for v in shape_rows.values()])
    names = [(n, I[k].size) for n, k in rows] + [(n, v.size) for n, v in shape_rows.items()]
    return {k: np.ascontiguousarray(v) for k, v in arr.items()}, names


def kernel(**inputs):
    import numpy as np
    import concourse.bacc as bacc
    from concourse.bass_utils import run_bass_kernel_spmd

    arrays, row_names = layout({k: np.asarray(v) for k, v in inputs.items()})
    nc = bacc.Bacc("TRN2", target_bir_lowering=False, num_devices=1)
    args = {k: nc.dram_tensor(k, a.shape, mybir.dt.from_np(a.dtype), kind="ExternalInput").ap() for k, a in arrays.items()}
    out = nc.dram_tensor("out", (B, P, D), F32, kind="ExternalOutput").ap()
    program(nc, args, row_names, out)
    r = run_bass_kernel_spmd(nc, [arrays], core_ids=[0])
    return r.results[0]["out"]
```

```python
from contextlib import ExitStack

import concourse.bass as bass
from concourse import mybir

F32 = mybir.dt.float32
I32 = mybir.dt.int32
ALU = mybir.AluOpType
ACT = mybir.ActivationFunctionType
X = mybir.AxisListType.X

P = 128
B = 16
D = 128
C = 77
H = 16
DH = 64
INNER = H * DH
NCH = INNER // P
QH = 4
FF = 512
EPS = 1e-5
TOK = B * P
EA, IA = 7, 352
CA = -(-IA // P)
EB, FB = 8, 512
NR = (2 * TOK + EA * (P - 1)) // P
NB = (TOK + EB * (P - 1)) // P
SLOT_ITERS = 3
ROW = D + 2
NSLOT = 4

PROJ_USES = [
    ("q2_0", "B", "act"), ("q2_1", "B", "act"), ("gate", "C", "dve"), ("lin", "C", "dve"),
    ("ffout", "C", "dve"), ("zT", "C", "act"), ("k2_0", "A", "act"), ("k2_1", "A", "act"),
    ("o2T_0", "B", "act"), ("o2T_1", "B", "act"), ("logit", "C", "dve"),
    ("v2_0", "A", "act"), ("v2_1", "A", "act"), ("wo2", "B", "dve"),
    ("q1_0", "N", "act"), ("q1_1", "N", "act"), ("o1T_0", "A", "act"), ("o1T_1", "A", "act"),
    ("h3T", "B", "act"), ("k1_0", "N", "act"), ("wo1", "A", "dve"), ("k1_1", "N", "act"),
    ("v1_0", "N", "act"), ("v1_1", "N", "act"), ("h2T", "A", "act"),
]
NBANK = 3
RSQRT_STEPS = 13
FIRST_LOOPED = 2


def streams(i):
    return {s for s, b in (("A", i), ("B", i - 1), ("C", i - 2), ("N", i + 1)) if 0 <= b < B}


def proj_plan():
    full, done, last, plan = 0, {"act": 0, "dve": 0}, [None] * NBANK, {}
    for i in range(-1, B + 2):
        for n, (name, stream, eng) in enumerate(PROJ_USES):
            if stream not in streams(i):
                continue
            full += 1
            done[eng] += 1
            plan[i, name] = (n % NBANK, full, done[eng], last[n % NBANK])
            last[n % NBANK] = (eng, done[eng])
    return plan


def units_before(i):
    return sum(QH * (("A" in streams(j)) + ("B" in streams(j))) for j in range(-1, i))


def unit_heads(j):
    return slice(8 * (j // 2) + j % 2, 8 * (j // 2) + 8, 2)


def is_iteration(i, n):
    return isinstance(i, int) and i == n


def at(i, count):
    if isinstance(i, int):
        return count(i)
    a, b = count(FIRST_LOOPED), count(FIRST_LOOPED + 1)
    assert all(count(j) == a + (j - FIRST_LOOPED) * (b - a) for j in range(FIRST_LOOPED, B - 1))
    return i * (b - a) + (a - FIRST_LOOPED * (b - a))


def from_one(eng, sem, count):
    if not isinstance(count, int) or count >= 1:
        eng.wait_ge(sem, count)


def skewed(eng, nblk, step):
    rounds = (nblk - 2 * NSLOT + 1) // NSLOT
    for n in range(-2, NSLOT + 1):
        step(n // NSLOT, n % NSLOT)
    with eng.Fori(1, 1 + rounds) as q:
        for u in range(1, NSLOT):
            step(q, u)
        step(q + 1, 0)
    for n in range(NSLOT * (rounds + 1) + 1, nblk + 1):
        step(n // NSLOT, n % NSLOT)


def exists(n, nblk):
    return not isinstance(n, int) or 0 <= n < nblk


def program(nc, A, row_names, out):
    PLAN = proj_plan()
    with ExitStack() as ctx:
        def sb(name, *shape, dt=F32):
            return ctx.enter_context(nc.sbuf_tensor("sb_" + name, list(shape), dt))

        phase1 = ctx.enter_context(ExitStack())

        def sb1(name, *shape, dt=F32):
            return phase1.enter_context(nc.sbuf_tensor("sb_" + name, list(shape), dt))

        def sem(name):
            return ctx.enter_context(nc.semaphore(name))

        eye = sb("eye", P, P)
        tri = sb("tri", P, P)
        ones = sb("ones", P, P)
        zeros = sb("zeros", P, P)
        cols = sb("cols", P, 24)
        rows = sb("rows", P, A["rows"].shape[0])
        x_sb = sb("x", P, B, D)
        z_all = sb("z_all", P, B, D)
        ctx_n = sb("ctx", C, B, D)
        logits = sb("logits", P, B, EB)
        gate_up = sb("gate_up", P, EA + 1, 2 * IA)
        down = sb("down", P, EA + 1, CA, D)
        wr = sb("wr", P, EA)
        wgate = sb("wgate", P, EB)
        slot_w = sb("slot_w", P, 6, D)
        st_all = sb("st_all", P, B, 6)
        mv_all = sb("mv_all", P, B, 2)
        rsq_all = sb("rsq_all", P, 2, B)
        rstd_all = sb("rstd_all", P, B)
        tok_ids = sb("tok_ids", P, 3, B)
        expert_a = sb("expert_a", 1, NR, dt=I32)
        expert_b = sb("expert_b", 1, NB, dt=I32)

        x0b = sb1("x0b", P, B, D)
        h1T = sb1("h1T", P, B, P)
        ctxT = sb1("ctxT", P, B * C)
        cond_t = sb1("cond_t", P, B)
        nw = sb1("norm_w", P, 3, 2 * D)
        ada = sb1("ada", P, 3, 2, B)
        watt = sb1("watt", P, 2, 4, INNER)
        w1 = sb1("ff_w1", P, 2 * FF)
        w2 = sb1("ff_w2", P, FF // P, D)
        q1T, k1T, q2T = (sb1(n, P, NCH, P) for n in ("q1T", "k1T", "q2T"))
        k2T = sb1("k2T", P, NCH, C)
        v1 = sb1("v1", P, H, DH + 1)
        v2 = sb1("v2", C, H, DH + 1)
        shifted = sb1("shifted", P, 2, QH, P)
        expd = sb1("expd", P, 2, QH, P)
        probT = sb1("probT", P, 2, QH, P)
        smax = sb1("smax", P, 2, QH)
        rden = sb1("rden", P, 2, QH)
        o_nat = {s: sb1("o" + s, P, H, DH) for s in "AB"}
        oT = {s: sb1("oT" + s, P, NCH, P) for s in "AB"}
        xa, xab, xb, xbx = (sb1(n, P, D) for n in ("xa", "xab", "xb", "xbx"))
        zA, zB, zC = (sb1("z" + s, P, D) for s in "ABC")
        hcur1, h2T, h3T, zT = (sb1(n, P, P) for n in ("hcur1", "h2T", "h3T", "zT"))
        ctxcur = sb1("ctxcur", P, C)
        gpre = sb1("gpre", P, FF // P, P)
        gact = sb1("gact", P, FF // P, P)
        glu = sb1("glu", P, FF // P, P)
        st = {s: sb1("st" + s, P, 6) for s in "ABC"}
        mv = {s: sb1("mv" + s, P, 2) for s in "ABC"}
        rsq = {s: sb1("rsq" + s, P, 2, 1) for s in "ABC"}
        rstd = {s: sb1("rstd" + s, P, 1) for s in "ABC"}
        phase1.close()

        w1b = sb("w1b", P, EB, FB)
        w2b = sb("w2b", P, EB, FB // P, D)
        spent = gate_up[:, :, :].rearrange("p e n -> p (e n)")
        b1b = spent[:, 0:EB * FB].rearrange("p (e n) -> p e n", e=EB)
        b2b = spent[:, EB * FB:EB * (FB + D)].rearrange("p (e n) -> p e n", e=EB)
        S = sb("S", P, B, D)
        s_rest = sb("s_rest", P, B, D)
        zs = z_all
        zsT = sb("zsT", P, B, P)
        hid = sb("hid", P, B, P)
        att_or_sent = sb("att_or_sent", P, B * ROW)
        att = att_or_sent[0:C, 0:B * P].rearrange("c (b t) -> c b t", b=B)
        cb2 = sb("cb2", P, B, D)
        kq = sb("kq", P, B, C)
        kqb = sb("kqb", 1, B, C)
        vu = sb("vu", C, B, D + 1)
        es_b = sb("es_b", P, D)
        picked = sb("picked", P, B, 2, D)
        xinT, kkT, vT = (picked[:, 5 * n:5 * n + 5, :, :].rearrange("p b k d -> p (b k d)")[:, 0:B * C].rearrange(
            "p (b c) -> p b c", b=B) for n in range(3))
        sh_act = hid[:, 0:4 * CA, :].rearrange("p (c b) t -> p c (b t)", c=CA)
        sh_h = [t[:, 0:4 * CA, :].rearrange("p (c b) t -> p c (b t)", c=CA) for t in (S, s_rest)]
        sent = [t.rearrange("p (b d) -> p b d", b=B) for t in (sb("sent", P, B * ROW)[:, :], att_or_sent[:, :])]
        blk_x = sb("blk_x", P, NSLOT, ROW)
        meta = sb("meta", P, NR, 2)
        dest = sb("dest", P, NSLOT, dt=I32)
        blk_xT = sb("blk_xT", P, 2, P)
        blk_act, blk_h = (hid[:, 8 * n:8 * n + 8, :].rearrange("p (u c) t -> p u (c t)", u=2) for n in range(2))
        blk_hT = zsT[:, 0:8, :].rearrange("p (u c) t -> p u c t", u=2)
        blk_y = sb("blk_y", P, NSLOT, D)
        hot1, hot2, hot, run, slot, rt = (sb(n, P, EB, B) for n in ("hot1", "hot2", "hot", "run", "slot", "rt"))
        top1, top2, idx, wgt1, wgt2, slot1f, slot2f = (
            sb(n, P, B) for n in ("top1", "top2", "idx", "wgt1", "wgt2", "slot1f", "slot2f"))
        slot1, slot2 = (sb(n, P, B, dt=I32) for n in ("slot1", "slot2"))
        cnt, nblk, cblk, base = (sb(n, P, EB) for n in ("cnt", "nblk", "cblk", "base"))
        bge = sb("bge", 1, NR, EB)
        bex = sb("bex", 1, NR)
        nmax, esum, rsum, rcol = (sb(n, P, B) for n in ("nmax", "esum", "rsum", "rcol"))

        rows_a = nc.dram_tensor("rows_a", (NR * P, ROW), F32, kind="Internal").ap()
        rows_b = nc.dram_tensor("rows_b", (NB * P, ROW), F32, kind="Internal").ap()
        back_a = nc.dram_tensor("back_a", (2 * TOK + NR * P, D), F32, kind="Internal").ap()
        back_b = nc.dram_tensor("back_b", (TOK + NB * P, D), F32, kind="Internal").ap()

        wq, wk, wv = ([watt[:, a, j, :] for a in range(2)] for j in range(3))
        wo = [watt[:, a, 3, :].rearrange("p (c n) -> p c n", c=NCH) for a in range(2)]
        R = {}
        at_col = 0
        for name, n in row_names:
            R[name] = rows[:, at_col:at_col + n]
            at_col += n
        wks, wvs, wqTs, wus, w1s, w2s = (slot_w[:, n, :] for n in range(6))
        lnkv_g, lnkv_b, lnq_g, lnq_b, lnm_g, lnm_b, bk, bq, sb1_, bv = (cols[:, 14 + n:15 + n] for n in range(10))

        bank = [ctx.enter_context(nc.psum_tensor(f"bank{n}", [P, 512], F32)) for n in range(8)]
        proj = bank[0:NBANK]

        def quads(t):
            return t[:, :].rearrange("p (h n) -> p h n", h=QH)

        score = [quads(t) for t in bank[3:5]]
        trans = [quads(t) for t in bank[5:7]]
        pvo = bank[7][:, 0:QH * (DH + 1)].rearrange("p (h d) -> p h d", h=QH)

        ld_x, ld_small, ld_att1, ld_att2, ld_ff, ld_ctx = (
            sem(n) for n in ("ld_x", "ld_small", "ld_att1", "ld_att2", "ld_ff", "ld_ctx"))
        pre_dve = sem("pre_dve")
        pre_ada = sem("pre_ada")
        pre_T = sem("pre_T")
        pre_act = sem("pre_act")
        hcur_ready = sem("hcur_ready")
        ctxcur_ready = sem("ctxcur_ready")
        proj_full = sem("proj_full")
        emptied = {"act": sem("proj_act"), "dve": sem("proj_dve")}
        score_done, max_done, sub_done, exp_done = (
            sem(n) for n in ("score_done", "max_done", "sub_done", "exp_done"))
        T_done, probT_ready, pv_done, rden_done, norm_done = (
            sem(n) for n in ("T_done", "probT_ready", "pv_done", "rden_done", "norm_done"))
        gelu_done = sem("gelu_done")
        stats_done, mv_ready, ln_step = (
            {s: sem(n + s) for s in "ABC"} for n in ("stats_done", "mv_ready", "ln_step"))
        pre_rsqrt = sem("pre_rsqrt")
        z_ready = {s: sem("z_ready" + s) for s in "ABC"}
        xab_ready, xbx_ready, z_kept = (sem(n) for n in ("xab_ready", "xbx_ready", "z_kept"))
        out_sem = sem("out_sem")

        ld_moe, ld_slot, ld_cond, ld_moe_b, zeroed, consts_ready, filled_rows = (
            sem(n) for n in ("ld_moe", "ld_slot", "ld_cond", "ld_moe_b", "zeroed", "consts_ready", "filled_rows"))
        pre_slot_full, pre_slot_done = sem("pre_slot_full"), sem("pre_slot_done")
        ctx_step, ctx_rsqrt = sem("ctx_step"), sem("ctx_rsqrt")
        rt_step = {x: sem("rt_step_" + x) for x in "ab"}
        hot_ready, rank_done, exp_in, exp_out, routed, scattered = (
            {x: sem(n + x) for x in "ab"} for n in (
                "hot_ready_", "rank_done_", "exp_in_", "exp_out_", "routed_", "scattered_"))
        blk_in, returned = ({x: [sem(f"{n}_{x}{u}") for u in range(NSLOT)] for x in "ab"} for n in ("blk_in", "returned"))
        meta_kept, dest_ready = ({x: sem(n + x) for x in "ab"} for n in ("meta_kept_", "dest_ready_"))
        sent_ready = sem("sent_ready")
        sh_T_done, sh_T_ready, sh_up_done, sh_act_done, sh_h_ready, sh_y_done, sh_added = (
            sem("sh_" + n) for n in ("T_done", "T_ready", "up_done", "act_done", "h_ready", "y_done", "added"))
        xT_done, xT_ready, up_done, act_done, h_ready, hT_done, hT_ready, y_done, y_ready = (
            {x: sem(n + x) for x in "ab"} for n in (
                "xT_done_", "xT_ready_", "up_done_", "act_done_", "h_ready_", "hT_done_", "hT_ready_", "y_done_", "y_ready_"))
        picked_a, picked_b = ([sem(f"picked_{x}{g}") for g in range(4)] for x in "ab")
        mean_ready, x2_ready = sem("mean_ready"), sem("x2_ready")
        sl_step, sl_rsqrt = sem("sl_step"), sem("sl_rsqrt")
        zq_ready, zqT_done, zqT_ready, lg_done, nmax_ready, att_exp, att_ready, upd_done, mid_ready, mid_rest = (
            sem("sl_" + n) for n in ("zq_ready", "zqT_done", "zqT_ready", "lg_done", "nmax_ready", "att_exp",
                                     "att_ready", "upd_done", "mid_ready", "mid_rest"))
        zm_ready, zmT_done, zmT_ready, hid_done, hid_ready, mlp_done, sum_ready, zp_ready, S_ready, S_rest = (
            sem("sl_" + n) for n in ("zm_ready", "zmT_done", "zmT_ready", "hid_done", "hid_ready", "mlp_done",
                                     "sum_ready", "zp_ready", "S_ready", "S_rest"))
        x3_ready, z3_ready, z3T_done, z3T_ready, lgb_done = (
            sem(n) for n in ("x3_ready", "z3_ready", "z3T_done", "z3T_ready", "lgb_done"))
        fin_step, fin_rsqrt = sem("fin_step"), sem("fin_rsqrt")
        fence, fence_pool = sem("fence"), sem("fence_pool")
        out_ready, sum_ready2 = sem("out_ready"), sem("sl_scaled")
        G = 4

        NBLK = {"a": NR, "b": NB}
        RANK_BANK = {"a": 7, "b": 2}

        def first_phase_over(eng):
            eng.wait_ge(emptied["dve"], PLAN[B + 1, "logit"][2])
            eng.wait_ge(z_kept, B + 1)

        N_SMALL = 6
        PRE_Z1 = 8
        block = ctx.enter_context(nc.Block())

        @block.sync
        def _(sp):
            for g in range(4):
                sp.dma_start(x_sb[:, 4 * g:4 * g + 4, :],
                             A["x"][4 * g:4 * g + 4].rearrange("b s d -> s b d")).then_inc(ld_x, 16)
            sp.dma_start(cond_t[:, :], A["cond_t"]).then_inc(ld_small, 16)
            sp.dma_start(nw[:, :, :], A["norm_w"].rearrange("n p d -> p n d")).then_inc(ld_small, 16)
            sp.dma_start(eye[:, :], A["eye"]).then_inc(ld_small, 16)
            sp.dma_start(cols[:, :], A["cols"]).then_inc(ld_small, 16)
            nrow = A["rows"].shape[0]
            sp.dma_start(rows[:, :], A["rows"].partition_broadcast(P)).then_inc(ld_small, 16)
            sp.dma_start(wr[:, 0:7], A["wr_t"]).then_inc(ld_small, 16)
            for j in range(3):
                sp.dma_start(watt[:, 0, j, :], A["att_w"][0, j]).then_inc(ld_att1, 16)
            sp.dma_start(ctx_n[:, :, :], A["ctx"].rearrange("b c d -> c b d")).then_inc(ld_ctx, 16)
            sp.dma_start(wo[0], A["att_wo"][0].rearrange("(c p) n -> p c n", p=P)).then_inc(ld_att1, 16)
            for j in range(3):
                sp.dma_start(watt[:, 1, j, :], A["att_w"][1, j]).then_inc(ld_att2, 16)
            sp.dma_start(wo[1], A["att_wo"][1].rearrange("(c p) n -> p c n", p=P)).then_inc(ld_att2, 16)
            sp.dma_start(w1[:, :], A["ff_w1"]).then_inc(ld_ff, 16)
            sp.dma_start(w2[:, :, :], A["ff_w2"].rearrange("(c p) n -> p c n", p=P)).then_inc(ld_ff, 16)
            sp.dma_start(gate_up[:, :, :], A["gate_up"]).then_inc(ld_moe, 16)
            sp.dma_start(down[:, :, :, :], A["down"]).then_inc(ld_moe, 16)
            sp.dma_start(tri[:, :], A["tri"]).then_inc(ld_moe, 16)
            sp.dma_start(tok_ids[:, :, :], A["tok_ids"]).then_inc(ld_slot, 16)
            sp.dma_start(wgate[:, :], A["wgate"]).then_inc(ld_slot, 16)
            sp.dma_start(slot_w[:, :, :], A["slot_w"].rearrange("n p d -> p n d")).then_inc(ld_slot, 16)
            sp.wait_ge(consts_ready, 1)
            for t, n, pad in ((rows_a, NR, A["pad_a"]), (rows_b, NB, A["pad_b"])):
                sp.dma_start(t[:, 0:D].rearrange("(n p) d -> p n d", p=P),
                             zeros[:, :].unsqueeze(1).broadcast_to([P, n, D])).then_inc(zeroed, 16)
                sp.dma_start(t[:, D:], pad).then_inc(zeroed, 16)
            first_phase_over(sp)
            sp.dma_start(cb2[:, :, :].rearrange("p b d -> p (b d)"),
                         A["cond"].rearrange("b d -> (b d)").partition_broadcast(P)).then_inc(ld_cond, 16)

            def load(x, src, m, u):
                from_one(sp, xT_done[x], m - NSLOT + 1)
                from_one(sp, meta_kept[x], m - NSLOT + 1)
                sp.dma_start(blk_x[:, u, 0:ROW], src[bass.ds(m * P, P), 0:ROW]).then_inc(blk_in[x][u], 16)

            def load_blocks(x, src):
                rounds = NBLK[x] // NSLOT
                for m in range(NSLOT):
                    load(x, src, m, m)
                with sp.Fori(1, rounds) as q:
                    for u in range(NSLOT):
                        load(x, src, NSLOT * q + u, u)
                for m in range(NSLOT * rounds, NBLK[x]):
                    load(x, src, m, m % NSLOT)
                for u in range(NSLOT):
                    sp.wait_ge(returned[x][u], 16 * len(range(u, NBLK[x], NSLOT)))

            sp.wait_ge(scattered["a"], 16 * 2 * B)
            load_blocks("a", rows_a)
            for g in range(G):
                sp.dma_start(picked[:, 4 * g:4 * g + 4, :, :],
                             back_a[8 * g * P:8 * (g + 1) * P, :].rearrange("(b s k) d -> s b k d", s=P, k=2)).then_inc(picked_a[g], 16)
            sp.dma_start(w1b[:, :, :], A["w1b"].rearrange("e p n -> p e n")).then_inc(ld_moe_b, 16)
            sp.dma_start(w2b[:, :, :, :], A["w2b"].rearrange("e (c p) d -> p e c d", p=P)).then_inc(ld_moe_b, 16)
            sp.dma_start(spent[:, 0:EB * (FB + D)], A["b12"].partition_broadcast(P)).then_inc(ld_moe_b, 16)
            sp.wait_ge(scattered["b"], 16 * B)
            load_blocks("b", rows_b)
            for g in range(G):
                sp.dma_start(picked[:, 4 * g:4 * g + 4, 0, :],
                             back_b[4 * g * P:4 * (g + 1) * P, :].rearrange("(b s) d -> s b d", s=P)).then_inc(picked_b[g], 16)
            for g in range(G):
                sp.wait_ge(out_ready, g + 1)
                sp.dma_start(out[4 * g:4 * g + 4].rearrange("b s d -> s b d"),
                             x_sb[:, 4 * g:4 * g + 4, :]).then_inc(out_sem, 16)
            sp.wait_ge(out_sem, 16 * G)

        @block.tensor
        def _(pe):
            pe.wait_ge(ld_small, 16 * N_SMALL)
            for n in range(3):
                for j in range(2):
                    mm = pe.matmul(proj[0][:, (2 * n + j) * B:(2 * n + j + 1) * B], nw[:, n, j * D:(j + 1) * D],
                                   cond_t[:, :], start=True, stop=True)
            mm.then_inc(pre_ada, 1)
            pe.wait_ge(pre_dve, PRE_Z1)
            for g in range(8):
                if g == 4:
                    pe.wait_ge(ld_ctx, 16)
                if g >= 2:
                    pe.wait_ge(pre_act, g - 1)
                for n in range(4):
                    b = 4 * (g % 4) + n
                    if g < 4:
                        mm = pe.transpose(trans[g % 2][:, n, :], z_all[:, b, :], eye[:, :])
                    else:
                        mm = pe.transpose(trans[g % 2][:, n, 0:C], ctx_n[:, b, :], eye[0:C, 0:C])
                mm.then_inc(pre_T, 1)

            def use(i, name):
                bank, _, _, free = PLAN[FIRST_LOOPED if not isinstance(i, int) else i, name]
                if free is not None:
                    pe.wait_ge(emptied[free[0]], at(i, lambda j: PLAN[j, name][3][1]))
                return proj[bank]

            def qk_proj(i, name, w, src, half, n):
                t = use(i, name)
                for c in range(4):
                    mm = pe.matmul(t[:, c * n:(c + 1) * n], w[:, (4 * half + c) * P:(4 * half + c + 1) * P], src,
                                   start=True, stop=True)
                mm.then_inc(proj_full, 1)

            def v_proj(i, name, w, src, half, n):
                t = use(i, name)
                pe.matmul(t[0:n, :], src, w[:, half * 512:(half + 1) * 512],
                          start=True, stop=True).then_inc(proj_full, 1)

            def turn(i, name, src):
                pe.transpose(use(i, name)[:, 0:P], src[:, :], eye[:, :]).then_inc(proj_full, 1)

            def o_turn(i, name, o, half):
                t = use(i, name)
                for c in range(4):
                    mm = pe.transpose(t[:, c * P:(c + 1) * P],
                                      o[:, 2 * (4 * half + c):2 * (4 * half + c) + 2, :].rearrange("p h d -> p (h d)"),
                                      eye[:, :])
                mm.then_inc(proj_full, 1)

            def o_proj(i, name, s, w):
                t = use(i, name)
                for c in range(NCH):
                    mm = pe.matmul(t[:, 0:D], oT[s][:, c, :], w[:, c, :], start=(c == 0), stop=(c == NCH - 1))
                mm.then_inc(proj_full, 1)

            def score_unit(i, u, s, j):
                q, k, n = (q1T, k1T, P) if s == "A" else (q2T, k2T, C)
                if not (isinstance(i, int) and units_before(i) + u < 2):
                    pe.wait_ge(sub_done, at(i, lambda t: units_before(t) + u - 1))
                p = slice(DH * (j % 2), DH * (j % 2) + DH)
                for h in range(QH):
                    mm = pe.matmul(score[u % 2][:, h, 0:n], q[p, 4 * (j // 2) + h, :],
                                   k[p, 4 * (j // 2) + h, 0:n], start=True, stop=True)
                mm.then_inc(score_done, 1)

            def prob_turn(i, u, s):
                n = P if s == "A" else C
                pe.wait_ge(exp_done, at(i, lambda t: units_before(t) + u + 1))
                if not (isinstance(i, int) and units_before(i) + u < 2):
                    pe.wait_ge(probT_ready, at(i, lambda t: units_before(t) + u - 1))
                for h in range(QH):
                    mm = pe.transpose(trans[u % 2][0:n, h, :], expd[:, u % 2, h, 0:n], eye[:, :])
                mm.then_inc(T_done, 1)

            def pv_unit(i, u, s, j):
                n, v = (P, v1) if s == "A" else (C, v2)
                pe.wait_ge(probT_ready, at(i, lambda t: units_before(t) + u + 1))
                if not (isinstance(i, int) and units_before(i) + u < 1):
                    pe.wait_ge(norm_done, at(i, lambda t: units_before(t) + u))
                for h in range(QH):
                    mm = pe.matmul(pvo[:, h, :], probT[0:n, u % 2, h, :], v[:, unit_heads(j), :][:, h, :],
                                   start=True, stop=True)
                mm.then_inc(pv_done, 1)

            def emptied_by(i, name, ago=0):
                eng = [e for n, _, e in PROJ_USES if n == name][0]
                pe.wait_ge(emptied[eng], at(i, lambda j: PLAN[j - ago, name][2]))

            def iteration(i, S):
                units = [("B", j) for j in range(4) if "B" in S] + [("A", j) for j in range(4) if "A" in S]
                if "B" in S:
                    emptied_by(i, "h2T", 1)
                    qk_proj(i, "q2_0", wq[1], h2T[:, :], 0, P)
                    qk_proj(i, "q2_1", wq[1], h2T[:, :], 1, P)
                if "C" in S:
                    pe.wait_ge(ld_ff, 32)
                    emptied_by(i, "h3T", 1)
                    qk_proj(i, "gate", w1[:, FF:2 * FF], h3T[:, :], 0, P)
                    qk_proj(i, "lin", w1[:, 0:FF], h3T[:, :], 0, P)
                for k in range(10):
                    if k < len(units):
                        s, j = units[k]
                        if j == 0:
                            if s == "A":
                                emptied_by(i, "k1_1", 1)
                            else:
                                emptied_by(i, "q2_1")
                        score_unit(i, k, s, j)
                    if 0 <= k - 2 < len(units):
                        s, j = units[k - 2]
                        if j == 0:
                            emptied_by(i, "v1_1" if s == "A" else "v2_1", 1)
                        pv_unit(i, k - 2, s, j)
                    if 0 <= k - 1 < len(units):
                        prob_turn(i, k - 1, units[k - 1][0])
                    if k == 2 and "C" in S:
                        t = use(i, "ffout")
                        emptied_by(i, "lin")
                        for c in range(FF // P):
                            mm = pe.matmul(t[:, 0:D], glu[:, c, :], w2[:, c, :], start=(c == 0), stop=(c == FF // P - 1))
                        mm.then_inc(proj_full, 1)
                    if k == 4 and "C" in S:
                        pe.wait_ge(z_ready["C"], i - 2 + 1)
                        turn(i, "zT", zC)
                    if k in (4, 5) and "A" in S:
                        if k == 4:
                            if is_iteration(i, 0):
                                pe.wait_ge(ld_att2, 64)
                            pe.wait_ge(ctxcur_ready, i + 1)
                        qk_proj(i, f"k2_{k - 4}", wk[1], ctxcur[:, :], k - 4, C)
                    if k == 6 and "B" in S:
                        pe.wait_ge(norm_done, at(i, lambda t: units_before(t) + 4))
                        o_turn(i, "o2T_0", o_nat["B"], 0)
                        o_turn(i, "o2T_1", o_nat["B"], 1)
                    if k == 6 and "C" in S:
                        t = use(i, "logit")
                        emptied_by(i, "zT")
                        pe.matmul(t[:, 0:7], zT[:, :], wr[:, 0:7], start=True, stop=True).then_inc(proj_full, 1)
                    if k == 7 and "A" in S:
                        v_proj(i, "v2_0", wv[1], ctxcur[:, :], 0, C)
                        v_proj(i, "v2_1", wv[1], ctxcur[:, :], 1, C)
                    if k == 7 and "B" in S:
                        emptied_by(i, "o2T_1")
                        o_proj(i, "wo2", "B", wo[1])
                if "N" in S:
                    pe.wait_ge(hcur_ready, i + 2)
                    qk_proj(i, "q1_0", wq[0], hcur1[:, :], 0, P)
                    qk_proj(i, "q1_1", wq[0], hcur1[:, :], 1, P)
                if "A" in S:
                    pe.wait_ge(norm_done, at(i, lambda t: units_before(t + 1)))
                    o_turn(i, "o1T_0", o_nat["A"], 0)
                    o_turn(i, "o1T_1", o_nat["A"], 1)
                if "B" in S:
                    pe.wait_ge(z_ready["B"], i)
                    turn(i, "h3T", zB)
                if "N" in S:
                    qk_proj(i, "k1_0", wk[0], hcur1[:, :], 0, P)
                if "A" in S:
                    emptied_by(i, "o1T_1")
                    o_proj(i, "wo1", "A", wo[0])
                if "N" in S:
                    qk_proj(i, "k1_1", wk[0], hcur1[:, :], 1, P)
                    v_proj(i, "v1_0", wv[0], hcur1[:, :], 0, P)
                    v_proj(i, "v1_1", wv[0], hcur1[:, :], 1, P)
                if "A" in S:
                    pe.wait_ge(z_ready["A"], i + 1)
                    turn(i, "h2T", zA)


            def rank_sums(x, n_exp):
                pe.wait_ge(hot_ready[x], 1)
                pe.wait_ge(ld_moe, 48)
                src = hot[:, 0:n_exp, :].rearrange("p e t -> p (e t)")
                w = n_exp * B
                t = bank[RANK_BANK[x]]
                pe.matmul(t[:, 0:w], tri[:, :], src, start=True, stop=True)
                mm = pe.matmul(t[:, P:P + w], ones[:, :], src, start=True, stop=True)
                mm.then_inc(rank_done[x], 1)

            pe.wait_ge(ld_att1, 64)
            for i in (-1, 0, 1):
                iteration(i, streams(i))
            with pe.Fori(FIRST_LOOPED, B - 1) as i:
                iteration(i, set("ABCN"))
            for i in (B - 1, B, B + 1):
                iteration(i, streams(i))

            first_phase_over(pe)
            pe.wait_ge(ld_slot, 48)
            uses = [0]

            def slot_bank():
                from_one(pe, pre_slot_done, uses[0] - 6)
                uses[0] += 1
                return bank[(uses[0] - 1) % 7]

            def flat(t, g):
                return t[:, 4 * g:4 * g + 4, :].rearrange("p b c -> p (b c)")

            for g in range(G):
                t = slot_bank()
                pe.wait_ge(ctx_step, 3)
                for n in range(4):
                    mm = pe.transpose(t[:, n * C:(n + 1) * C], ctx_n[:, 4 * g + n, :], eye[0:C, 0:C])
                mm.then_inc(pre_slot_full, 1)
            for stage, (w, src, rowsn) in enumerate(((wks, xinT, P), (wvs, xinT, P), (wqTs, kkT, P), (bq, kkT, 1))):
                for g in range(G):
                    t = slot_bank()
                    pe.wait_ge(pre_slot_done, (g + 1) if src is xinT else G + g + 1)
                    pe.matmul(t[0:rowsn, 0:4 * C], w, flat(src, g), start=True, stop=True).then_inc(pre_slot_full, 1)
                if stage == 0:
                    rank_sums("a", EA)
            for g in range(G):
                t = slot_bank()
                pe.wait_ge(pre_slot_done, 2 * G + g + 1)
                for n in range(4):
                    mm = pe.matmul(t[0:C, n * D:(n + 1) * D], vT[:, 4 * g + n, :], wus, start=True, stop=True)
                mm.then_inc(pre_slot_full, 1)

            pe.wait_ge(ld_moe, 48)
            pe.wait_ge(pre_slot_done, 6 * G)

            def sh_turn(g):
                from_one(pe, sh_T_ready, g)
                for n in range(4):
                    mm = pe.transpose(quads(bank[0])[:, n, :], z_all[:, 4 * g + n, :], eye[:, :])
                mm.then_inc(sh_T_done, 1)

            def sh_down(g):
                pe.wait_ge(sh_h_ready, CA * (g + 1))
                from_one(pe, sh_added, g)
                for n in range(4):
                    for c in range(CA):
                        w = min(P, IA - c * P)
                        mm = pe.matmul(quads(bank[7])[:, n, :], sh_h[g % 2][0:w, c, n * P:(n + 1) * P], down[0:w, EA, c, :],
                                       start=(c == 0), stop=(c == CA - 1))
                mm.then_inc(sh_y_done, 1)

            sh_turn(0)
            for g in range(G):
                pe.wait_ge(sh_T_ready, g + 1)
                for c in range(CA):
                    w = min(P, IA - c * P)
                    from_one(pe, sh_act_done, CA * (g - 1) + c + 1)
                    from_one(pe, sh_h_ready, CA * (g - 1) + c + 1)
                    for j in range(2):
                        mm = pe.matmul(bank[1 + CA * j + c][0:w, :], gate_up[:, EA, j * IA + c * P:j * IA + c * P + w],
                                       flat(zsT, g), start=True, stop=True)
                    mm.then_inc(sh_up_done, 1)
                    if c == 0 and g >= 1:
                        sh_down(g - 1)
                    if c == 1 and g + 1 < G:
                        sh_turn(g + 1)
            sh_down(G - 1)
            pe.wait_ge(sh_added, G)

            def turn_rows(x, q, u):
                m, r = NSLOT * q + u + 2, (u + 2) % NSLOT
                if exists(m, NBLK[x]):
                    pe.wait_ge(blk_in[x][r], 16 * (q + 1 + (u + 2) // NSLOT))
                    from_one(pe, xT_ready[x], m)
                    pe.transpose(bank[0][:, 0:P], blk_x[:, r, 0:D], eye[:, :]).then_inc(xT_done[x], 1)

            def expert_of(table, m, n_exp):
                return pe.value_load(table[0:1, bass.ds(m, 1)], min_val=0, max_val=n_exp - 1)

            def step_a(q, u):
                n, v, here = NSLOT * q + u, 1 - u % 2, u % 2
                turn_rows("a", q, u)
                m = n + 1
                if exists(m, NR):
                    e = expert_of(expert_a, m, EA)
                    pe.wait_ge(xT_ready["a"], m + 1)
                    from_one(pe, h_ready["a"], m - 1)
                    for j in range(2):
                        mm = pe.matmul(bank[1 + 2 * j + v][:, 0:IA], blk_xT[:, v, :],
                                       gate_up[:, bass.ds(e, 1), j * IA:(j + 1) * IA].rearrange("p a n -> p (a n)"),
                                       start=True, stop=True)
                    mm.then_inc(up_done["a"], 1)
                if exists(n, NR):
                    pe.wait_ge(h_ready["a"], n + 1)
                    from_one(pe, hT_ready["a"], n)
                    for c in range(CA):
                        w = min(P, IA - c * P)
                        mm = pe.transpose(bank[5][0:w, c * P:(c + 1) * P], blk_h[:, here, c * P:c * P + w], eye[:, :])
                    mm.then_inc(hT_done["a"], 1)
                m = n - 1
                if exists(m, NR):
                    e = expert_of(expert_a, m, EA)
                    pe.wait_ge(hT_ready["a"], m + 1)
                    from_one(pe, y_ready["a"], m - 1)
                    for c in range(CA):
                        w = min(P, IA - c * P)
                        mm = pe.matmul(bank[6 + v][:, 0:D], blk_hT[0:w, v, c, :],
                                       down[0:w, bass.ds(e, 1), c, :].rearrange("p a n -> p (a n)"),
                                       start=(c == 0), stop=(c == CA - 1))
                    mm.then_inc(y_done["a"], 1)

            skewed(pe, NR, step_a)

            def turn_group(g, ready, count, done, src=zs):
                pe.wait_ge(ready, count)
                for n in range(4):
                    mm = pe.transpose(quads(bank[2 * g])[:, n, :], src[:, 4 * g + n, 0:D], eye[:, :])
                mm.then_inc(done, 1)

            pe.wait_ge(y_ready["a"], NR)
            with pe.Fori(0, SLOT_ITERS) as it:
                for g in range(G):
                    turn_group(g, zq_ready, it * G + g + 1, zqT_done)
                for g in range(G):
                    pe.wait_ge(zqT_ready, it * G + g + 1)
                    for n in range(4):
                        b = 4 * g + n
                        pe.matmul(quads(bank[2 * g + 1])[0:C, n, :], kqb[0:1, b, :], ones[0:1, :], start=True, stop=False)
                        mm = pe.matmul(quads(bank[2 * g + 1])[0:C, n, :], kq[:, b, :], zsT[:, b, :], start=False, stop=True)
                    mm.then_inc(lg_done, 1)
                for g in range(G):
                    pe.wait_ge(att_ready, it * G + g + 1)
                    for n in range(4):
                        b = 4 * g + n
                        mm = pe.matmul(bank[2 * g + n // 2][:, (n % 2) * (D + 1):(n % 2 + 1) * (D + 1)],
                                       att[:, b, :], vu[:, b, :], start=True, stop=True)
                    mm.then_inc(upd_done, 1)
                for g in range(G):
                    turn_group(g, zm_ready, it * G + g + 1, zmT_done)
                for g in range(G):
                    pe.wait_ge(zmT_ready, it * G + g + 1)
                    pe.matmul(bank[2 * g + 1][:, :], w1s, flat(zsT, g), start=True, stop=True).then_inc(hid_done, 1)
                for g in range(G):
                    pe.wait_ge(hid_ready, it * G + g + 1)
                    for n in range(4):
                        mm = pe.matmul(quads(bank[2 * g])[:, n, :], hid[:, 4 * g + n, :], w2s, start=True, stop=True)
                    mm.then_inc(mlp_done, 1)

            for g in range(G):
                turn_group(g, z3_ready, g + 1, z3T_done, sent[0])
            for g in range(G):
                pe.wait_ge(z3T_ready, g + 1)
                for n in range(4):
                    b = 4 * g + n
                    mm = pe.matmul(bank[1][:, b * EB:(b + 1) * EB], zsT[:, b, :], wgate[:, :], start=True, stop=True)
            mm.then_inc(lgb_done, 1)
            rank_sums("b", EB)
            pe.wait_ge(ld_moe_b, 48)

            def step_b(q, u):
                n, v, here = NSLOT * q + u, 1 - u % 2, u % 2
                turn_rows("b", q, u)
                m = n + 1
                if exists(m, NB):
                    e = expert_of(expert_b, m, EB)
                    pe.wait_ge(xT_ready["b"], m + 1)
                    from_one(pe, h_ready["b"], m - 1)
                    pe.matmul(bank[1 + v][:, :], blk_xT[:, v, :], w1b[:, bass.ds(e, 1), :].rearrange("p a n -> p (a n)"),
                              start=True, stop=True).then_inc(up_done["b"], 1)
                if exists(n, NB):
                    pe.wait_ge(h_ready["b"], n + 1)
                    from_one(pe, hT_ready["b"], n - 1)
                    for c in range(FB // P):
                        mm = pe.transpose(bank[3 + here][:, c * P:(c + 1) * P], blk_h[:, here, c * P:(c + 1) * P], eye[:, :])
                    mm.then_inc(hT_done["b"], 1)
                m = n - 1
                if exists(m, NB):
                    e = expert_of(expert_b, m, EB)
                    pe.wait_ge(hT_ready["b"], m + 1)
                    from_one(pe, y_ready["b"], m - 1)
                    for c in range(FB // P):
                        mm = pe.matmul(bank[5 + v][:, 0:D], blk_hT[:, v, c, :],
                                       w2b[:, bass.ds(e, 1), c, :].rearrange("p a n -> p (a n)"),
                                       start=(c == 0), stop=(c == FB // P - 1))
                    mm.then_inc(y_done["b"], 1)

            skewed(pe, NB, step_b)

        @block.scalar
        def _(act):
            act.wait_ge(pre_dve, 2)
            for g in range(8):
                act.wait_ge(pre_T, g + 1)
                for n in range(4):
                    b = 4 * (g % 4) + n
                    if g < 4:
                        ins = act.activation(h1T[:, b, :], trans[g % 2][:, n, :], ACT.Identity,
                                             bias=ada[:, 0, 1, b:b + 1], scale=ada[:, 0, 0, b:b + 1])
                    elif n == 0:
                        ins = act.activation(ctxT[:, 4 * (g - 4) * C:4 * (g - 3) * C].rearrange("p (n c) -> p n c", n=4),
                                             trans[g % 2][:, :, 0:C], ACT.Copy)
                ins.then_inc(pre_act, 1)

            def empty(i, name, dst, src=None, **kw):
                bank = PLAN[FIRST_LOOPED if not isinstance(i, int) else i, name][0]
                act.wait_ge(proj_full, at(i, lambda j: PLAN[j, name][1]))
                act.activation(dst, src(proj[bank]), kw.pop("f", ACT.Copy), **kw).then_inc(emptied["act"], 1)

            def chunks(t, n):
                return t[:, 0:4 * n].rearrange("p (c n) -> p c n", c=4)

            def heads(t, n):
                return t[0:n, :].rearrange("p (h d) -> p h d", d=DH)

            def modulated(i, name, dst, norm, b):
                empty(i, name, dst[:, :], lambda t: t[:, 0:P], f=ACT.Identity,
                      bias=ada[:, norm, 1, bass.ds(b, 1)], scale=ada[:, norm, 0, bass.ds(b, 1)])

            def iteration(i, S):
                units = [("B", j) for j in range(4) if "B" in S] + [("A", j) for j in range(4) if "A" in S]
                if "B" in S:
                    empty(i, "q2_0", q2T[:, 0:4, :], lambda t: chunks(t, P))
                    empty(i, "q2_1", q2T[:, 4:8, :], lambda t: chunks(t, P))
                if "C" in S:
                    act.wait_ge(emptied["dve"], at(i, lambda j: PLAN[j, "gate"][2]))
                    act.activation(gact[:, :, :], gpre[:, :, :], ACT.Gelu).then_inc(gelu_done, 1)
                for k in range(10):
                    if 0 <= k - 1 < len(units):
                        n = P if units[k - 1][0] == "A" else C
                        act.wait_ge(T_done, at(i, lambda t: units_before(t) + k))
                        act.activation(probT[0:n, (k - 1) % 2, :, :], trans[(k - 1) % 2][0:n, :, :],
                                       ACT.Copy).then_inc(probT_ready, 1)
                    if k < len(units):
                        n = P if units[k][0] == "A" else C
                        act.wait_ge(sub_done, at(i, lambda t: units_before(t) + k + 1))
                        act.activation(expd[:, k % 2, :, 0:n], shifted[:, k % 2, :, 0:n], ACT.Exp,
                                       scale=DH ** -0.5).then_inc(exp_done, 1)
                    if k == 4 and "C" in S:
                        empty(i, "zT", zT[:, :], lambda t: t[:, 0:P])
                    if k in (4, 5) and "A" in S:
                        empty(i, f"k2_{k - 4}", k2T[:, 4 * (k - 4):4 * (k - 3), :], lambda t: chunks(t, C))
                    if k == 6 and "B" in S:
                        for half in range(2):
                            empty(i, f"o2T_{half}", oT["B"][:, 4 * half:4 * half + 4, :], lambda t: chunks(t, P))
                    if k == 7 and "A" in S:
                        for half in range(2):
                            empty(i, f"v2_{half}", v2[:, 8 * half:8 * half + 8, 0:DH], lambda t: heads(t, C))
                if "N" in S:
                    empty(i, "q1_0", q1T[:, 0:4, :], lambda t: chunks(t, P))
                    empty(i, "q1_1", q1T[:, 4:8, :], lambda t: chunks(t, P))
                if "A" in S:
                    for half in range(2):
                        empty(i, f"o1T_{half}", oT["A"][:, 4 * half:4 * half + 4, :], lambda t: chunks(t, P))
                if "B" in S:
                    modulated(i, "h3T", h3T, 2, i - 1)
                if "N" in S:
                    empty(i, "k1_0", k1T[:, 0:4, :], lambda t: chunks(t, P))
                    empty(i, "k1_1", k1T[:, 4:8, :], lambda t: chunks(t, P))
                    for half in range(2):
                        empty(i, f"v1_{half}", v1[:, 8 * half:8 * half + 8, 0:DH], lambda t: heads(t, P))
                if "A" in S:
                    modulated(i, "h2T", h2T, 1, i)

            for i in (-1, 0, 1):
                iteration(i, streams(i))
            with act.Fori(FIRST_LOOPED, B - 1) as i:
                iteration(i, set("ABCN"))
            for i in (B - 1, B, B + 1):
                iteration(i, streams(i))

            first_phase_over(act)
            seen = [0]

            def from_slot_bank(dst, view, f=ACT.Copy, **kw):
                t = bank[seen[0] % 7]
                seen[0] += 1
                act.wait_ge(pre_slot_full, seen[0])
                act.activation(dst, view(t), f, **kw).then_inc(pre_slot_done, 1)

            def group_of(t, g):
                return t[:, 4 * g:4 * g + 4, :].rearrange("p b c -> p (b c)")

            wide = lambda t: t[:, 0:4 * C]
            for g in range(G):
                from_slot_bank(group_of(xinT, g), wide, ACT.Identity, scale=lnkv_g, bias=lnkv_b)
            for g in range(G):
                from_slot_bank(group_of(kkT, g), wide, ACT.Identity, bias=bk)
            act.wait_ge(exp_in["a"], 1)
            act.activation(wgt2[:, :], top2[:, :], ACT.Exp).then_inc(exp_out["a"], 1)
            for g in range(G):
                from_slot_bank(group_of(vT, g), wide, ACT.Identity, bias=bv)
            for g in range(G):
                from_slot_bank(group_of(kq, g), wide, scale=D ** 0.5)
            for g in range(G):
                from_slot_bank(group_of(kqb, g), lambda t: t[0:1, 0:4 * C], scale=D ** 0.5)
            for g in range(G):
                from_slot_bank(vu[:, 4 * g:4 * g + 4, 0:D], lambda t: quads(t)[0:C, :, :])

            def sh_turned(g):
                act.wait_ge(sh_T_done, g + 1)
                act.activation(group_of(zsT, g), bank[0][:, :], ACT.Copy).then_inc(sh_T_ready, 1)

            sh_turned(0)
            for g in range(G):
                for c in range(CA):
                    w = min(P, IA - c * P)
                    act.wait_ge(sh_up_done, CA * g + c + 1)
                    from_one(act, sh_h_ready, CA * (g - 1) + c + 1)
                    act.activation(sh_act[0:w, c, :], bank[1 + c][0:w, :], ACT.Silu).then_inc(sh_act_done, 1)
                    if c == 1 and g + 1 < G:
                        sh_turned(g + 1)

            def turned_rows(x, q, u, nblk):
                m = NSLOT * q + u + 2
                if exists(m, nblk):
                    act.wait_ge(xT_done[x], m + 1)
                    act.activation(blk_xT[:, u % 2, :], bank[0][:, 0:P], ACT.Copy).then_inc(xT_ready[x], 1)

            def step_a(q, u):
                n, v, here = NSLOT * q + u, 1 - u % 2, u % 2
                turned_rows("a", q, u, NR)
                if exists(n + 1, NR):
                    act.wait_ge(up_done["a"], n + 2)
                    act.activation(blk_act[:, v, 0:IA], bank[1 + v][:, 0:IA], ACT.Silu).then_inc(act_done["a"], 1)
                if exists(n, NR):
                    act.wait_ge(hT_done["a"], n + 1)
                    full = IA // P
                    act.activation(blk_hT[:, here, 0:full, :],
                                   bank[5][:, 0:full * P].rearrange("p (c n) -> p c n", n=P), ACT.Copy)
                    act.activation(blk_hT[0:IA - full * P, here, full, :], bank[5][0:IA - full * P, full * P:(full + 1) * P],
                                   ACT.Copy).then_inc(hT_ready["a"], 1)

            skewed(act, NR, step_a)

            act.wait_ge(ld_slot, 48)
            act.activation(es_b[:, :], R["q_logsig"], ACT.Exp).then_inc(exp_out["a"], 1)

            def modulated_group(g, done, count, ready, scale, bias):
                act.wait_ge(done, count)
                act.activation(group_of(zsT, g), bank[2 * g][:, :], ACT.Identity, scale=scale, bias=bias).then_inc(ready, 1)

            with act.Fori(0, SLOT_ITERS) as it:
                for g in range(G):
                    modulated_group(g, zqT_done, it * G + g + 1, zqT_ready, lnq_g, lnq_b)
                for g in range(G):
                    act.wait_ge(nmax_ready, it * G + g + 1)
                    for n in range(4):
                        b = 4 * g + n
                        ins = act.activation(att[:, b, :], quads(bank[2 * g + 1])[0:C, n, :], ACT.Exp,
                                             bias=nmax[0:C, b:b + 1], accum_out=esum[0:C, b:b + 1])
                    ins.then_inc(att_exp, 1)
                for g in range(G):
                    modulated_group(g, zmT_done, it * G + g + 1, zmT_ready, lnm_g, lnm_b)
                for g in range(G):
                    act.wait_ge(hid_done, it * G + g + 1)
                    act.activation(group_of(hid, g), bank[2 * g + 1][:, :], ACT.Gelu, bias=sb1_).then_inc(hid_ready, 1)

            for g in range(G):
                act.wait_ge(z3T_done, g + 1)
                act.activation(group_of(zsT, g), bank[2 * g][:, :], ACT.Copy).then_inc(z3T_ready, 1)
            act.wait_ge(exp_in["b"], 1)
            act.activation(hot1[:, :, :].rearrange("p e t -> p t e"), hot2[:, :, :].rearrange("p e t -> p t e"),
                           ACT.Exp).then_inc(exp_out["b"], 1)

            def step_b(q, u):
                n, v, here = NSLOT * q + u, 1 - u % 2, u % 2
                turned_rows("b", q, u, NB)
                if exists(n, NB):
                    act.wait_ge(hT_done["b"], n + 1)
                    act.activation(blk_hT[:, here, :, :], bank[3 + here][:, :].rearrange("p (c n) -> p c n", n=P),
                                   ACT.Relu).then_inc(hT_ready["b"], 1)

            skewed(act, NB, step_b)

        @block.vector
        def _(dve):
            count, roots = [0], [0]

            def step(ins):
                count[0] += 1
                ins.then_inc(pre_dve, 1)

            def settle():
                dve.wait_ge(pre_dve, count[0])

            def rsqrt_steps(y, var, tmp, done, base):
                v, t = tmp[:, 0, :], tmp[:, 1, :]
                yi, vi = y.bitcast(I32), v.bitcast(I32)
                steps = [lambda: dve.tensor_scalar(v, var, EPS, None, ALU.add),
                         lambda: dve.tensor_scalar(yi, vi, 1, None, ALU.logical_shift_right),
                         lambda: dve.tensor_scalar(yi, yi, -1, 0x5F3759DF, ALU.mult, ALU.add)]
                for square in (1.0, 4.0, 256.0):
                    steps += [lambda: dve.tensor_tensor(t, y, y, ALU.mult),
                              lambda: dve.tensor_tensor(t, t, v, ALU.mult),
                              lambda q=square: dve.scalar_tensor_tensor(y, t, -3.0 * q, y, ALU.add, ALU.mult)]
                steps += [lambda: dve.tensor_scalar(y, y, -1.0 / 8192.0, None, ALU.mult)]
                assert len(steps) == RSQRT_STEPS
                for n, ins in enumerate(steps):
                    ins().then_inc(done, 1)
                    dve.wait_ge(done, base + n + 1)

            def norm_all(src, dst, n):
                for b in range(B):
                    ins = dve.bn_stats(st_all[0:n, b, :], src[:, b, :])
                step(ins)
                settle()
                for b in range(B):
                    ins = dve.bn_aggr(mv_all[0:n, b, :], st_all[0:n, b, :])
                step(ins)
                settle()
                settle()
                rsqrt_steps(rstd_all[0:n, :], mv_all[0:n, :, 1], rsq_all[0:n], pre_rsqrt, RSQRT_STEPS * roots[0])
                roots[0] += 1
                for b in range(B):
                    ins = dve.tensor_scalar(dst[:, b, :], src[:, b, :], mv_all[0:n, b, 0:1], rstd_all[0:n, b:b + 1],
                                            ALU.subtract, ALU.mult)
                step(ins)
                settle()

            dve.memset(v1[:, :, DH:DH + 1], 1.0)
            step(dve.memset(v2[:, :, DH:DH + 1], 1.0))
            dve.wait_ge(ld_small, 16 * N_SMALL)
            dve.wait_ge(pre_ada, 1)
            adaP = proj[0][:, 0:6 * B].rearrange("p (n j b) -> p n j b", n=3, j=2)
            for n in range(3):
                dve.tensor_scalar(ada[:, n, 0, :], adaP[:, n, 0, :], cols[:, 2 * n:2 * n + 1], 1.0, ALU.add, ALU.add)
                ins = dve.tensor_scalar(ada[:, n, 1, :], adaP[:, n, 1, :], cols[:, 2 * n + 1:2 * n + 2], None, ALU.add)
            step(ins)
            dve.wait_ge(ld_x, 64)
            norm_all(x_sb, x0b, P)
            norm_all(x0b, z_all, P)
            assert count[0] == PRE_Z1
            dve.tensor_tensor(x0b[:, :, :], x0b[:, :, :], R["bo1"].unsqueeze(1).broadcast_to([P, B, D]), ALU.add)
            step(dve.tensor_tensor(x_sb[:, :, :], x_sb[:, :, :], R["ffb2"].unsqueeze(1).broadcast_to([P, B, D]), ALU.add))

            dve.wait_ge(pre_T, 8)
            for b in range(B):
                ins = dve.bn_stats(st_all[0:C, b, :], ctx_n[:, b, :])
            ins.then_inc(ctx_step, 1)
            dve.wait_ge(ctx_step, 1)
            for b in range(B):
                ins = dve.bn_aggr(mv_all[0:C, b, :], st_all[0:C, b, :])
            ins.then_inc(ctx_step, 1)
            dve.wait_ge(ctx_step, 2)
            rsqrt_steps(rstd_all[0:C, :], mv_all[0:C, :, 1], rsq_all[0:C], ctx_rsqrt, 0)
            for b in range(B):
                ins = dve.tensor_scalar(ctx_n[:, b, :], ctx_n[:, b, :], mv_all[0:C, b, 0:1], rstd_all[0:C, b:b + 1],
                                        ALU.subtract, ALU.mult)
            ins.then_inc(ctx_step, 1)

            def bank_of(i, name):
                return proj[PLAN[FIRST_LOOPED if not isinstance(i, int) else i, name][0]]

            def filled(i, name):
                dve.wait_ge(proj_full, at(i, lambda j: PLAN[j, name][1]))

            def stand():
                dve.sem_inc(fence, 1)

            def layernorm(s, b, src, dst):
                stand()
                dve.bn_stats(st[s][:, :], src).then_inc(stats_done[s], 1)
                dve.wait_ge(stats_done[s], b + 1)
                stand()
                dve.bn_aggr(mv[s][:, :], st[s][:, :]).then_inc(mv_ready[s], 1)
                dve.wait_ge(mv_ready[s], b + 1)
                rsqrt_steps(rstd[s][:, :], mv[s][:, 1:2], rsq[s], ln_step[s], RSQRT_STEPS * b)
                if s == "C":
                    dve.wait_ge(z_kept, b + 1)
                dve.tensor_scalar(dst[:, :], src, mv[s][:, 0:1], rstd[s][:, 0:1],
                                  ALU.subtract, ALU.mult).then_inc(z_ready[s], 1)

            def residual(i, name, dst, rest):
                filled(i, name)
                dve.tensor_tensor(dst, bank_of(i, name)[:, 0:D], rest, ALU.add).then_inc(emptied["dve"], 1)
                dve.wait_ge(emptied["dve"], at(i, lambda j: PLAN[j, name][2]))

            def iteration(i, S):
                units = [("B", j) for j in range(4) if "B" in S] + [("A", j) for j in range(4) if "A" in S]
                b, c = i - 1, i - 2
                if "C" in S:
                    filled(i, "gate")
                    dve.tensor_tensor(gpre[:, :, :], bank_of(i, "gate")[:, :].rearrange("p (c n) -> p c n", c=4),
                                      cols[:, 10:14].unsqueeze(2).broadcast_to([P, 4, P]),
                                      ALU.add).then_inc(emptied["dve"], 1)
                for k in range(10):
                    if k < len(units):
                        n = P if units[k][0] == "A" else C
                        s_in = score[k % 2][:, :, 0:n]
                        dve.wait_ge(score_done, at(i, lambda t: units_before(t) + k + 1))
                        dve.tensor_reduce(smax[:, k % 2, :], s_in, X,
                                          ALU.max).then_inc(max_done, 1)
                        dve.wait_ge(max_done, at(i, lambda t: units_before(t) + k + 1))
                        dve.tensor_tensor(shifted[:, k % 2, :, 0:n], s_in,
                                          smax[:, k % 2, :].unsqueeze(2).broadcast_to([P, QH, n]),
                                          ALU.subtract).then_inc(sub_done, 1)
                    if 0 <= k - 2 < len(units):
                        u = k - 2
                        s, j = units[u]
                        dve.wait_ge(pv_done, at(i, lambda t: units_before(t) + u + 1))
                        dve.reciprocal(rden[:, u % 2, :], pvo[:, :, DH]).then_inc(rden_done, 1)
                        dve.wait_ge(rden_done, at(i, lambda t: units_before(t) + u + 1))
                        dve.tensor_tensor(o_nat[s][:, unit_heads(j), :], pvo[:, :, 0:DH],
                                          rden[:, u % 2, :].unsqueeze(2).broadcast_to([P, QH, DH]),
                                          ALU.mult).then_inc(norm_done, 1)
                    if k == 0 and "C" in S:
                        filled(i, "lin")
                        dve.wait_ge(gelu_done, c + 1)
                        for n in range(FF // P):
                            ins = dve.scalar_tensor_tensor(glu[:, n, :], bank_of(i, "lin")[:, n * P:(n + 1) * P],
                                                           cols[:, 6 + n:7 + n], gact[:, n, :], ALU.add, ALU.mult)
                        ins.then_inc(emptied["dve"], 1)
                    if k == 3 and "C" in S:
                        x1 = x_sb[:, bass.ds(c, 1), :].rearrange("p a d -> p (a d)")
                        dve.wait_ge(xbx_ready, c + 1)
                        residual(i, "ffout", x1, xbx[:, :])
                        layernorm("C", c, x1, zC)
                    if k == 7 and "C" in S:
                        filled(i, "logit")
                        dve.tensor_tensor(logits[:, bass.ds(c, 1), 0:7].rearrange("p a e -> p (a e)"),
                                          bank_of(i, "logit")[:, 0:7], R["rb"], ALU.add).then_inc(emptied["dve"], 1)
                    if k == 8 and "B" in S:
                        dve.wait_ge(xab_ready, b + 1)
                        residual(i, "wo2", xb[:, :], xab[:, :])
                        layernorm("B", b, xb[:, :], zB)
                if "A" in S:
                    residual(i, "wo1", xa[:, :], x0b[:, bass.ds(i, 1), :].rearrange("p a d -> p (a d)"))
                    layernorm("A", i, xa[:, :], zA)

            for i in (-1, 0, 1):
                iteration(i, streams(i))
            with dve.Fori(FIRST_LOOPED, B - 1) as i:
                iteration(i, set("ABCN"))
            for i in (B - 1, B, B + 1):
                iteration(i, streams(i))

            def routing(x, n_exp, picks, table, first_block, n_blk):
                done, at_step = rt_step[x], [0]

                def link(ins):
                    at_step[0] += 1
                    ins.then_inc(done, 1)
                    dve.wait_ge(done, at_step[0])

                lg = logits[:, :, 0:n_exp]
                by_e = lambda t: t[:, 0:n_exp, :]
                by_t = lambda t: by_e(t).rearrange("p e t -> p t e")
                flat = lambda t: by_e(t).rearrange("p e t -> p (e t)")
                per_t = lambda t: t.unsqueeze(2).broadcast_to([P, B, n_exp])
                per_e = lambda t: t.unsqueeze(1).broadcast_to([P, B, n_exp])
                iota, iota100 = (per_e(R[n][:, 0:n_exp]) for n in ("iota", "iota100"))

                def first_best(vals, best, one_hot):
                    link(dve.tensor_reduce(best[:, :], vals, X, ALU.max))
                    link(dve.tensor_tensor(by_t(rt), vals, per_t(best[:, :]), ALU.is_equal))
                    link(dve.scalar_tensor_tensor(by_t(rt), by_t(rt), -100.0, iota100, ALU.mult, ALU.add))
                    link(dve.tensor_reduce(idx[:, :], by_t(rt), X, ALU.min))
                    link(dve.tensor_tensor(by_t(one_hot), iota, per_t(idx[:, :]), ALU.is_equal))

                if picks == 2:
                    first_best(lg, top1, hot1)
                    link(dve.scalar_tensor_tensor(by_t(slot), by_t(hot1), -3e38, lg, ALU.mult, ALU.add))
                    first_best(by_t(slot), top2, hot2)
                    link(dve.tensor_tensor(flat(hot), flat(hot1), flat(hot2), ALU.add))
                    dve.sem_inc(hot_ready[x], 1)
                    link(dve.tensor_tensor(top2[:, :], top2[:, :], top1[:, :], ALU.subtract))
                    dve.sem_inc(exp_in[x], 1)
                else:
                    first_best(lg, top1, hot)
                    dve.sem_inc(hot_ready[x], 1)
                    link(dve.tensor_tensor(by_t(hot2), lg, per_t(top1[:, :]), ALU.subtract))
                    dve.sem_inc(exp_in[x], 1)
                dve.wait_ge(rank_done[x], 1)
                t = bank[RANK_BANK[x]]
                w = n_exp * B
                link(dve.tensor_copy(flat(rt), t[:, P:P + w]))
                link(dve.tensor_tensor_scan(flat(run), flat(rt), zeros[:, 0:w], 0.0, ALU.add, ALU.add))
                link(dve.tensor_reduce(cnt[:, 0:n_exp], by_e(rt), X, ALU.add))
                link(dve.tensor_tensor(by_e(slot), cnt[:, 0:n_exp].unsqueeze(2).broadcast_to([P, n_exp, B]),
                                       R["edges"].unsqueeze(1).broadcast_to([P, n_exp, B]), ALU.is_gt))
                link(dve.tensor_reduce(nblk[:, 0:n_exp], by_e(slot), X, ALU.add))
                link(dve.tensor_tensor_scan(cblk[:, 0:n_exp], nblk[:, 0:n_exp], zeros[:, 0:n_exp], 0.0, ALU.add, ALU.add))
                link(dve.tensor_tensor(base[:, 0:n_exp], cblk[:, 0:n_exp], nblk[:, 0:n_exp], ALU.subtract))
                link(dve.scalar_tensor_tensor(base[:, 0:n_exp], base[:, 0:n_exp], float(P), cnt[:, 0:n_exp], ALU.mult, ALU.add))
                link(dve.tensor_tensor(base[:, 0:n_exp], base[:, 0:n_exp], run[:, 0:n_exp, B - 1], ALU.subtract))
                link(dve.tensor_tensor(flat(slot), flat(run), flat(rt), ALU.subtract))
                link(dve.tensor_tensor(flat(slot), flat(slot), t[:, 0:w], ALU.add))
                link(dve.tensor_tensor(by_e(slot), by_e(slot), base[:, 0:n_exp].unsqueeze(2).broadcast_to([P, n_exp, B]), ALU.add))
                for one_hot, f, i in (((hot1, slot1f, slot1), (hot2, slot2f, slot2)) if picks == 2 else ((hot, slot1f, slot1),)):
                    link(dve.tensor_tensor(flat(rt), flat(one_hot), flat(slot), ALU.mult))
                    link(dve.tensor_reduce(f[:, :], by_t(rt), X, ALU.add))
                    link(dve.tensor_copy(i[:, :], f[:, :]))
                nb = n_blk - first_block
                link(dve.tensor_tensor(bge[0:1, 0:nb, 0:n_exp], R["blocks"][0:1, 0:nb].unsqueeze(2).broadcast_to([1, nb, n_exp]),
                                       cblk[0:1, 0:n_exp].unsqueeze(1).broadcast_to([1, nb, n_exp]), ALU.is_ge))
                link(dve.tensor_reduce(bex[0:1, 0:nb], bge[0:1, 0:nb, 0:n_exp], X, ALU.add))
                link(dve.tensor_scalar(table[0:1, first_block:n_blk], bex[0:1, 0:nb], float(n_exp - 1), None, ALU.min))
                if picks == 2:
                    dve.wait_ge(exp_out[x], 1)
                    link(dve.tensor_scalar(top1[:, :], wgt2[:, :], 1.0, None, ALU.add))
                    link(dve.reciprocal(wgt1[:, :], top1[:, :]))
                    link(dve.tensor_copy(sent[0][:, :, D + 1], wgt1[:, :]))
                    link(dve.tensor_tensor(sent[1][:, :, D + 1], wgt2[:, :], wgt1[:, :], ALU.mult))
                    dve.sem_inc(routed[x], 1)
                else:
                    dve.sem_inc(routed[x], 1)
                    dve.wait_ge(exp_out[x], 1)
                    link(dve.tensor_reduce(top1[:, :], by_t(hot1), X, ALU.add))
                    link(dve.reciprocal(wgt1[:, :], top1[:, :]))

            first_phase_over(dve)
            dve.memset(vu[:, :, D:D + 1], 1.0)
            routing("a", EA, 2, expert_a, 0, NR)

            def group(t, g):
                return t[:, 4 * g:4 * g + 4, :]

            def add_shared(g):
                dve.wait_ge(sh_y_done, g + 1)
                dve.tensor_tensor(group(x_sb, g), group(x_sb, g), quads(bank[7])[:, :, :], ALU.add).then_inc(sh_added, 1)

            for g in range(G):
                from_one(dve, sh_y_done, g - 1)
                for c in range(CA):
                    w = min(P, IA - c * P)
                    dve.wait_ge(sh_act_done, CA * g + c + 1)
                    dve.tensor_tensor(sh_h[g % 2][0:w, c, :], bank[1 + CA + c][0:w, :], sh_act[0:w, c, :],
                                      ALU.mult).then_inc(sh_h_ready, 1)
                    if c == 0 and g >= 1:
                        add_shared(g - 1)
            add_shared(G - 1)

            def step_a(q, u):
                n, v, here = NSLOT * q + u, 1 - u % 2, u % 2
                if exists(n + 1, NR):
                    dve.wait_ge(act_done["a"], n + 2)
                    dve.tensor_tensor(blk_h[:, v, 0:IA], bank[3 + v][:, 0:IA], blk_act[:, v, 0:IA],
                                      ALU.mult).then_inc(h_ready["a"], 1)
                if exists(n - 1, NR):
                    dve.wait_ge(meta_kept["a"], n)
                    leave("a", q, u, bank[6 + v], meta[:, bass.ds(n - 1, 1), 1:2].rearrange("p a n -> p (a n)"), ALU.mult)

            def leave(x, q, u, t, other, op):
                m, r = NSLOT * q + u - 1, (u - 1) % NSLOT
                dve.wait_ge(y_done[x], m + 1)
                from_one(dve, returned[x][r], 16 * (q - (u == 0)))
                if op == ALU.mult:
                    dve.tensor_scalar(blk_y[:, r, :], t[:, 0:D], other, None, op).then_inc(y_ready[x], 1)
                else:
                    dve.tensor_tensor(blk_y[:, r, :], t[:, 0:D], other, op).then_inc(y_ready[x], 1)

            skewed(dve, NR, step_a)

            for g in range(G):
                dve.wait_ge(picked_a[g], 16)
                for k in range(2):
                    dve.tensor_tensor(group(x_sb, g), group(x_sb, g), picked[:, 4 * g:4 * g + 4, k, :],
                                      ALU.add).then_inc(mean_ready, 1)
                    dve.wait_ge(mean_ready, 2 * g + k + 1)
                dve.sem_inc(x2_ready, 1)

            def norm_groups(src, link, done, base, ready, count, dst=zs):
                stand()
                for b in range(B):
                    ins = dve.bn_stats(st_all[:, b, :], src[:, b, :])
                link(ins)
                stand()
                for b in range(B):
                    ins = dve.bn_aggr(mv_all[:, b, :], st_all[:, b, :])
                link(ins)
                rsqrt_steps(rstd_all[:, :], mv_all[:, :, 1], rsq_all, done, base)
                for g in range(G):
                    for b in range(4 * g, 4 * g + 4):
                        ins = dve.tensor_scalar(dst[:, b, 0:D], src[:, b, :], mv_all[:, b, 0:1], rstd_all[:, b:b + 1],
                                                ALU.subtract, ALU.mult)
                    ins.then_inc(ready, 1)
                dve.wait_ge(ready, count)

            def chain(sem_, start):
                at_step = [0]

                def link(ins):
                    at_step[0] += 1
                    ins.then_inc(sem_, 1)
                    dve.wait_ge(sem_, start + at_step[0])
                return link, at_step

            link, _ = chain(sl_step, 0)
            norm_groups(x_sb, link, sl_rsqrt, 0, zp_ready, G)
            dve.wait_ge(exp_out["a"], 2)
            for g in range(G):
                ins = dve.tensor_tensor(group(S, g), group(zs, g), es_b[:, :].unsqueeze(1).broadcast_to([P, 4, D]), ALU.mult)
            link(ins)
            for g in range(G):
                ins = dve.tensor_tensor(group(S, g), group(S, g), R["q_mu"].unsqueeze(1).broadcast_to([P, 4, D]), ALU.add)
                ins.then_inc(S_ready, 1)
            dve.wait_ge(S_ready, G)
            SETUP, STEPS = 3, 6 + 2 * G

            with dve.Fori(0, SLOT_ITERS) as it:
                link, n_steps = chain(sl_step, it * STEPS + SETUP)
                per_round = 3 * RSQRT_STEPS
                at_rsqrt = it * per_round + RSQRT_STEPS
                norm_groups(S, link, sl_rsqrt, at_rsqrt, zq_ready, it * G + G)
                for g in range(G):
                    dve.wait_ge(lg_done, it * G + g + 1)
                    dve.tensor_reduce(nmax[0:C, 4 * g:4 * g + 4], quads(bank[2 * g + 1])[0:C, :, :], X, ALU.max,
                                      negate=True).then_inc(nmax_ready, 1)
                for g in range(G):
                    dve.wait_ge(att_exp, it * G + g + 1)
                    link(dve.reciprocal(rsum[0:C, 4 * g:4 * g + 4], esum[0:C, 4 * g:4 * g + 4]))
                    for b in range(4 * g, 4 * g + 4):
                        ins = dve.tensor_scalar(att[:, b, :], att[:, b, :], rsum[0:C, b:b + 1], 1e-8, ALU.mult, ALU.add)
                    ins.then_inc(att_ready, 1)
                for g in range(G):
                    dve.wait_ge(upd_done, it * G + g + 1)
                    for j in range(2):
                        ins = dve.reciprocal(rcol[:, 4 * g + 2 * j:4 * g + 2 * j + 2],
                                             bank[2 * g + j][:, D:2 * (D + 1):D + 1])
                    link(ins)
                    dve.wait_ge(S_rest, it * G + g + 1)
                    for n in range(4):
                        b = 4 * g + n
                        ins = dve.scalar_tensor_tensor(S[:, b, :], bank[2 * g + n // 2][:, (n % 2) * (D + 1):(n % 2) * (D + 1) + D],
                                                       rcol[:, b:b + 1], s_rest[:, b, :], ALU.mult, ALU.add)
                    ins.then_inc(mid_ready, 1)
                dve.wait_ge(mid_ready, it * G + G)
                norm_groups(S, link, sl_rsqrt, at_rsqrt + RSQRT_STEPS, zm_ready, it * G + G)
                for g in range(G):
                    dve.wait_ge(mlp_done, it * G + g + 1)
                    dve.wait_ge(mid_rest, it * G + g + 1)
                    dve.tensor_tensor(group(S, g), quads(bank[2 * g])[:, :, :], group(s_rest, g), ALU.add).then_inc(sum_ready, 1)
                dve.wait_ge(sum_ready, it * G + G)
                norm_groups(S, link, sl_rsqrt, at_rsqrt + 2 * RSQRT_STEPS, zp_ready, it * G + 2 * G)
                for g in range(G):
                    dve.tensor_tensor(group(S, g), group(zs, g), R["lnp_g"].unsqueeze(1).broadcast_to([P, 4, D]),
                                      ALU.mult).then_inc(sum_ready2, 1)
                    dve.wait_ge(sum_ready2, it * G + g + 1)
                    dve.tensor_tensor(group(S, g), group(S, g), R["lnp_b"].unsqueeze(1).broadcast_to([P, 4, D]),
                                      ALU.add).then_inc(S_ready, 1)
                dve.wait_ge(S_ready, it * G + 2 * G)
                assert n_steps[0] == STEPS, n_steps

            for g in range(G):
                dve.tensor_tensor(group(x_sb, g), group(x_sb, g), group(S, g), ALU.add).then_inc(x3_ready, 1)
            dve.wait_ge(x3_ready, G)

            link, _ = chain(fin_step, 0)
            norm_groups(x_sb, link, fin_rsqrt, 0, z3_ready, G, sent[0])
            dve.wait_ge(lgb_done, 1)
            link(dve.tensor_tensor(logits[:, :, :], bank[1][:, 0:B * EB].rearrange("p (b e) -> p b e", b=B),
                                   R["b_gate"].unsqueeze(1).broadcast_to([P, B, EB]), ALU.add))
            routing("b", EB, 1, expert_b, 0, NB)

            def expert_of(m):
                return dve.value_load(expert_b[0:1, bass.ds(m, 1)], min_val=0, max_val=EB - 1)

            def step_b(q, u):
                n, v, here = NSLOT * q + u, 1 - u % 2, u % 2
                if exists(n + 1, NB):
                    dve.wait_ge(up_done["b"], n + 2)
                    e = expert_of(n + 1)
                    dve.tensor_tensor(blk_h[:, v, :], bank[1 + v][:, :], b1b[:, bass.ds(e, 1), :].rearrange("p a n -> p (a n)"),
                                      ALU.add).then_inc(h_ready["b"], 1)
                if exists(n - 1, NB):
                    e = expert_of(n - 1)
                    leave("b", q, u, bank[5 + v], b2b[:, bass.ds(e, 1), :].rearrange("p a n -> p (a n)"), ALU.add)

            dve.wait_ge(ld_moe_b, 48)
            skewed(dve, NB, step_b)
            for g in range(G):
                dve.wait_ge(picked_b[g], 16)
                for b in range(4 * g, 4 * g + 4):
                    ins = dve.scalar_tensor_tensor(x_sb[:, b, :], picked[:, b, 0, :], wgt1[:, b:b + 1], x_sb[:, b, :],
                                                   ALU.mult, ALU.add)
                ins.then_inc(out_ready, 1)

        @block.gpsimd
        def _(pool):
            pool.memset(ones[:, :], 1.0)
            pool.memset(zeros[:, :], 0.0).then_inc(consts_ready, 1)
            pool.sem_inc(z_kept, 1)

            def tile(t, b):
                return t[:, bass.ds(b, 1), :].rearrange("p a d -> p (a d)")

            def iteration(i, S):
                if "N" in S:
                    if is_iteration(i, -1):
                        pool.wait_ge(pre_act, 4)
                    else:
                        pool.wait_ge(proj_full, at(i, lambda j: PLAN[j - 1, "v1_1"][1]))
                    pool.tensor_copy(hcur1[:, :], tile(h1T, i + 1)).then_inc(hcur_ready, 1)
                if "A" in S:
                    if is_iteration(i, 0):
                        pool.wait_ge(pre_act, 8)
                    else:
                        pool.wait_ge(proj_full, at(i, lambda j: PLAN[j - 1, "v2_1"][1]))
                    pool.tensor_copy(ctxcur[:, :], ctxT[:, bass.ds(i * C, C)]).then_inc(ctxcur_ready, 1)
                if "C" in S:
                    pool.wait_ge(z_ready["C"], i - 1)
                    pool.tensor_copy(tile(z_all, i - 2), zC[:, :]).then_inc(z_kept, 1)
                if "B" in S:
                    pool.wait_ge(emptied["dve"], at(i, lambda j: PLAN[j, "wo2"][2]))
                    pool.tensor_tensor(xbx[:, :], xb[:, :], tile(x_sb, i - 1), ALU.add).then_inc(xbx_ready, 1)
                if "A" in S:
                    pool.wait_ge(emptied["dve"], at(i, lambda j: PLAN[j, "wo1"][2]))
                    pool.tensor_tensor(xab[:, :], xa[:, :], R["bo2"], ALU.add).then_inc(xab_ready, 1)

            for i in (-1, 0, 1):
                iteration(i, streams(i))
            with pool.Fori(FIRST_LOOPED, B - 1) as i:
                iteration(i, set("ABCN"))
            for i in (B - 1, B, B + 1):
                iteration(i, streams(i))

            def scatter(x, picks, dst):
                pool.wait_ge(zeroed, 64)
                pool.wait_ge(routed[x], 1)
                for b in range(B):
                    for k, slots in enumerate(picks):
                        pool.indirect_dma_start(dst, bass.IndirectOffsetOnAxis(ap=slots[:, b:b + 1], axis=0),
                                                sent[k][:, b, 0:ROW], None).then_inc(scattered[x], 16)

            def stand():
                pool.sem_inc(fence_pool, 1)

            def send_back(x, dst):
                def step(q, u):
                    n = NSLOT * q + u
                    m, r = n + 2, (u + 2) % NSLOT
                    if exists(m, NBLK[x]):
                        pool.wait_ge(blk_in[x][r], 16 * (q + 1 + (u + 2) // NSLOT))
                        stand()
                        pool.tensor_copy(meta[:, bass.ds(m, 1), :].rearrange("p a n -> p (a n)"),
                                         blk_x[:, r, D:ROW]).then_inc(meta_kept[x], 1)
                    m, r = n - 1, (u - 1) % NSLOT
                    if exists(m, NBLK[x]):
                        pool.wait_ge(meta_kept[x], m + 1)
                        from_one(pool, returned[x][r], 16 * (q - (u == 0)))
                        stand()
                        pool.tensor_copy(dest[:, r:r + 1], meta[:, bass.ds(m, 1), 0:1].rearrange("p a n -> p (a n)")).then_inc(
                            dest_ready[x], 1)
                        pool.wait_ge(dest_ready[x], m + 1)
                        pool.wait_ge(y_ready[x], m + 1)
                        stand()
                        pool.indirect_dma_start(dst, bass.IndirectOffsetOnAxis(ap=dest[:, r:r + 1], axis=0),
                                                blk_y[:, r, :], None).then_inc(returned[x][r], 16)

                skewed(pool, NBLK[x], step)

            first_phase_over(pool)
            pool.wait_ge(ld_slot, 48)
            for k in range(2):
                pool.tensor_copy(sent[k][:, :, 0:D], z_all[:, :, :]).then_inc(sent_ready, 1)
                pool.tensor_copy(sent[k][:, :, D], tok_ids[:, k, :]).then_inc(sent_ready, 1)
            pool.wait_ge(sent_ready, 4)
            scatter("a", (slot1, slot2), rows_a)
            send_back("a", back_a)

            def group(t, g):
                return t[:, 4 * g:4 * g + 4, :]

            pool.wait_ge(ld_cond, 16)
            for g in range(G):
                ins = pool.tensor_tensor(group(cb2, g), group(cb2, g), R["b2"].unsqueeze(1).broadcast_to([P, 4, D]), ALU.add)
            ins.then_inc(filled_rows, 1)
            pool.wait_ge(filled_rows, 1)
            with pool.Fori(0, SLOT_ITERS) as it:
                for g in range(G):
                    pool.wait_ge(S_ready, it * G + g + 1)
                    pool.tensor_tensor(group(s_rest, g), group(S, g), R["bu"].unsqueeze(1).broadcast_to([P, 4, D]),
                                       ALU.add).then_inc(S_rest, 1)
                for g in range(G):
                    pool.wait_ge(mid_ready, it * G + g + 1)
                    pool.tensor_tensor(group(s_rest, g), group(S, g), group(cb2, g), ALU.add).then_inc(mid_rest, 1)
            pool.wait_ge(scattered["a"], 16 * 2 * B)
            pool.tensor_copy(sent[0][:, :, D], tok_ids[:, 2, :]).then_inc(sent_ready, 1)
            pool.wait_ge(sent_ready, 5)
            pool.wait_ge(z3_ready, G)
            scatter("b", (slot1,), rows_b)
            send_back("b", back_b)


def layout(I):
    import numpy as np

    arr = {
        "x": I["x"], "ctx": I["ctx_1024"], "cond_t": I["cond_1024"].T,
        "norm_w": np.stack([I[f"L0_xcond_norm{n}_w"] for n in (1, 2, 3)]),
        "eye": np.eye(P, dtype=np.float32),
        "att_w": np.stack([[I[f"L0_xcond_attn{a}_w{j}"] for j in "qkv"] for a in (1, 2)]),
        "att_wo": np.stack([I[f"L0_xcond_attn{a}_wo"] for a in (1, 2)]),
        "ff_w1": I["L0_xcond_ff_w1"], "ff_w2": I["L0_xcond_ff_w2"],
        "wr_t": I["L0_ffn_wr"].T,
    }
    col_list = [I[f"L0_xcond_norm{n}_b"].reshape(2, D) for n in (1, 2, 3)]
    col_list += [I["L0_xcond_ff_b1"].reshape(2 * FF // P, P)]
    col_list += [I[f"L1_xcond_{n}"].reshape(1, D) for n in ("lnkv_g", "lnkv_b", "lnq_g", "lnq_b", "lnm_g", "lnm_b", "bk", "bq", "b1", "bv")]
    arr["cols"] = np.concatenate(col_list).T
    arr["gate_up"] = np.concatenate([np.concatenate([I["L0_ffn_rg"], I["L0_ffn_ru"]], 1),
                                     np.concatenate([I["L0_ffn_sg"], I["L0_ffn_su"]], 0)[None]]).transpose(2, 0, 1)
    downs = np.concatenate([I["L0_ffn_rd"], I["L0_ffn_sd"][None]]).transpose(0, 2, 1)
    downs = np.concatenate([downs, np.zeros((EA + 1, CA * P - IA, D), np.float32)], 1)
    arr["down"] = downs.reshape(EA + 1, CA, P, D).transpose(2, 0, 1, 3)
    arr["tri"] = np.triu(np.ones((P, P), np.float32), 1)
    arr["wgate"] = I["L1_ffn_w_gate"]
    arr["slot_w"] = np.stack([I["L1_xcond_wk"], I["L1_xcond_wv"], I["L1_xcond_wq"].T, I["L1_xcond_wu"],
                              I["L1_xcond_w1"], I["L1_xcond_w2"]])
    arr["cond"] = I["cond_1024"]
    arr["w1b"], arr["w2b"] = I["L1_ffn_W1"], I["L1_ffn_W2"]
    arr["b12"] = np.concatenate([I["L1_ffn_b1"].reshape(-1), I["L1_ffn_b2"].reshape(-1)])
    token = np.arange(B)[None, :] * P + np.arange(P)[:, None]
    arr["tok_ids"] = np.stack([2 * token, 2 * token + 1, token], 1).astype(np.float32)
    pad = np.arange(NR * P, dtype=np.float32)[:, None]
    arr["pad_a"], arr["pad_b"] = (np.concatenate([n + pad[:m * P], 0 * pad[:m * P]], 1) for n, m in ((2 * TOK, NR), (TOK, NB)))
    shape_rows = {"iota": np.arange(EB), "iota100": np.arange(EB) + 100, "edges": np.arange(B) * P, "blocks": np.arange(NR)}
    rows = [("bo1", "L0_xcond_attn1_bo"), ("bo2", "L0_xcond_attn2_bo"), ("ffb2", "L0_xcond_ff_b2"), ("rb", "L0_ffn_rb")]
    rows += [(n, "L1_xcond_" + n) for n in ("q_mu", "q_logsig", "bu", "b2", "lnp_g", "lnp_b")] + [("b_gate", "L1_ffn_b_gate")]
    arr["rows"] = np.concatenate([I[k].reshape(-1) for _, k in rows] + [v.astype(np.float32) for v in shape_rows.values()])
    names = [(n, I[k].size) for n, k in rows] + [(n, v.size) for n, v in shape_rows.items()]
    return {k: np.ascontiguousarray(v) for k, v in arr.items()}, names


def kernel(**inputs):
    import numpy as np
    import concourse.bacc as bacc
    from concourse.bass_utils import run_bass_kernel_spmd

    arrays, row_names = layout({k: np.asarray(v) for k, v in inputs.items()})
    nc = bacc.Bacc("TRN2", target_bir_lowering=False, num_devices=1)
    args = {k: nc.dram_tensor(k, a.shape, mybir.dt.from_np(a.dtype), kind="ExternalInput").ap() for k, a in arrays.items()}
    out = nc.dram_tensor("out", (B, P, D), F32, kind="ExternalOutput").ap()
    program(nc, args, row_names, out)
    r = run_bass_kernel_spmd(nc, [arrays], core_ids=[0])
    return r.results[0]["out"]
```

```python
from contextlib import ExitStack

import concourse.bass as bass
from concourse import mybir

F32 = mybir.dt.float32
I32 = mybir.dt.int32
ALU = mybir.AluOpType
ACT = mybir.ActivationFunctionType
X = mybir.AxisListType.X

P = 128
B = 16
D = 128
C = 77
H = 16
DH = 64
INNER = H * DH
NCH = INNER // P
QH = 4
FF = 512
EPS = 1e-5
TOK = B * P
EA, IA = 7, 352
CA = -(-IA // P)
EB, FB = 8, 512
NR = (2 * TOK + EA * (P - 1)) // P
NB = (TOK + EB * (P - 1)) // P
SLOT_ITERS = 3
ROW = D + 2
NSLOT = 4

N_STEPS = 10
FILL = [
    (("h2T",), ()),
    ((), ("wo2",)),
    (("k2_0", "k2_1"), ()),
    (("q2_0", "q2_1"), ("v2_0",)),
    (("q1_0", "v2_1", "h3T"), ()),
    ((), ("gate",)),
    (("lin",), ()),
    (("wo1", "ffout"), ("v1_0", "k1_1")),
    ((), ("k1_0",)),
    ((), ("q1_1", "zT", "v1_1", "logit")),
]
AT = {"wo2": 2, "gate": 5, "gelu": 6, "glu": 6, "sums": 8, "logit": 8}
STREAM = {n: s for s, names in (("A", "wo1"), ("B", "k2_0 k2_1 h2T q2_0 q2_1 v2_0 v2_1"),
                                ("C", "wo2 h3T gate lin ffout zT logit"),
                                ("N", "q1_0 q1_1 k1_0 k1_1 v1_0 v1_1")) for n in names.split()}
ON_DVE = ("gate", "lin", "ffout", "logit", "wo1", "wo2")
PROJ_USES = [(n, STREAM[n], "dve" if n in ON_DVE else "act") for parts in FILL for part in parts for n in part]
NBANK = 3
RSQRT_STEPS = 11
FIRST_LOOPED = 3


def streams(i):
    return {s for s, b in (("A", i), ("B", i - 1), ("C", i - 2), ("N", i + 1)) if 0 <= b < B}


def proj_plan():
    full, done, last, plan = 0, {"act": 0, "dve": 0}, [None] * NBANK, {}
    for i in range(-1, B + 2):
        for n, (name, stream, eng) in enumerate(PROJ_USES):
            if stream not in streams(i):
                continue
            full += 1
            done[eng] += 1
            plan[i, name] = (n % NBANK, full, done[eng], last[n % NBANK])
            last[n % NBANK] = (eng, done[eng])
    return plan


def units_before(i):
    return sum(QH * (("A" in streams(j)) + ("B" in streams(j))) for j in range(-1, i))


def units(S):
    found = [(s, j) for s in "AB" for j in range(QH)]
    places = [n for n, (s, _) in enumerate(found) if s in S]
    row = [(*unit, places.index(n)) if n in places else None for n, unit in enumerate(found)]
    return lambda k: row[k] if 0 <= k < len(row) else None


def is_iteration(i, n):
    return isinstance(i, int) and i == n


def at(i, count):
    if isinstance(i, int):
        return count(i)
    a, b = count(FIRST_LOOPED), count(FIRST_LOOPED + 1)
    assert all(count(j) == a + (j - FIRST_LOOPED) * (b - a) for j in range(FIRST_LOOPED, B - 1))
    return i * (b - a) + (a - FIRST_LOOPED * (b - a))


def from_one(eng, sem, count):
    if not isinstance(count, int) or count >= 1:
        eng.wait_ge(sem, count)


def skewed(eng, nblk, step):
    rounds = (nblk - 2 * NSLOT + 1) // NSLOT
    for n in range(-2, NSLOT + 1):
        step(n // NSLOT, n % NSLOT)
    with eng.Fori(1, 1 + rounds) as q:
        for u in range(1, NSLOT):
            step(q, u)
        step(q + 1, 0)
    for n in range(NSLOT * (rounds + 1) + 1, nblk + 1):
        step(n // NSLOT, n % NSLOT)


def exists(n, nblk):
    return not isinstance(n, int) or 0 <= n < nblk


def program(nc, A, row_names, out):
    PLAN = proj_plan()
    with ExitStack() as ctx:
        def sb(name, *shape, dt=F32):
            return ctx.enter_context(nc.sbuf_tensor("sb_" + name, list(shape), dt))

        phase1 = ctx.enter_context(ExitStack())

        def sb1(name, *shape, dt=F32):
            return phase1.enter_context(nc.sbuf_tensor("sb_" + name, list(shape), dt))

        def sem(name):
            return ctx.enter_context(nc.semaphore(name))

        eye = sb("eye", P, P)
        tri = sb("tri", P, P)
        ones = sb("ones", P, P)
        zeros = sb("zeros", P, P)
        cols = sb("cols", P, 24)
        rows = sb("rows", P, A["rows"].shape[0])
        x_sb = sb("x", P, B, D)
        z_all = sb("z_all", P, B, D)
        ctx_n = sb("ctx", C, B, D)
        logits = sb("logits", P, B, EB)
        gate_up = sb("gate_up", P, EA + 1, 2 * IA)
        down = sb("down", P, EA + 1, CA, D)
        wr = sb("wr", P, EA)
        wgate = sb("wgate", P, EB)
        slot_w = sb("slot_w", P, 6, D)
        st_all = sb("st_all", P, B, 6)
        mv_all = sb("mv_all", P, B, 2)
        rsq_all = sb("rsq_all", P, 3, B)
        rstd_all = sb("rstd_all", P, B)
        tok_ids = sb("tok_ids", P, 3, B)
        expert_a = sb("expert_a", 1, NR, dt=I32)
        expert_b = sb("expert_b", 1, NB, dt=I32)

        x0b = sb1("x0b", P, B, D)
        h1T = sb1("h1T", P, B, P)
        ctxT = sb1("ctxT", P, B * C)
        cond_t = sb1("cond_t", P, B)
        nw = sb1("norm_w", P, 3, 2 * D)
        ada = sb1("ada", P, 3, 2, B)
        watt = sb1("watt", P, 2, 4, INNER)
        w1 = sb1("ff_w1", P, 2 * FF)
        w2 = sb1("ff_w2", P, FF // P, D)
        q1T, k1T, q2T = (sb1(n, P, NCH, P) for n in ("q1T", "k1T", "q2T"))
        k2T = sb1("k2T", P, NCH, C)
        v1 = sb1("v1", P, H, DH)
        v2 = sb1("v2", C, H, DH)
        shifted = sb1("shifted", P, 2, QH, P)
        expd = sb1("expd", P, 2, QH, P)
        probT = sb1("probT", P, 2, QH, P)
        smax = sb1("smax", P, 2, QH)
        row_sum = sb1("row_sum", P, 2, QH)
        rden = sb1("rden", P, 2, QH)
        oT = {s: sb1("oT" + s, P, NCH, P) for s in "AB"}
        xa, xb, xbx = (sb1(n, P, D) for n in ("xa", "xb", "xbx"))
        zA, zB, zC = (sb1("z" + s, P, D) for s in "ABC")
        hcur1, h2T, h3T, zT = (sb1(n, P, P) for n in ("hcur1", "h2T", "h3T", "zT"))
        ctxcur = sb1("ctxcur", P, C)
        gpre = sb1("gpre", P, FF // P, P)
        gact = sb1("gact", P, FF // P, P)
        glu = sb1("glu", P, FF // P, P)
        st = [sb1(f"st{n}", P, 6) for n in range(3)]
        mv, rsq, rstd = sb1("mv", P, 3, 2), sb1("rsq", P, 3, 3), sb1("rstd", P, 3)
        phase1.close()

        w1b = sb("w1b", P, EB, FB)
        w2b = sb("w2b", P, EB, FB // P, D)
        spent = gate_up[:, :, :].rearrange("p e n -> p (e n)")
        b1b = spent[:, 0:EB * FB].rearrange("p (e n) -> p e n", e=EB)
        b2b = spent[:, EB * FB:EB * (FB + D)].rearrange("p (e n) -> p e n", e=EB)
        S = sb("S", P, B, D)
        s_rest = sb("s_rest", P, B, D)
        zs = z_all
        zsT = sb("zsT", P, B, P)
        hid = sb("hid", P, B, P)
        att_or_sent = sb("att_or_sent", P, B * ROW)
        att = att_or_sent[0:C, 0:B * P].rearrange("c (b t) -> c b t", b=B)
        cb2 = sb("cb2", P, B, D)
        kq = sb("kq", P, B, C)
        kqb = sb("kqb", C, B)
        vu = sb("vu", C, B, D + 1)
        es_b = sb("es_b", P, D)
        picked = sb("picked", P, B, 2, D)
        xinT, kkT, vT = (picked[:, 5 * n:5 * n + 5, :, :].rearrange("p b k d -> p (b k d)")[:, 0:B * C].rearrange(
            "p (b c) -> p b c", b=B) for n in range(3))
        sh_act = hid[:, 0:4 * CA, :].rearrange("p (c b) t -> p c (b t)", c=CA)
        sh_h = [t[:, 0:4 * CA, :].rearrange("p (c b) t -> p c (b t)", c=CA) for t in (S, s_rest)]
        sent = [t.rearrange("p (b d) -> p b d", b=B) for t in (sb("sent", P, B * ROW)[:, :], att_or_sent[:, :])]
        blk_x = sb("blk_x", P, NSLOT, ROW)
        meta = sb("meta", P, NR, 2)
        dest = sb("dest", P, NSLOT, dt=I32)
        blk_xT = sb("blk_xT", P, 2, P)
        blk_act, blk_h = (hid[:, 8 * n:8 * n + 8, :].rearrange("p (u c) t -> p u (c t)", u=2) for n in range(2))
        blk_hT = zsT[:, 0:8, :].rearrange("p (u c) t -> p u c t", u=2)
        blk_y = sb("blk_y", P, NSLOT, D)
        hot1, hot2, hot, run, slot, rt = (sb(n, P, EB, B) for n in ("hot1", "hot2", "hot", "run", "slot", "rt"))
        top1, top2, idx, wgt1, wgt2, slot1f, slot2f = (
            sb(n, P, B) for n in ("top1", "top2", "idx", "wgt1", "wgt2", "slot1f", "slot2f"))
        slot1, slot2 = (sb(n, P, B, dt=I32) for n in ("slot1", "slot2"))
        cnt, nblk, cblk, base = (sb(n, P, EB) for n in ("cnt", "nblk", "cblk", "base"))
        bge = sb("bge", 1, NR, EB)
        bex = sb("bex", 1, NR)
        lgmax, nmax, esum, rsum, rcol, nbias = (sb(n, P, B) for n in ("lgmax", "nmax", "esum", "rsum", "rcol", "nbias"))

        rows_a = nc.dram_tensor("rows_a", (NR * P, ROW), F32, kind="Internal").ap()
        rows_b = nc.dram_tensor("rows_b", (NB * P, ROW), F32, kind="Internal").ap()
        back_a = nc.dram_tensor("back_a", (2 * TOK + NR * P, D), F32, kind="Internal").ap()
        back_b = nc.dram_tensor("back_b", (TOK + NB * P, D), F32, kind="Internal").ap()

        wq, wk, wv = ([watt[:, a, j, :] for a in range(2)] for j in range(3))
        wo = [watt[:, a, 3, :].rearrange("p (c n) -> p c n", c=NCH) for a in range(2)]
        R = {}
        at_col = 0
        for name, n in row_names:
            R[name] = rows[:, at_col:at_col + n]
            at_col += n
        wks, wvs, wqTs, wus, w1s, w2s = (slot_w[:, n, :] for n in range(6))
        lnkv_g, lnkv_b, lnq_g, lnq_b, lnm_g, lnm_b, bk, bq, sb1_, bv = (cols[:, 14 + n:15 + n] for n in range(10))

        bank = [ctx.enter_context(nc.psum_tensor(f"bank{n}", [P, 512], F32)) for n in range(8)]
        proj = bank[0:NBANK]

        def quads(t):
            return t[:, :].rearrange("p (h n) -> p h n", h=QH)

        score = [quads(t) for t in bank[3:5]]
        trans = [quads(t) for t in bank[5:7]]
        pvo = quads(bank[7])

        ld_x, ld_small, ld_att1, ld_att2, ld_ff, ld_ctx = (
            sem(n) for n in ("ld_x", "ld_small", "ld_att1", "ld_att2", "ld_ff", "ld_ctx"))
        ld_x_first, ld_rows, rows_added = sem("ld_x_first"), sem("ld_rows"), sem("rows_added")
        pre_dve = sem("pre_dve")
        pre_ada = sem("pre_ada")
        pre_T = sem("pre_T")
        pre_act = sem("pre_act")
        hcur_ready = sem("hcur_ready")
        ctxcur_ready = sem("ctxcur_ready")
        proj_full = sem("proj_full")
        emptied = {"act": sem("proj_act"), "dve": sem("proj_dve")}
        score_done, max_done, sub_done, exp_done = (
            sem(n) for n in ("score_done", "max_done", "sub_done", "exp_done"))
        row_sum_done, rden_done, norm_done, T_done, probT_ready, pv_done, o_kept = (
            sem(n) for n in ("row_sum_done", "rden_done", "norm_done", "T_done", "probT_ready", "pv_done", "o_kept"))
        gelu_done = sem("gelu_done")
        stats_done, mv_ready, ln_step = (
            {s: sem(n + s) for s in ("B", "CA")} for n in ("stats_done", "mv_ready", "ln_step"))
        pre_rsqrt = sem("pre_rsqrt")
        z_ready = {s: sem("z_ready" + s) for s in "ABC"}
        xab_ready, xbx_ready, z_kept = (sem(n) for n in ("xab_ready", "xbx_ready", "z_kept"))
        out_sem = sem("out_sem")

        ld_moe, ld_slot, ld_cond, ld_moe_b, zeroed, consts_ready, filled_rows = (
            sem(n) for n in ("ld_moe", "ld_slot", "ld_cond", "ld_moe_b", "zeroed", "consts_ready", "filled_rows"))
        pre_slot_full, pre_slot_done = sem("pre_slot_full"), sem("pre_slot_done")
        ctx_step, ctx_rsqrt = sem("ctx_step"), sem("ctx_rsqrt")
        rt_step = {x: sem("rt_step_" + x) for x in "ab"}
        hot_ready, rank_done, exp_in, exp_out, routed, table_ready, scattered = (
            {x: sem(n + x) for x in "ab"} for n in (
                "hot_ready_", "rank_done_", "exp_in_", "exp_out_", "routed_", "table_ready_", "scattered_"))
        blk_in, returned = ({x: [sem(f"{n}_{x}{u}") for u in range(NSLOT)] for x in "ab"} for n in ("blk_in", "returned"))
        meta_kept, dest_ready = ({x: sem(n + x) for x in "ab"} for n in ("meta_kept_", "dest_ready_"))
        sent_ready = sem("sent_ready")
        sh_T_done, sh_T_ready, sh_up_done, sh_act_done, sh_h_ready, sh_y_done, sh_added = (
            sem("sh_" + n) for n in ("T_done", "T_ready", "up_done", "act_done", "h_ready", "y_done", "added"))
        xT_done, xT_ready, up_done, act_done, h_ready, hT_done, hT_ready, y_done, y_ready = (
            {x: sem(n + x) for x in "ab"} for n in (
                "xT_done_", "xT_ready_", "up_done_", "act_done_", "h_ready_", "hT_done_", "hT_ready_", "y_done_", "y_ready_"))
        came_back = [sem(f"came_back{g}") for g in range(4)]
        x2_step = sem("x2_step")
        sl_step, sl_rsqrt = sem("sl_step"), sem("sl_rsqrt")
        statq_ready, statm_ready, stat3_ready = (
            sem("sl_" + n) for n in ("statq_ready", "statm_ready", "stat3_ready"))
        zqT_done, zqT_ready, lg_done, nmax_ready, att_exp, att_ready, upd_done, mid_ready, mid_rest = (
            sem("sl_" + n) for n in ("zqT_done", "zqT_ready", "lg_done", "nmax_ready", "att_exp",
                                     "att_ready", "upd_done", "mid_ready", "mid_rest"))
        zmT_done, zmT_ready, hid_done, hid_ready, mlp_done, sum_ready, S_ready, S_rest = (
            sem("sl_" + n) for n in ("zmT_done", "zmT_ready", "hid_done", "hid_ready", "mlp_done",
                                     "sum_ready", "S_ready", "S_rest"))
        zq_ready, zm_ready, z3_ready = (sem(n + "_ready") for n in ("sl_zq", "sl_zm", "z3"))
        normed_by_dve = sem("normed_by_dve")
        x3_ready, z3T_done, z3T_ready, lgb_done = (
            sem(n) for n in ("x3_ready", "z3T_done", "z3T_ready", "lgb_done"))
        fin_step = sem("fin_step")
        x2_by_pool = sem("x2_by_pool")
        fence, fence_pool = sem("fence"), sem("fence_pool")
        out_ready = sem("out_ready")
        G = 4
        LANES = ((0, 1), (2, 3))

        def tiles(lane):
            return range(4 * LANES[lane][0], 4 * LANES[lane][-1] + 4)

        NBLK = {"a": NR, "b": NB}
        RANK_BANK = {"a": 7, "b": 2}

        def first_phase_over(eng):
            eng.wait_ge(emptied["dve"], PLAN[B + 1, "logit"][2])
            eng.wait_ge(z_kept, B + 1)

        N_SMALL = 4
        FIRST_TILES = 4
        PRE_Z1, PRE_ADA, PRE_ALL = 6, 7, 13
        block = ctx.enter_context(nc.Block())

        @block.sync
        def _(sp):
            def load_x(first, last, sem_):
                sp.dma_start(x_sb[:, first:last, :], A["x"][first:last].rearrange("b s d -> s b d")).then_inc(sem_, 16)

            load_x(0, FIRST_TILES, ld_x_first)
            sp.dma_start(cond_t[:, :], A["cond_t"]).then_inc(ld_small, 16)
            sp.dma_start(nw[:, :, :], A["norm_w"].rearrange("n p d -> p n d")).then_inc(ld_small, 16)
            sp.dma_start(eye[:, :], A["eye"]).then_inc(ld_small, 16)
            sp.dma_start(cols[:, :], A["cols"]).then_inc(ld_small, 16)
            for j in range(3):
                sp.dma_start(watt[:, 0, j, :], A["att_w"][0, j]).then_inc(ld_att1, 16)
            load_x(FIRST_TILES, B, ld_x)
            sp.dma_start(rows[:, :], A["rows"].partition_broadcast(P)).then_inc(ld_rows, 16)
            sp.dma_start(ctx_n[:, :, :], A["ctx"].rearrange("b c d -> c b d")).then_inc(ld_ctx, 16)
            sp.dma_start(wo[0], A["att_wo"][0].rearrange("(c p) n -> p c n", p=P)).then_inc(ld_att1, 16)
            sp.dma_start(wr[:, :], A["wr_t"]).then_inc(ld_rows, 16)
            for j in range(3):
                sp.dma_start(watt[:, 1, j, :], A["att_w"][1, j]).then_inc(ld_att2, 16)
            sp.dma_start(wo[1], A["att_wo"][1].rearrange("(c p) n -> p c n", p=P)).then_inc(ld_att2, 16)
            sp.dma_start(w1[:, :], A["ff_w1"]).then_inc(ld_ff, 16)
            sp.dma_start(w2[:, :, :], A["ff_w2"].rearrange("(c p) n -> p c n", p=P)).then_inc(ld_ff, 16)
            sp.dma_start(gate_up[:, :, :], A["gate_up"]).then_inc(ld_moe, 16)
            sp.dma_start(down[:, :, :, :], A["down"]).then_inc(ld_moe, 16)
            sp.dma_start(tri[:, :], A["tri"]).then_inc(ld_moe, 16)
            sp.dma_start(tok_ids[:, :, :], A["tok_ids"]).then_inc(ld_slot, 16)
            sp.dma_start(wgate[:, :], A["wgate"]).then_inc(ld_slot, 16)
            sp.dma_start(slot_w[:, :, :], A["slot_w"].rearrange("n p d -> p n d")).then_inc(ld_slot, 16)
            sp.wait_ge(consts_ready, 1)
            for t, n, pad in ((rows_a, NR, A["pad_a"]), (rows_b, NB, A["pad_b"])):
                sp.dma_start(t[:, 0:D].rearrange("(n p) d -> p n d", p=P),
                             zeros[:, :].unsqueeze(1).broadcast_to([P, n, D])).then_inc(zeroed, 16)
                sp.dma_start(t[:, D:], pad).then_inc(zeroed, 16)
            first_phase_over(sp)
            sp.dma_start(cb2[:, :, :].rearrange("p b d -> p (b d)"),
                         A["cond"].rearrange("b d -> (b d)").partition_broadcast(P)).then_inc(ld_cond, 16)

            def load(x, src, m, u):
                from_one(sp, xT_done[x], m - NSLOT + 1)
                from_one(sp, meta_kept[x], m - NSLOT + 1)
                sp.dma_start(blk_x[:, u, 0:ROW], src[bass.ds(m * P, P), 0:ROW]).then_inc(blk_in[x][u], 16)

            def load_blocks(x, src):
                rounds = NBLK[x] // NSLOT
                for m in range(NSLOT):
                    load(x, src, m, m)
                with sp.Fori(1, rounds) as q:
                    for u in range(NSLOT):
                        load(x, src, NSLOT * q + u, u)
                for m in range(NSLOT * rounds, NBLK[x]):
                    load(x, src, m, m % NSLOT)
                for u in range(NSLOT):
                    sp.wait_ge(returned[x][u], 16 * len(range(u, NBLK[x], NSLOT)))

            sp.wait_ge(scattered["a"], 16 * 2 * B)
            load_blocks("a", rows_a)
            for g in range(G):
                sp.dma_start(picked[:, 4 * g:4 * g + 4, :, :],
                             back_a[8 * g * P:8 * (g + 1) * P, :].rearrange("(b s k) d -> s b k d", s=P, k=2)).then_inc(came_back[g], 16)
            sp.dma_start(w1b[:, :, :], A["w1b"].rearrange("e p n -> p e n")).then_inc(ld_moe_b, 16)
            sp.dma_start(w2b[:, :, :, :], A["w2b"].rearrange("e (c p) d -> p e c d", p=P)).then_inc(ld_moe_b, 16)
            sp.dma_start(spent[:, 0:EB * (FB + D)], A["b12"].partition_broadcast(P)).then_inc(ld_moe_b, 16)
            sp.wait_ge(scattered["b"], 16 * B)
            load_blocks("b", rows_b)
            for g in range(G):
                sp.dma_start(picked[:, 4 * g:4 * g + 4, 0, :],
                             back_b[4 * g * P:4 * (g + 1) * P, :].rearrange("(b s) d -> s b d", s=P)).then_inc(came_back[g], 16)
            for g in range(G):
                sp.wait_ge(out_ready, g + 1)
                sp.dma_start(out[4 * g:4 * g + 4].rearrange("b s d -> s b d"),
                             x_sb[:, 4 * g:4 * g + 4, :]).then_inc(out_sem, 16)
            sp.wait_ge(out_sem, 16 * G)

        @block.tensor
        def _(pe):
            pe.wait_ge(ld_small, 16 * N_SMALL)
            for n in range(3):
                for j in range(2):
                    mm = pe.matmul(proj[0][:, (2 * n + j) * B:(2 * n + j + 1) * B], nw[:, n, j * D:(j + 1) * D],
                                   cond_t[:, :], start=True, stop=True)
            mm.then_inc(pre_ada, 1)
            def turns(first, last):
                for g in range(first, last):
                    from_one(pe, pre_act, g - 1)
                    for n in range(4):
                        if 1 <= g <= 4:
                            mm = pe.transpose(trans[g % 2][:, n, 0:C], ctx_n[:, 4 * (g - 1) + n, :], eye[0:C, 0:C])
                        else:
                            mm = pe.transpose(trans[g % 2][:, n, :], z_all[:, 4 * max(g - 4, 0) + n, :], eye[:, :])
                    mm.then_inc(pre_T, 1)

            pe.wait_ge(pre_dve, PRE_Z1)
            turns(0, 1)

            def use(i, name):
                bank, _, _, free = PLAN[FIRST_LOOPED if not isinstance(i, int) else i, name]
                if free is not None:
                    pe.wait_ge(emptied[free[0]], at(i, lambda j: PLAN[j, name][3][1]))
                return proj[bank]

            def qk_proj(i, name, w, src, half, n):
                t = use(i, name)
                for c in range(4):
                    mm = pe.matmul(t[:, c * n:(c + 1) * n], w[:, (4 * half + c) * P:(4 * half + c + 1) * P], src,
                                   start=True, stop=True)
                mm.then_inc(proj_full, 1)

            def v_proj(i, name, w, src, half, n):
                t = use(i, name)
                pe.matmul(t[0:n, :], src, w[:, half * 512:(half + 1) * 512],
                          start=True, stop=True).then_inc(proj_full, 1)

            def turn(i, name, src):
                pe.transpose(use(i, name)[:, 0:P], src[:, :], eye[:, :]).then_inc(proj_full, 1)

            def o_proj(i, name, s, w):
                t = use(i, name)
                for c in range(NCH):
                    mm = pe.matmul(t[:, 0:D], oT[s][:, c, :], w[:, c, :], start=(c == 0), stop=(c == NCH - 1))
                mm.then_inc(proj_full, 1)

            def score_unit(i, u, s, j):
                q, k, n = (q1T, k1T, P) if s == "A" else (q2T, k2T, C)
                if not (isinstance(i, int) and units_before(i) + u < 2):
                    pe.wait_ge(sub_done, at(i, lambda t: units_before(t) + u - 1))
                p = slice(DH * (j % 2), DH * (j % 2) + DH)
                for h in range(QH):
                    mm = pe.matmul(score[u % 2][:, h, 0:n], q[p, 4 * (j // 2) + h, :],
                                   k[p, 4 * (j // 2) + h, 0:n], start=True, stop=True)
                mm.then_inc(score_done, 1)

            def prob_turn(i, u, s):
                n = P if s == "A" else C
                pe.wait_ge(norm_done, at(i, lambda t: units_before(t) + u + 1))
                if is_iteration(i, 1) and u == 0:
                    pe.wait_ge(pre_act, 8)
                if not (isinstance(i, int) and units_before(i) + u < 2):
                    pe.wait_ge(probT_ready, at(i, lambda t: units_before(t) + u - 1))
                for h in range(QH):
                    mm = pe.transpose(trans[u % 2][0:n, h, :], expd[:, u % 2, h, 0:n], eye[:, :])
                mm.then_inc(T_done, 1)

            def pv_pair(i, u, s, j):
                n, v = (P, v1) if s == "A" else (C, v2)
                pe.wait_ge(probT_ready, at(i, lambda t: units_before(t) + u + 1))
                if not (isinstance(i, int) and units_before(i) + u < 2):
                    pe.wait_ge(o_kept, at(i, lambda t: (units_before(t) + u - 1) // 2))
                for h in range(QH):
                    for r in range(2):
                        mm = pe.matmul(pvo[DH * r:DH * r + DH, h, :], v[:, 8 * (j // 2) + 2 * h + r, :],
                                       probT[0:n, (u - 1 + r) % 2, h, :], start=True, stop=True)
                mm.then_inc(pv_done, 1)

            def emptied_by(i, name, ago=0):
                eng = [e for n, _, e in PROJ_USES if n == name][0]
                pe.wait_ge(emptied[eng], at(i, lambda j: PLAN[j - ago, name][2]))

            def fill(i, name):
                half = int(name[-1]) if name[-1] in "01" and "_" in name else 0
                if name.startswith("k2"):
                    if is_iteration(i, 1):
                        pe.wait_ge(ld_att2, 64)
                    pe.wait_ge(ctxcur_ready, i)
                    qk_proj(i, name, wk[1], ctxcur[:, :], half, C)
                if name.startswith("v2"):
                    v_proj(i, name, wv[1], ctxcur[:, :], half, C)
                if name.startswith("q2"):
                    emptied_by(i, "h2T")
                    qk_proj(i, name, wq[1], h2T[:, :], half, P)
                if name.startswith("q1"):
                    pe.wait_ge(hcur_ready, i + 2)
                    qk_proj(i, name, wq[0], hcur1[:, :], half, P)
                if name.startswith("k1"):
                    qk_proj(i, name, wk[0], hcur1[:, :], half, P)
                if name.startswith("v1"):
                    v_proj(i, name, wv[0], hcur1[:, :], half, P)
                if name == "wo1":
                    pe.wait_ge(o_kept, at(i, lambda t: units_before(t) // 2 + QH // 2))
                    o_proj(i, name, "A", wo[0])
                if name == "wo2":
                    pe.wait_ge(o_kept, at(i, lambda t: units_before(t) // 2))
                    o_proj(i, name, "B", wo[1])
                if name == "h2T":
                    pe.wait_ge(z_ready["A"], i)
                    turn(i, name, zA)
                if name == "h3T":
                    pe.wait_ge(z_ready["B"], i - 1)
                    turn(i, name, zB)
                if name == "gate":
                    if is_iteration(i, 2):
                        pe.wait_ge(ld_ff, 32)
                        pe.wait_ge(ld_rows, 32)
                    emptied_by(i, "h3T")
                    qk_proj(i, name, w1[:, FF:2 * FF], h3T[:, :], 0, P)
                if name == "lin":
                    qk_proj(i, name, w1[:, 0:FF], h3T[:, :], 0, P)
                if name == "ffout":
                    t = use(i, name)
                    emptied_by(i, "lin")
                    for c in range(FF // P):
                        mm = pe.matmul(t[:, 0:D], glu[:, c, :], w2[:, c, :], start=(c == 0), stop=(c == FF // P - 1))
                    mm.then_inc(proj_full, 1)
                if name == "zT":
                    pe.wait_ge(z_ready["C"], i - 1)
                    turn(i, name, zC)
                if name == "logit":
                    t = use(i, name)
                    emptied_by(i, "zT")
                    pe.matmul(t[:, 0:EA], zT[:, :], wr[:, :], start=True, stop=True).then_inc(proj_full, 1)

            def iteration(i, S):
                unit = units(S)
                for k in range(N_STEPS):
                    if unit(k):
                        s, j, u = unit(k)
                        if j == 0:
                            emptied_by(i, "k1_1" if s == "A" else "q2_1", 1 if s == "A" else 0)
                        score_unit(i, u, s, j)
                    for name in FILL[k][0]:
                        if STREAM[name] in S:
                            fill(i, name)
                    if unit(k - 2):
                        prob_turn(i, unit(k - 2)[2], unit(k - 2)[0])
                    for name in FILL[k][1]:
                        if STREAM[name] in S:
                            fill(i, name)
                    if unit(k - 2) and unit(k - 2)[1] % 2:
                        s, j, u = unit(k - 2)
                        if j == 1:
                            emptied_by(i, "v1_1" if s == "A" else "v2_1", 1 if s == "A" else 0)
                        pv_pair(i, u, s, j)

            def rank_sums(x, n_exp):
                pe.wait_ge(hot_ready[x], 1)
                pe.wait_ge(ld_moe, 48)
                src = hot[:, 0:n_exp, :].rearrange("p e t -> p (e t)")
                w = n_exp * B
                t = bank[RANK_BANK[x]]
                pe.matmul(t[:, 0:w], tri[:, :], src, start=True, stop=True)
                mm = pe.matmul(t[:, P:P + w], ones[:, :], src, start=True, stop=True)
                mm.then_inc(rank_done[x], 1)

            pe.wait_ge(ld_att1, 64)
            iteration(-1, streams(-1))
            pe.wait_ge(ld_ctx, 16)
            turns(1, 5)
            pe.wait_ge(pre_act, 5)
            iteration(0, streams(0))
            pe.wait_ge(pre_dve, PRE_ALL)
            pe.wait_ge(probT_ready, units_before(1))
            turns(5, 8)
            for i in range(1, FIRST_LOOPED):
                iteration(i, streams(i))
            with pe.Fori(FIRST_LOOPED, B - 1) as i:
                iteration(i, set("ABCN"))
            for i in range(B - 1, B + 2):
                iteration(i, streams(i))

            first_phase_over(pe)
            pe.wait_ge(ld_slot, 48)
            uses = [0]

            def slot_bank():
                from_one(pe, pre_slot_done, uses[0] - 6)
                uses[0] += 1
                return bank[(uses[0] - 1) % 7]

            def flat(t, g):
                return t[:, 4 * g:4 * g + 4, :].rearrange("p b c -> p (b c)")

            for g in range(G):
                t = slot_bank()
                pe.wait_ge(ctx_step, 3)
                for n in range(4):
                    mm = pe.transpose(t[:, n * C:(n + 1) * C], ctx_n[:, 4 * g + n, :], eye[0:C, 0:C])
                mm.then_inc(pre_slot_full, 1)
            for stage, (w, src, rowsn) in enumerate(((wks, xinT, P), (wvs, xinT, P), (wqTs, kkT, P))):
                for g in range(G):
                    t = slot_bank()
                    pe.wait_ge(pre_slot_done, (g + 1) if src is xinT else G + g + 1)
                    pe.matmul(t[0:rowsn, 0:4 * C], w, flat(src, g), start=True, stop=True).then_inc(pre_slot_full, 1)
                if stage == 0:
                    rank_sums("a", EA)
            t = slot_bank()
            pe.wait_ge(pre_slot_done, 2 * G)
            for b in range(B):
                mm = pe.matmul(t[0:C, b:b + 1], kkT[:, b, :], bq, start=True, stop=True)
            mm.then_inc(pre_slot_full, 1)
            for g in range(G):
                t = slot_bank()
                pe.wait_ge(pre_slot_done, 2 * G + g + 1)
                for n in range(4):
                    mm = pe.matmul(t[0:C, n * D:(n + 1) * D], vT[:, 4 * g + n, :], wus, start=True, stop=True)
                mm.then_inc(pre_slot_full, 1)

            pe.wait_ge(ld_moe, 48)
            pe.wait_ge(pre_slot_done, 5 * G + 1)

            def sh_turn(g):
                from_one(pe, sh_T_ready, g)
                for n in range(4):
                    mm = pe.transpose(quads(bank[0])[:, n, :], z_all[:, 4 * g + n, :], eye[:, :])
                mm.then_inc(sh_T_done, 1)

            def sh_down(g):
                pe.wait_ge(sh_h_ready, CA * (g + 1))
                from_one(pe, sh_added, g)
                for n in range(4):
                    for c in range(CA):
                        w = min(P, IA - c * P)
                        mm = pe.matmul(quads(bank[7])[:, n, :], sh_h[g % 2][0:w, c, n * P:(n + 1) * P], down[0:w, EA, c, :],
                                       start=(c == 0), stop=(c == CA - 1))
                mm.then_inc(sh_y_done, 1)

            sh_turn(0)
            for g in range(G):
                pe.wait_ge(sh_T_ready, g + 1)
                for c in range(CA):
                    w = min(P, IA - c * P)
                    from_one(pe, sh_act_done, CA * (g - 1) + c + 1)
                    from_one(pe, sh_h_ready, CA * (g - 1) + c + 1)
                    for j in range(2):
                        mm = pe.matmul(bank[1 + CA * j + c][0:w, :], gate_up[:, EA, j * IA + c * P:j * IA + c * P + w],
                                       flat(zsT, g), start=True, stop=True)
                    mm.then_inc(sh_up_done, 1)
                    if c == 0 and g >= 1:
                        sh_down(g - 1)
                    if c == 1 and g + 1 < G:
                        sh_turn(g + 1)
            sh_down(G - 1)
            pe.wait_ge(sh_added, G)
            pe.wait_ge(table_ready["a"], 1)

            def turn_rows(x, q, u):
                m, r = NSLOT * q + u + 2, (u + 2) % NSLOT
                if exists(m, NBLK[x]):
                    pe.wait_ge(blk_in[x][r], 16 * (q + 1 + (u + 2) // NSLOT))
                    pe.transpose(bank[0][:, 0:P], blk_x[:, r, 0:D], eye[:, :]).then_inc(xT_done[x], 1)

            def expert_of(table, m, n_exp):
                return pe.value_load(table[0:1, bass.ds(m, 1)], min_val=0, max_val=n_exp - 1)

            def step_a(q, u):
                n, v, here = NSLOT * q + u, 1 - u % 2, u % 2
                if exists(n + 1, NR):
                    e_up = expert_of(expert_a, n + 1, EA)
                if exists(n - 1, NR):
                    e_down = expert_of(expert_a, n - 1, EA)
                if exists(n + 1, NR):
                    pe.wait_ge(xT_ready["a"], n + 2)
                turn_rows("a", q, u)
                if exists(n + 1, NR):
                    for j in range(2):
                        mm = pe.matmul(bank[1 + 2 * j + v][:, 0:IA], blk_xT[:, v, :],
                                       gate_up[:, bass.ds(e_up, 1), j * IA:(j + 1) * IA].rearrange("p a n -> p (a n)"),
                                       start=True, stop=True)
                    mm.then_inc(up_done["a"], 1)
                if exists(n, NR):
                    pe.wait_ge(h_ready["a"], n + 1)
                    from_one(pe, hT_ready["a"], n)
                    for c in range(CA):
                        w = min(P, IA - c * P)
                        mm = pe.transpose(bank[5][0:w, c * P:(c + 1) * P], blk_h[:, here, c * P:c * P + w], eye[:, :])
                    mm.then_inc(hT_done["a"], 1)
                if exists(n - 1, NR):
                    if is_iteration(n, NR):
                        pe.wait_ge(hT_ready["a"], NR)
                    from_one(pe, y_ready["a"], n - 2)
                    for c in range(CA):
                        w = min(P, IA - c * P)
                        mm = pe.matmul(bank[6 + v][:, 0:D], blk_hT[0:w, v, c, :],
                                       down[0:w, bass.ds(e_down, 1), c, :].rearrange("p a n -> p (a n)"),
                                       start=(c == 0), stop=(c == CA - 1))
                    mm.then_inc(y_done["a"], 1)

            skewed(pe, NR, step_a)

            def turn_group(g, ready, count, done, src=zs):
                pe.wait_ge(ready, count)
                for n in range(4):
                    mm = pe.transpose(quads(bank[2 * g])[:, n, :], src[:, 4 * g + n, 0:D], eye[:, :])
                mm.then_inc(done, 1)

            def slot_logits(it, lane):
                for g in LANES[lane]:
                    turn_group(g, zq_ready, it * G + g + 1, zqT_done)
                for g in LANES[lane]:
                    pe.wait_ge(zqT_ready, it * G + g + 1)
                    for n in range(4):
                        b = 4 * g + n
                        mm = pe.matmul(quads(bank[2 * g + 1])[0:C, n, :], kq[:, b, :], zsT[:, b, :], start=True, stop=True)
                    mm.then_inc(lg_done, 1)

            def slot_update(it, lane):
                for g in LANES[lane]:
                    pe.wait_ge(att_ready, it * G + g + 1)
                    for n in range(4):
                        b = 4 * g + n
                        mm = pe.matmul(bank[2 * g + n // 2][:, (n % 2) * (D + 1):(n % 2 + 1) * (D + 1)],
                                       att[:, b, :], vu[:, b, :], start=True, stop=True)
                    mm.then_inc(upd_done, 1)

            def slot_hidden(it, lane):
                for g in LANES[lane]:
                    if g == LANES[0][1]:
                        turn_group(g, normed_by_dve, it + 1, zmT_done)
                    else:
                        turn_group(g, zm_ready, it * (G - 1) + max(g, 1), zmT_done)
                for g in LANES[lane]:
                    pe.wait_ge(zmT_ready, it * G + g + 1)
                    pe.matmul(bank[2 * g + 1][:, :], w1s, flat(zsT, g), start=True, stop=True).then_inc(hid_done, 1)

            def slot_mlp(it, lane):
                for g in LANES[lane]:
                    pe.wait_ge(hid_ready, it * G + g + 1)
                    for n in range(4):
                        mm = pe.matmul(quads(bank[2 * g])[:, n, :], hid[:, 4 * g + n, :], w2s, start=True, stop=True)
                    mm.then_inc(mlp_done, 1)

            pe.wait_ge(y_ready["a"], NR)
            with pe.Fori(0, SLOT_ITERS) as it:
                slot_logits(it, 0)
                slot_update(it, 0)
                slot_logits(it, 1)
                slot_hidden(it, 0)
                slot_update(it, 1)
                slot_mlp(it, 0)
                slot_hidden(it, 1)
                slot_mlp(it, 1)

            for lane in range(2):
                for g in LANES[lane]:
                    if g == G - 1:
                        turn_group(g, normed_by_dve, SLOT_ITERS + 1, z3T_done, sent[0])
                    else:
                        turn_group(g, z3_ready, g + 1, z3T_done, sent[0])
                for g in LANES[lane]:
                    pe.wait_ge(z3T_ready, g + 1)
                    for n in range(4):
                        b = 4 * g + n
                        mm = pe.matmul(bank[1][:, b * EB:(b + 1) * EB], zsT[:, b, :], wgate[:, :], start=True, stop=True)
            mm.then_inc(lgb_done, 1)
            rank_sums("b", EB)
            pe.wait_ge(ld_moe_b, 48)
            pe.wait_ge(table_ready["b"], 1)

            def step_b(q, u):
                n, v, here = NSLOT * q + u, 1 - u % 2, u % 2
                if exists(n + 1, NB):
                    e_up = expert_of(expert_b, n + 1, EB)
                if exists(n - 1, NB):
                    e_down = expert_of(expert_b, n - 1, EB)
                if exists(n + 1, NB):
                    pe.wait_ge(xT_ready["b"], n + 2)
                turn_rows("b", q, u)
                if exists(n + 1, NB):
                    pe.matmul(bank[1 + v][:, :], blk_xT[:, v, :], w1b[:, bass.ds(e_up, 1), :].rearrange("p a n -> p (a n)"),
                              start=True, stop=True).then_inc(up_done["b"], 1)
                if exists(n, NB):
                    pe.wait_ge(h_ready["b"], n + 1)
                    for c in range(FB // P):
                        mm = pe.transpose(bank[3 + here][:, c * P:(c + 1) * P], blk_h[:, here, c * P:(c + 1) * P], eye[:, :])
                    mm.then_inc(hT_done["b"], 1)
                if exists(n - 1, NB):
                    pe.wait_ge(hT_ready["b"], n)
                    from_one(pe, y_ready["b"], n - 2)
                    for c in range(FB // P):
                        mm = pe.matmul(bank[5 + v][:, 0:D], blk_hT[:, v, c, :],
                                       w2b[:, bass.ds(e_down, 1), c, :].rearrange("p a n -> p (a n)"),
                                       start=(c == 0), stop=(c == FB // P - 1))
                    mm.then_inc(y_done["b"], 1)

            skewed(pe, NB, step_b)

        @block.scalar
        def _(act):
            def turned(first, last):
                for g in range(first, last):
                    act.wait_ge(pre_T, g + 1)
                    if 1 <= g <= 4:
                        ins = act.activation(ctxT[:, 4 * (g - 1) * C:4 * g * C].rearrange("p (n c) -> p n c", n=4),
                                             trans[g % 2][:, :, 0:C], ACT.Copy)
                    else:
                        for n in range(4):
                            b = 4 * max(g - 4, 0) + n
                            ins = act.activation(h1T[:, b, :], trans[g % 2][:, n, :], ACT.Identity,
                                                 bias=ada[:, 0, 1, b:b + 1], scale=ada[:, 0, 0, b:b + 1])
                    ins.then_inc(pre_act, 1)

            act.wait_ge(pre_dve, PRE_ADA)
            turned(0, 1)

            def empty(i, name, dst, src=None, **kw):
                bank = PLAN[FIRST_LOOPED if not isinstance(i, int) else i, name][0]
                act.wait_ge(proj_full, at(i, lambda j: PLAN[j, name][1]))
                act.activation(dst, src(proj[bank]), kw.pop("f", ACT.Copy), **kw).then_inc(emptied["act"], 1)

            def chunks(t, n):
                return t[:, 0:4 * n].rearrange("p (c n) -> p c n", c=4)

            def heads(t, n):
                return t[0:n, :].rearrange("p (h d) -> p h d", d=DH)

            def modulated(i, name, dst, norm, b):
                empty(i, name, dst[:, :], lambda t: t[:, 0:P], f=ACT.Identity,
                      bias=ada[:, norm, 1, bass.ds(b, 1)], scale=ada[:, norm, 0, bass.ds(b, 1)])

            def fill(i, name):
                half = int(name[-1]) if "_" in name else 0
                wide, head8 = slice(4 * half, 4 * half + 4), slice(8 * half, 8 * half + 8)
                if name[0] in "qk":
                    n = C if name[:2] == "k2" else P
                    empty(i, name, {"q1": q1T, "k1": k1T, "q2": q2T, "k2": k2T}[name[:2]][:, wide, :], lambda t: chunks(t, n))
                if name[0] == "v":
                    v, n = (v1, P) if name[1] == "1" else (v2, C)
                    empty(i, name, v[:, head8, :], lambda t: heads(t, n))
                if name == "h2T":
                    modulated(i, name, h2T, 1, i - 1)
                if name == "h3T":
                    modulated(i, name, h3T, 2, i - 2)
                if name == "zT":
                    empty(i, name, zT[:, :], lambda t: t[:, 0:P])

            def iteration(i, S):
                unit = units(S)
                for k in range(N_STEPS):
                    for name in FILL[k][0]:
                        if STREAM[name] in S and name not in ON_DVE:
                            fill(i, name)
                    if k == AT["gelu"] and "C" in S:
                        act.wait_ge(emptied["dve"], at(i, lambda j: PLAN[j, "gate"][2]))
                        act.activation(gact[:, :, :], gpre[:, :, :], ACT.Gelu).then_inc(gelu_done, 1)
                    if unit(k - 2):
                        s, _, u = unit(k - 2)
                        n = P if s == "A" else C
                        act.wait_ge(T_done, at(i, lambda t: units_before(t) + u + 1))
                        act.activation(probT[0:n, u % 2, :, :], trans[u % 2][0:n, :, :], ACT.Copy).then_inc(probT_ready, 1)
                    if unit(k):
                        s, _, u = unit(k)
                        n = P if s == "A" else C
                        act.wait_ge(sub_done, at(i, lambda t: units_before(t) + u + 1))
                        act.activation(expd[:, u % 2, :, 0:n], shifted[:, u % 2, :, 0:n], ACT.Exp,
                                       scale=DH ** -0.5).then_inc(exp_done, 1)
                    for name in FILL[k][1]:
                        if STREAM[name] in S and name not in ON_DVE:
                            fill(i, name)
                    if unit(k - 2) and unit(k - 2)[1] % 2:
                        s, j, u = unit(k - 2)
                        act.wait_ge(pv_done, at(i, lambda t: (units_before(t) + u + 1) // 2))
                        act.activation(oT[s][:, 4 * (j // 2):4 * (j // 2) + 4, :], pvo[:, :, :], ACT.Copy).then_inc(o_kept, 1)

            iteration(-1, streams(-1))
            turned(1, 5)
            iteration(0, streams(0))
            turned(5, 8)
            for i in range(1, FIRST_LOOPED):
                iteration(i, streams(i))
            with act.Fori(FIRST_LOOPED, B - 1) as i:
                iteration(i, set("ABCN"))
            for i in range(B - 1, B + 2):
                iteration(i, streams(i))

            first_phase_over(act)
            seen = [0]

            def from_slot_bank(dst, view, f=ACT.Copy, **kw):
                t = bank[seen[0] % 7]
                seen[0] += 1
                act.wait_ge(pre_slot_full, seen[0])
                act.activation(dst, view(t), f, **kw).then_inc(pre_slot_done, 1)

            def group_of(t, g):
                return t[:, 4 * g:4 * g + 4, :].rearrange("p b c -> p (b c)")

            wide = lambda t: t[:, 0:4 * C]
            for g in range(G):
                from_slot_bank(group_of(xinT, g), wide, ACT.Identity, scale=lnkv_g, bias=lnkv_b)
            for g in range(G):
                from_slot_bank(group_of(kkT, g), wide, ACT.Identity, bias=bk)
            act.wait_ge(exp_in["a"], 1)
            act.activation(wgt2[:, :], top2[:, :], ACT.Exp).then_inc(exp_out["a"], 1)
            for g in range(G):
                from_slot_bank(group_of(vT, g), wide, ACT.Identity, bias=bv)
            for g in range(G):
                from_slot_bank(group_of(kq, g), wide, scale=D ** 0.5)
            from_slot_bank(kqb[:, :], lambda t: t[0:C, 0:B], scale=D ** 0.5)
            for g in range(G):
                from_slot_bank(vu[:, 4 * g:4 * g + 4, 0:D], lambda t: quads(t)[0:C, :, :])

            def sh_turned(g):
                act.wait_ge(sh_T_done, g + 1)
                act.activation(group_of(zsT, g), bank[0][:, :], ACT.Copy).then_inc(sh_T_ready, 1)

            sh_turned(0)
            for g in range(G):
                for c in range(CA):
                    w = min(P, IA - c * P)
                    act.wait_ge(sh_up_done, CA * g + c + 1)
                    from_one(act, sh_h_ready, CA * (g - 1) + c + 1)
                    act.activation(sh_act[0:w, c, :], bank[1 + c][0:w, :], ACT.Silu).then_inc(sh_act_done, 1)
                    if c == 1 and g + 1 < G:
                        sh_turned(g + 1)

            def turned_rows(x, q, u, nblk):
                m = NSLOT * q + u + 2
                if exists(m, nblk):
                    act.wait_ge(xT_done[x], m + 1)
                    act.activation(blk_xT[:, u % 2, :], bank[0][:, 0:P], ACT.Copy).then_inc(xT_ready[x], 1)

            def step_a(q, u):
                n, v, here = NSLOT * q + u, 1 - u % 2, u % 2
                turned_rows("a", q, u, NR)
                if exists(n + 1, NR):
                    act.wait_ge(up_done["a"], n + 2)
                    act.activation(blk_act[:, v, 0:IA], bank[1 + v][:, 0:IA], ACT.Silu).then_inc(act_done["a"], 1)
                if exists(n, NR):
                    act.wait_ge(hT_done["a"], n + 1)
                    full = IA // P
                    act.activation(blk_hT[:, here, 0:full, :],
                                   bank[5][:, 0:full * P].rearrange("p (c n) -> p c n", n=P), ACT.Copy)
                    act.activation(blk_hT[0:IA - full * P, here, full, :], bank[5][0:IA - full * P, full * P:(full + 1) * P],
                                   ACT.Copy).then_inc(hT_ready["a"], 1)

            skewed(act, NR, step_a)

            act.wait_ge(ld_slot, 48)
            act.activation(es_b[:, :], R["q_logsig"], ACT.Exp).then_inc(exp_out["a"], 1)

            def modulated_group(g, done, count, ready, scale, bias):
                act.wait_ge(done, count)
                act.activation(group_of(zsT, g), bank[2 * g][:, :], ACT.Identity, scale=scale, bias=bias).then_inc(ready, 1)

            def normed(lane, stat, count, ready, src=S, dst=zs, groups=2):
                act.wait_ge(stat, count)
                for b in tiles(lane)[:4 * groups]:
                    ins = act.activation(dst[:, b, 0:D], src[:, b, :], ACT.Identity, scale=rstd_all[:, b:b + 1],
                                         bias=nbias[:, b:b + 1])
                    if b % 4 == 3:
                        ins.then_inc(ready, 1)

            def slot_queries(it, lane):
                normed(lane, statq_ready, it * 2 + lane + 1, zq_ready)
                for g in LANES[lane]:
                    modulated_group(g, zqT_done, it * G + g + 1, zqT_ready, lnq_g, lnq_b)

            def slot_exps(it, lane):
                act.wait_ge(nmax_ready, it * 2 + lane + 1)
                for g in LANES[lane]:
                    for n in range(4):
                        b = 4 * g + n
                        ins = act.activation(att[:, b, :], quads(bank[2 * g + 1])[0:C, n, :], ACT.Exp,
                                             bias=nmax[0:C, b:b + 1], accum_out=esum[0:C, b:b + 1])
                    ins.then_inc(att_exp, 1)

            def slot_turned(it, lane):
                for g in LANES[lane]:
                    modulated_group(g, zmT_done, it * G + g + 1, zmT_ready, lnm_g, lnm_b)

            def slot_gelu(it, lane):
                for g in LANES[lane]:
                    act.wait_ge(hid_done, it * G + g + 1)
                    act.activation(group_of(hid, g), bank[2 * g + 1][:, :], ACT.Gelu, bias=sb1_).then_inc(hid_ready, 1)

            with act.Fori(0, SLOT_ITERS) as it:
                slot_queries(it, 0)
                slot_exps(it, 0)
                slot_queries(it, 1)
                normed(0, statm_ready, it * 2 + 1, zm_ready, groups=1)
                slot_turned(it, 0)
                slot_exps(it, 1)
                slot_gelu(it, 0)
                normed(1, statm_ready, it * 2 + 2, zm_ready)
                slot_turned(it, 1)
                slot_gelu(it, 1)

            for lane in range(2):
                normed(lane, stat3_ready, lane + 1, z3_ready, x_sb, sent[0], groups=2 - lane)
                for g in LANES[lane]:
                    act.wait_ge(z3T_done, g + 1)
                    act.activation(group_of(zsT, g), bank[2 * g][:, :], ACT.Copy).then_inc(z3T_ready, 1)
            act.wait_ge(exp_in["b"], 1)
            act.activation(hot1[:, :, :].rearrange("p e t -> p t e"), hot2[:, :, :].rearrange("p e t -> p t e"),
                           ACT.Exp).then_inc(exp_out["b"], 1)

            def step_b(q, u):
                n, v, here = NSLOT * q + u, 1 - u % 2, u % 2
                turned_rows("b", q, u, NB)
                if exists(n, NB):
                    act.wait_ge(hT_done["b"], n + 1)
                    act.activation(blk_hT[:, here, :, :], bank[3 + here][:, :].rearrange("p (c n) -> p c n", n=P),
                                   ACT.Relu).then_inc(hT_ready["b"], 1)

            skewed(act, NB, step_b)

        @block.vector
        def _(dve):
            count, roots = [0], [0]

            def step(ins):
                count[0] += 1
                ins.then_inc(pre_dve, 1)

            def settle():
                dve.wait_ge(pre_dve, count[0])

            def rsqrt_steps(y, var, tmp, done, base, meanwhile=()):
                v, t = tmp[:, 0, :], tmp[:, 1, :]
                yi, vi = y.bitcast(I32), v.bitcast(I32)
                p = tmp[:, 2, :]
                steps = [lambda: dve.tensor_scalar(v, var, EPS, None, ALU.add),
                         lambda: dve.tensor_scalar(yi, vi, 1, None, ALU.logical_shift_right),
                         lambda: dve.tensor_scalar(yi, yi, -1, 0x5F3759DF, ALU.mult, ALU.add),
                         lambda: dve.tensor_tensor(t, y, y, ALU.mult),
                         lambda: dve.tensor_tensor(t, t, v, ALU.mult),
                         lambda: dve.scalar_tensor_tensor(y, t, -3.0, y, ALU.add, ALU.mult),
                         lambda: dve.tensor_tensor(t, y, y, ALU.mult),
                         lambda: dve.tensor_tensor(t, t, v, ALU.mult),
                         lambda: dve.tensor_scalar(p, t, -3.0 / 256.0, 10.0 / 64.0, ALU.mult, ALU.add),
                         lambda: dve.tensor_tensor(p, p, t, ALU.mult),
                         lambda: dve.scalar_tensor_tensor(y, p, -15.0 / 16.0, y, ALU.add, ALU.mult)]
                assert len(steps) == RSQRT_STEPS
                other = iter(meanwhile)
                for n, ins in enumerate(steps):
                    ins().then_inc(done, 1)
                    next(other, None)
                    dve.wait_ge(done, base + n + 1)
                if meanwhile:
                    stand()
                    for _ in other:
                        pass

            def norm_tiles(src, dst, first, last):
                some = range(first, last)
                for b in some:
                    ins = dve.bn_stats(st_all[:, b, :], src[:, b, :])
                step(ins)
                settle()
                for b in some:
                    ins = dve.bn_aggr(mv_all[:, b, :], st_all[:, b, :])
                step(ins)
                settle()
                rsqrt_steps(rstd_all[:, first:last], mv_all[:, first:last, 1], rsq_all[:, :, first:last], pre_rsqrt,
                            RSQRT_STEPS * roots[0])
                roots[0] += 1
                for b in some:
                    ins = dve.tensor_scalar(dst[:, b, :], src[:, b, :], mv_all[:, b, 0:1], rstd_all[:, b:b + 1],
                                            ALU.subtract, ALU.mult)
                step(ins)
                settle()

            def norm_x(first, last):
                norm_tiles(x_sb, x0b, first, last)
                norm_tiles(x0b, z_all, first, last)

            def norm_context():
                dve.wait_ge(pre_T, 5)
                for b in range(B):
                    ins = dve.bn_stats(st_all[0:C, b, :], ctx_n[:, b, :])
                ins.then_inc(ctx_step, 1)
                dve.wait_ge(ctx_step, 1)
                for b in range(B):
                    ins = dve.bn_aggr(mv_all[0:C, b, :], st_all[0:C, b, :])
                ins.then_inc(ctx_step, 1)
                dve.wait_ge(ctx_step, 2)
                rsqrt_steps(rstd_all[0:C, :], mv_all[0:C, :, 1], rsq_all[0:C], ctx_rsqrt, 0)
                for b in range(B):
                    ins = dve.tensor_scalar(ctx_n[:, b, :], ctx_n[:, b, :], mv_all[0:C, b, 0:1], rstd_all[0:C, b:b + 1],
                                            ALU.subtract, ALU.mult)
                ins.then_inc(ctx_step, 1)

            dve.wait_ge(ld_x_first, 16)
            norm_x(0, FIRST_TILES)
            assert count[0] == PRE_Z1
            dve.wait_ge(ld_small, 16 * N_SMALL)
            dve.wait_ge(pre_ada, 1)
            adaP = proj[0][:, 0:6 * B].rearrange("p (n j b) -> p n j b", n=3, j=2)
            for n in range(3):
                dve.tensor_scalar(ada[:, n, 0, :], adaP[:, n, 0, :], cols[:, 2 * n:2 * n + 1], 1.0, ALU.add, ALU.add)
                ins = dve.tensor_scalar(ada[:, n, 1, :], adaP[:, n, 1, :], cols[:, 2 * n + 1:2 * n + 2], None, ALU.add)
            step(ins)
            assert count[0] == PRE_ADA
            dve.wait_ge(ld_x, 16)
            norm_x(FIRST_TILES, B)
            assert count[0] == PRE_ALL

            def bank_of(i, name):
                return proj[PLAN[FIRST_LOOPED if not isinstance(i, int) else i, name][0]]

            def filled(i, name):
                dve.wait_ge(proj_full, at(i, lambda j: PLAN[j, name][1]))

            def stand():
                dve.sem_inc(fence, 1)

            def layernorms(key, b, parts, between=None):
                stand()
                for n, src, _, _ in parts:
                    ins = dve.bn_stats(st[n][:, :], src)
                ins.then_inc(stats_done[key], 1)
                if between:
                    between()
                dve.wait_ge(stats_done[key], b + 1)
                stand()
                for n, _, _, _ in parts:
                    ins = dve.bn_aggr(mv[:, n, :], st[n][:, :])
                ins.then_inc(mv_ready[key], 1)
                dve.wait_ge(mv_ready[key], b + 1)
                c = slice(parts[0][0], parts[-1][0] + 1)
                rsqrt_steps(rstd[:, c], mv[:, c, 1], rsq[:, :, c], ln_step[key], RSQRT_STEPS * b)
                for n, src, dst, ready in parts:
                    dve.tensor_scalar(dst[:, :], src, mv[:, n, 0:1], rstd[:, n:n + 1],
                                      ALU.subtract, ALU.mult).then_inc(ready, 1)

            def residual(i, name, dst, rest):
                filled(i, name)
                dve.tensor_tensor(dst, bank_of(i, name)[:, 0:D], rest, ALU.add).then_inc(emptied["dve"], 1)
                dve.wait_ge(emptied["dve"], at(i, lambda j: PLAN[j, name][2]))

            def tile(t, b):
                return t[:, bass.ds(b, 1), :].rearrange("p a d -> p (a d)")

            def softmax_in(i, s, u):
                n = P if s == "A" else C
                s_in = score[u % 2][:, :, 0:n]
                dve.wait_ge(score_done, at(i, lambda t: units_before(t) + u + 1))
                dve.tensor_reduce(smax[:, u % 2, :], s_in, X, ALU.max).then_inc(max_done, 1)
                dve.wait_ge(max_done, at(i, lambda t: units_before(t) + u + 1))
                dve.tensor_tensor(shifted[:, u % 2, :, 0:n], s_in, smax[:, u % 2, :].unsqueeze(2).broadcast_to([P, QH, n]),
                                  ALU.subtract).then_inc(sub_done, 1)

            def softmax_sums(i, s, u):
                n = P if s == "A" else C
                dve.wait_ge(exp_done, at(i, lambda t: units_before(t) + u + 1))
                dve.tensor_reduce(row_sum[:, u % 2, :], expd[:, u % 2, :, 0:n], X, ALU.add).then_inc(row_sum_done, 1)
                dve.wait_ge(row_sum_done, at(i, lambda t: units_before(t) + u + 1))
                if not (isinstance(i, int) and units_before(i) + u < 2):
                    dve.wait_ge(norm_done, at(i, lambda t: units_before(t) + u - 1))
                dve.reciprocal(rden[:, u % 2, :], row_sum[:, u % 2, :]).then_inc(rden_done, 1)

            def iteration(i, S):
                unit = units(S)
                c = i - 2
                for k in range(N_STEPS):
                    if is_iteration(i, B) and k == 0:
                        norm_context()
                    if unit(k):
                        softmax_in(i, unit(k)[0], unit(k)[2])
                    if unit(k - 1) and k != AT["sums"]:
                        softmax_sums(i, unit(k - 1)[0], unit(k - 1)[2])
                    if k == AT["wo2"] and "C" in S:
                        dve.wait_ge(xab_ready, c + 1)
                        residual(i, "wo2", xb[:, :], tile(x0b, c))
                        layernorms("B", c, [(2, xb[:, :], zB, z_ready["B"])])
                    if k == AT["gate"] and "C" in S:
                        filled(i, "gate")
                        dve.tensor_tensor(gpre[:, :, :], bank_of(i, "gate")[:, :].rearrange("p (c n) -> p c n", c=4),
                                          cols[:, 10:14].unsqueeze(2).broadcast_to([P, 4, P]),
                                          ALU.add).then_inc(emptied["dve"], 1)
                    if k == AT["glu"] and "C" in S:
                        filled(i, "lin")
                        dve.wait_ge(gelu_done, c + 1)
                        for n in range(FF // P):
                            ins = dve.scalar_tensor_tensor(glu[:, n, :], bank_of(i, "lin")[:, n * P:(n + 1) * P],
                                                           cols[:, 6 + n:7 + n], gact[:, n, :], ALU.add, ALU.mult)
                        ins.then_inc(emptied["dve"], 1)
                    if k == AT["sums"]:
                        parts = []
                        if "A" in S:
                            if isinstance(i, int) and i <= 1:
                                dve.wait_ge(rows_added, i + 1)
                            residual(i, "wo1", xa[:, :], tile(x0b, i))
                            parts += [(1, xa[:, :], zA, z_ready["A"])]
                        if "C" in S:
                            dve.wait_ge(xbx_ready, c + 1)
                            residual(i, "ffout", tile(x_sb, c), xbx[:, :])
                            dve.wait_ge(z_kept, c + 1)
                            parts = [(0, tile(x_sb, c), zC, z_ready["C"])] + parts
                        if parts:
                            layernorms("CA", i, parts, lambda: softmax_sums(i, unit(k - 1)[0], unit(k - 1)[2]) if unit(k - 1) else None)
                        elif unit(k - 1):
                            softmax_sums(i, unit(k - 1)[0], unit(k - 1)[2])
                    if k == AT["logit"] and "C" in S:
                        filled(i, "logit")
                        dve.tensor_tensor(tile(logits, c)[:, 0:EA], bank_of(i, "logit")[:, 0:EA], R["rb"],
                                          ALU.add).then_inc(emptied["dve"], 1)

            for i in range(-1, FIRST_LOOPED):
                iteration(i, streams(i))
            with dve.Fori(FIRST_LOOPED, B - 1) as i:
                iteration(i, set("ABCN"))
            for i in range(B - 1, B + 2):
                iteration(i, streams(i))


            def routing(x, n_exp, picks, table, n_blk):
                done, at_step = rt_step[x], [0]

                def link(ins):
                    at_step[0] += 1
                    ins.then_inc(done, 1)
                    dve.wait_ge(done, at_step[0])

                lg = logits[:, :, 0:n_exp]
                by_e = lambda t: t[:, 0:n_exp, :]
                by_t = lambda t: by_e(t).rearrange("p e t -> p t e")
                flat = lambda t: by_e(t).rearrange("p e t -> p (e t)")
                per_t = lambda t: t.unsqueeze(2).broadcast_to([P, B, n_exp])
                per_e = lambda t: t.unsqueeze(1).broadcast_to([P, B, n_exp])
                iota, iota100 = (per_e(R[n][:, 0:n_exp]) for n in ("iota", "iota100"))

                def first_best(vals, best, one_hot):
                    link(dve.tensor_reduce(best[:, :], vals, X, ALU.max))
                    link(dve.tensor_tensor(by_t(rt), vals, per_t(best[:, :]), ALU.is_equal))
                    link(dve.scalar_tensor_tensor(by_t(rt), by_t(rt), -100.0, iota100, ALU.mult, ALU.add))
                    link(dve.tensor_reduce(idx[:, :], by_t(rt), X, ALU.min))
                    link(dve.tensor_tensor(by_t(one_hot), iota, per_t(idx[:, :]), ALU.is_equal))

                if picks == 2:
                    first_best(lg, top1, hot1)
                    link(dve.scalar_tensor_tensor(by_t(slot), by_t(hot1), -3e38, lg, ALU.mult, ALU.add))
                    first_best(by_t(slot), top2, hot2)
                    link(dve.tensor_tensor(flat(hot), flat(hot1), flat(hot2), ALU.add))
                    dve.sem_inc(hot_ready[x], 1)
                    link(dve.tensor_tensor(top2[:, :], top2[:, :], top1[:, :], ALU.subtract))
                    dve.sem_inc(exp_in[x], 1)
                else:
                    first_best(lg, top1, hot)
                    dve.sem_inc(hot_ready[x], 1)
                    link(dve.tensor_tensor(by_t(hot2), lg, per_t(top1[:, :]), ALU.subtract))
                    dve.sem_inc(exp_in[x], 1)
                dve.wait_ge(rank_done[x], 1)
                t = bank[RANK_BANK[x]]
                w = n_exp * B
                link(dve.tensor_copy(flat(rt), t[:, P:P + w]))
                link(dve.tensor_tensor_scan(flat(run), flat(rt), zeros[:, 0:w], 0.0, ALU.add, ALU.add))
                link(dve.tensor_reduce(cnt[:, 0:n_exp], by_e(rt), X, ALU.add))
                link(dve.tensor_tensor(by_e(slot), cnt[:, 0:n_exp].unsqueeze(2).broadcast_to([P, n_exp, B]),
                                       R["edges"].unsqueeze(1).broadcast_to([P, n_exp, B]), ALU.is_gt))
                link(dve.tensor_reduce(nblk[:, 0:n_exp], by_e(slot), X, ALU.add))
                link(dve.tensor_tensor_scan(cblk[:, 0:n_exp], nblk[:, 0:n_exp], zeros[:, 0:n_exp], 0.0, ALU.add, ALU.add))
                link(dve.tensor_tensor(base[:, 0:n_exp], cblk[:, 0:n_exp], nblk[:, 0:n_exp], ALU.subtract))
                link(dve.scalar_tensor_tensor(base[:, 0:n_exp], base[:, 0:n_exp], float(P), cnt[:, 0:n_exp], ALU.mult, ALU.add))
                link(dve.tensor_tensor(base[:, 0:n_exp], base[:, 0:n_exp], run[:, 0:n_exp, B - 1], ALU.subtract))
                link(dve.tensor_tensor(flat(slot), flat(run), flat(rt), ALU.subtract))
                link(dve.tensor_tensor(flat(slot), flat(slot), t[:, 0:w], ALU.add))
                link(dve.tensor_tensor(by_e(slot), by_e(slot), base[:, 0:n_exp].unsqueeze(2).broadcast_to([P, n_exp, B]), ALU.add))
                for one_hot, f, i in (((hot1, slot1f, slot1), (hot2, slot2f, slot2)) if picks == 2 else ((hot, slot1f, slot1),)):
                    link(dve.tensor_tensor(flat(rt), flat(one_hot), flat(slot), ALU.mult))
                    link(dve.tensor_reduce(f[:, :], by_t(rt), X, ALU.add))
                    link(dve.tensor_copy(i[:, :], f[:, :]))
                if picks == 2:
                    dve.wait_ge(exp_out[x], 1)
                    link(dve.tensor_scalar(top1[:, :], wgt2[:, :], 1.0, None, ALU.add))
                    link(dve.reciprocal(wgt1[:, :], top1[:, :]))
                    link(dve.tensor_copy(sent[0][:, :, D + 1], wgt1[:, :]))
                    link(dve.tensor_tensor(sent[1][:, :, D + 1], wgt2[:, :], wgt1[:, :], ALU.mult))
                dve.sem_inc(routed[x], 1)
                link(dve.tensor_tensor(bge[0:1, 0:n_blk, 0:n_exp], R["blocks"][0:1, 0:n_blk].unsqueeze(2).broadcast_to([1, n_blk, n_exp]),
                                       cblk[0:1, 0:n_exp].unsqueeze(1).broadcast_to([1, n_blk, n_exp]), ALU.is_ge))
                link(dve.tensor_reduce(bex[0:1, 0:n_blk], bge[0:1, 0:n_blk, 0:n_exp], X, ALU.add))
                link(dve.tensor_scalar(table[0:1, :], bex[0:1, 0:n_blk], float(n_exp - 1), None, ALU.min))
                dve.sem_inc(table_ready[x], 1)
                if picks == 1:
                    dve.wait_ge(exp_out[x], 1)
                    link(dve.tensor_reduce(top1[:, :], by_t(hot1), X, ALU.add))
                    link(dve.reciprocal(wgt1[:, :], top1[:, :]))

            first_phase_over(dve)
            dve.memset(vu[:, :, D:D + 1], 1.0)
            routing("a", EA, 2, expert_a, NR)

            def group(t, g):
                return t[:, 4 * g:4 * g + 4, :]

            def add_shared(g):
                dve.wait_ge(sh_y_done, g + 1)
                dve.tensor_tensor(group(x_sb, g), group(x_sb, g), quads(bank[7])[:, :, :], ALU.add).then_inc(sh_added, 1)

            for g in range(G):
                from_one(dve, sh_y_done, g - 1)
                for c in range(CA):
                    w = min(P, IA - c * P)
                    dve.wait_ge(sh_act_done, CA * g + c + 1)
                    dve.tensor_tensor(sh_h[g % 2][0:w, c, :], bank[1 + CA + c][0:w, :], sh_act[0:w, c, :],
                                      ALU.mult).then_inc(sh_h_ready, 1)
                    if c == 0 and g >= 1:
                        add_shared(g - 1)
            add_shared(G - 1)

            def step_a(q, u):
                n, v, here = NSLOT * q + u, 1 - u % 2, u % 2
                if exists(n + 1, NR):
                    dve.wait_ge(act_done["a"], n + 2)
                    dve.tensor_tensor(blk_h[:, v, 0:IA], bank[3 + v][:, 0:IA], blk_act[:, v, 0:IA],
                                      ALU.mult).then_inc(h_ready["a"], 1)
                if exists(n - 1, NR):
                    dve.wait_ge(meta_kept["a"], n)
                    leave("a", q, u, bank[6 + v], meta[:, bass.ds(n - 1, 1), 1:2].rearrange("p a n -> p (a n)"), ALU.mult)

            def leave(x, q, u, t, other, op):
                m, r = NSLOT * q + u - 1, (u - 1) % NSLOT
                dve.wait_ge(y_done[x], m + 1)
                from_one(dve, returned[x][r], 16 * (q - (u == 0)))
                if op == ALU.mult:
                    dve.tensor_scalar(blk_y[:, r, :], t[:, 0:D], other, None, op).then_inc(y_ready[x], 1)
                else:
                    dve.tensor_tensor(blk_y[:, r, :], t[:, 0:D], other, op).then_inc(y_ready[x], 1)

            skewed(dve, NR, step_a)

            class Count:

                def __init__(self, links, roots):
                    self.links0, self.roots0, self.links, self.roots = links, roots, 0, 0

            def link(at_, ins):
                at_.links += 1
                ins.then_inc(sl_step, 1)
                dve.wait_ge(sl_step, at_.links0 + at_.links)

            def measured(at_, lane, src):
                last = tiles(lane)[-1]
                stand()
                for b in tiles(lane):
                    ins = dve.bn_stats(st_all[:, b, :], src[:, b, :])
                    if b == last:
                        link(at_, ins)
                        stand()
                    yield
                for b in tiles(lane):
                    ins = dve.bn_aggr(mv_all[:, b, :], st_all[:, b, :])
                    if b == last:
                        link(at_, ins)
                    yield

            def deviations(at_, lane, meanwhile=()):
                c = slice(tiles(lane)[0], tiles(lane)[-1] + 1)
                root = at_.roots0 + at_.roots
                at_.roots += 1
                rsqrt_steps(rstd_all[:, c], mv_all[:, c, 1], rsq_all[:, :, c], sl_rsqrt, root * RSQRT_STEPS, meanwhile)

            def statistics(at_, lane, src, stat, meanwhile=()):
                for _ in measured(at_, lane, src):
                    pass
                deviations(at_, lane, meanwhile)
                c = slice(tiles(lane)[0], tiles(lane)[-1] + 1)
                dve.scalar_tensor_tensor(nbias[:, c], mv_all[:, c, 0], -1.0, rstd_all[:, c], ALU.mult, ALU.mult).then_inc(stat, 1)

            def scaled(at_, lane, src, scale, shift):
                def centred():
                    for b in tiles(lane):
                        ins = dve.scalar_tensor_tensor(S[:, b, :], src[:, b, :], mv_all[:, b, 0:1], scale, ALU.subtract, ALU.mult)
                        if b == tiles(lane)[-1]:
                            link(at_, ins)
                        yield

                deviations(at_, lane, centred())
                for b in tiles(lane):
                    ins = dve.scalar_tensor_tensor(S[:, b, :], S[:, b, :], rstd_all[:, b:b + 1], shift, ALU.mult, ALU.add)
                    if b % 4 == 3:
                        ins.then_inc(S_ready, 1)

            def last_of(it, lane):
                return it * G + LANES[lane][-1] + 1

            def queries(at_, it, lane, meanwhile=()):
                dve.wait_ge(S_ready, last_of(it, lane))
                statistics(at_, lane, S, statq_ready, meanwhile)

            def maxima(at_, it, lane):
                c = slice(tiles(lane)[0], tiles(lane)[-1] + 1)
                for g in LANES[lane]:
                    dve.wait_ge(lg_done, it * G + g + 1)
                    ins = dve.tensor_reduce(lgmax[0:C, 4 * g:4 * g + 4], quads(bank[2 * g + 1])[0:C, :, :], X, ALU.max)
                link(at_, ins)
                link(at_, dve.scalar_tensor_tensor(nmax[0:C, c], lgmax[0:C, c], -1.0, kqb[:, c], ALU.mult, ALU.subtract))
                dve.tensor_tensor(nmax[0:C, c], nmax[0:C, c], kqb[:, c], ALU.add).then_inc(nmax_ready, 1)

            def shares(at_, it, lane):
                for g in LANES[lane]:
                    dve.wait_ge(att_exp, it * G + g + 1)
                    link(at_, dve.reciprocal(rsum[0:C, 4 * g:4 * g + 4], esum[0:C, 4 * g:4 * g + 4]))
                    yield
                    for b in range(4 * g, 4 * g + 4):
                        ins = dve.tensor_scalar(att[:, b, :], att[:, b, :], rsum[0:C, b:b + 1], 1e-8, ALU.mult, ALU.add)
                        if b % 4 == 3:
                            ins.then_inc(att_ready, 1)
                        yield

            def updates(at_, it, lane):
                for g in LANES[lane]:
                    dve.wait_ge(upd_done, it * G + g + 1)
                    for j in range(2):
                        ins = dve.reciprocal(rcol[:, 4 * g + 2 * j:4 * g + 2 * j + 2],
                                             bank[2 * g + j][:, D:2 * (D + 1):D + 1])
                    link(at_, ins)
                    dve.wait_ge(S_rest, it * G + g + 1)
                    for n in range(4):
                        b = 4 * g + n
                        ins = dve.scalar_tensor_tensor(S[:, b, :], bank[2 * g + n // 2][:, (n % 2) * (D + 1):(n % 2) * (D + 1) + D],
                                                       rcol[:, b:b + 1], s_rest[:, b, :], ALU.mult, ALU.add)
                    ins.then_inc(mid_ready, 1)

            def mlp_in(at_, it, lane, meanwhile=()):
                dve.wait_ge(mid_ready, last_of(it, lane))
                statistics(at_, lane, S, statm_ready, meanwhile)

            def normed_here(g, src, dst):
                for b in range(4 * g, 4 * g + 4):
                    ins = dve.tensor_scalar(dst[:, b, 0:D], src[:, b, :], mv_all[:, b, 0:1], rstd_all[:, b:b + 1],
                                            ALU.subtract, ALU.mult)
                ins.then_inc(normed_by_dve, 1)

            def mlp_sums(at_, it, lane):
                for g in LANES[lane]:
                    dve.wait_ge(mlp_done, it * G + g + 1)
                    dve.wait_ge(mid_rest, it * G + g + 1)
                    dve.tensor_tensor(group(S, g), quads(bank[2 * g])[:, :, :], group(s_rest, g), ALU.add).then_inc(sum_ready, 1)
                    yield
                dve.wait_ge(sum_ready, last_of(it, lane))
                yield from measured(at_, lane, S)

            def mlp_out(at_, lane):
                scaled(at_, lane, S, R["lnp_g"], R["lnp_b"])

            def layer1_in(at_, lane, meanwhile=()):
                dve.wait_ge(S_ready, last_of(SLOT_ITERS, lane))
                for g in LANES[lane]:
                    dve.tensor_tensor(group(x_sb, g), group(x_sb, g), group(S, g), ALU.add).then_inc(x3_ready, 1)
                dve.wait_ge(x3_ready, LANES[lane][-1] + 1)
                statistics(at_, lane, x_sb, stat3_ready, meanwhile)

            def slot_round(at_, it, last):
                maxima(at_, it, 0)
                queries(at_, it, 1, shares(at_, it, 0))
                updates(at_, it, 0)
                mlp_in(at_, it, 0)
                normed_here(LANES[0][1], S, zs)
                maxima(at_, it, 1)
                for _ in shares(at_, it, 1):
                    pass
                updates(at_, it, 1)
                mlp_in(at_, it, 1, mlp_sums(at_, it, 0))
                mlp_out(at_, 0)
                if last:
                    layer1_in(at_, 0, mlp_sums(at_, it, 1))
                else:
                    queries(at_, it + 1, 0, mlp_sums(at_, it, 1))
                mlp_out(at_, 1)
                if last:
                    layer1_in(at_, 1)
                    normed_here(G - 1, x_sb, sent[0])

            setup = Count(0, 0)
            dve.wait_ge(exp_out["a"], 2)

            def x2_sums(lane):
                if lane == 0:
                    for k in range(2):
                        for g in LANES[lane]:
                            dve.wait_ge(came_back[g], 16)
                            dve.tensor_tensor(group(x_sb, g), group(x_sb, g), picked[:, 4 * g:4 * g + 4, k, :],
                                              ALU.add).then_inc(x2_step, 1)
                        dve.wait_ge(x2_step, 2 * k + 2)
                else:
                    dve.wait_ge(x2_by_pool, 4)
                yield from measured(setup, lane, x_sb)

            for _ in x2_sums(0):
                pass
            scaled(setup, 0, x_sb, es_b[:, :], R["q_mu"])
            queries(setup, 0, 0, x2_sums(1))
            scaled(setup, 1, x_sb, es_b[:, :], R["q_mu"])
            LINKS, ROOTS = 26, 6
            with dve.Fori(0, SLOT_ITERS - 1) as it:
                inner = Count(it * LINKS + setup.links, it * ROOTS + setup.roots)
                slot_round(inner, it, False)
                assert (inner.links, inner.roots) == (LINKS, ROOTS)
            slot_round(Count((SLOT_ITERS - 1) * LINKS + setup.links, (SLOT_ITERS - 1) * ROOTS + setup.roots),
                       SLOT_ITERS - 1, True)

            dve.wait_ge(lgb_done, 1)
            dve.tensor_tensor(logits[:, :, :], bank[1][:, 0:B * EB].rearrange("p (b e) -> p b e", b=B),
                              R["b_gate"].unsqueeze(1).broadcast_to([P, B, EB]), ALU.add).then_inc(fin_step, 1)
            dve.wait_ge(fin_step, 1)
            routing("b", EB, 1, expert_b, NB)

            def expert_of(m):
                return dve.value_load(expert_b[0:1, bass.ds(m, 1)], min_val=0, max_val=EB - 1)

            def step_b(q, u):
                n, v, here = NSLOT * q + u, 1 - u % 2, u % 2
                if exists(n + 1, NB):
                    dve.wait_ge(up_done["b"], n + 2)
                    e = expert_of(n + 1)
                    dve.tensor_tensor(blk_h[:, v, :], bank[1 + v][:, :], b1b[:, bass.ds(e, 1), :].rearrange("p a n -> p (a n)"),
                                      ALU.add).then_inc(h_ready["b"], 1)
                if exists(n - 1, NB):
                    e = expert_of(n - 1)
                    leave("b", q, u, bank[5 + v], b2b[:, bass.ds(e, 1), :].rearrange("p a n -> p (a n)"), ALU.add)

            dve.wait_ge(ld_moe_b, 48)
            skewed(dve, NB, step_b)
            for g in range(G):
                dve.wait_ge(came_back[g], 32)
                for b in range(4 * g, 4 * g + 4):
                    ins = dve.scalar_tensor_tensor(x_sb[:, b, :], picked[:, b, 0, :], wgt1[:, b:b + 1], x_sb[:, b, :],
                                                   ALU.mult, ALU.add)
                ins.then_inc(out_ready, 1)

        @block.gpsimd
        def _(pool):
            pool.memset(ones[:, :], 1.0)
            pool.memset(zeros[:, :], 0.0).then_inc(consts_ready, 1)
            pool.sem_inc(z_kept, 1)

            def tile(t, b):
                return t[:, bass.ds(b, 1), :].rearrange("p a d -> p (a d)")

            def iteration(i, S):
                if "N" in S:
                    if is_iteration(i, -1):
                        pool.wait_ge(pre_act, 1)
                    else:
                        pool.wait_ge(proj_full, at(i, lambda j: PLAN[j - 1, "v1_1"][1]))
                    pool.tensor_copy(hcur1[:, :], tile(h1T, i + 1)).then_inc(hcur_ready, 1)
                if "B" in S:
                    if is_iteration(i, 1):
                        pool.wait_ge(pre_act, 8)
                    else:
                        pool.wait_ge(proj_full, at(i, lambda j: PLAN[j - 1, "v2_1"][1]))
                    pool.tensor_copy(ctxcur[:, :], ctxT[:, bass.ds((i - 1) * C, C)]).then_inc(ctxcur_ready, 1)
                unit = units(S)
                for k in range(N_STEPS):
                    if unit(k - 1):
                        s, _, u = unit(k - 1)
                        n = P if s == "A" else C
                        e = expd[:, u % 2, :, 0:n]
                        pool.wait_ge(rden_done, at(i, lambda t: units_before(t) + u + 1))
                        pool.tensor_tensor(e, e, rden[:, u % 2, :].unsqueeze(2).broadcast_to([P, QH, n]),
                                           ALU.mult).then_inc(norm_done, 1)
                    if "C" in S and k == AT["wo2"] + 1:
                        pool.wait_ge(emptied["dve"], at(i, lambda j: PLAN[j, "wo2"][2]))
                        pool.tensor_tensor(xbx[:, :], xb[:, :], tile(x_sb, i - 2), ALU.add).then_inc(xbx_ready, 1)
                if "A" in S:
                    pool.wait_ge(emptied["dve"], at(i, lambda j: PLAN[j, "wo1"][2]))
                    pool.tensor_tensor(tile(x0b, i), xa[:, :], R["bo2"], ALU.add).then_inc(xab_ready, 1)
                if "C" in S:
                    pool.wait_ge(z_ready["C"], i - 1)
                    pool.tensor_copy(tile(z_all, i - 2), zC[:, :]).then_inc(z_kept, 1)

            def add_row(t, first, last, row):
                return pool.tensor_tensor(t[:, first:last, :], t[:, first:last, :],
                                          R[row].unsqueeze(1).broadcast_to([P, last - first, D]), ALU.add)

            iteration(-1, streams(-1))
            pool.wait_ge(ld_rows, 32)
            pool.wait_ge(pre_dve, PRE_Z1)
            add_row(x0b, 0, FIRST_TILES, "bo1").then_inc(rows_added, 1)
            iteration(0, streams(0))
            pool.wait_ge(pre_dve, PRE_ALL)
            add_row(x0b, FIRST_TILES, B, "bo1").then_inc(rows_added, 1)
            add_row(x_sb, 0, B, "ffb2").then_inc(rows_added, 1)
            pool.wait_ge(rows_added, 3)
            for i in range(1, FIRST_LOOPED):
                iteration(i, streams(i))
            with pool.Fori(FIRST_LOOPED, B - 1) as i:
                iteration(i, set("ABCN"))
            for i in range(B - 1, B + 2):
                iteration(i, streams(i))

            def scatter(x, picks, dst):
                pool.wait_ge(zeroed, 64)
                pool.wait_ge(routed[x], 1)
                for b in range(B):
                    for k, slots in enumerate(picks):
                        pool.indirect_dma_start(dst, bass.IndirectOffsetOnAxis(ap=slots[:, b:b + 1], axis=0),
                                                sent[k][:, b, 0:ROW], None).then_inc(scattered[x], 16)

            def stand():
                pool.sem_inc(fence_pool, 1)

            def send_back(x, dst):
                def step(q, u):
                    n = NSLOT * q + u
                    m, r = n + 2, (u + 2) % NSLOT
                    if exists(m, NBLK[x]):
                        pool.wait_ge(blk_in[x][r], 16 * (q + 1 + (u + 2) // NSLOT))
                        stand()
                        pool.tensor_copy(meta[:, bass.ds(m, 1), :].rearrange("p a n -> p (a n)"),
                                         blk_x[:, r, D:ROW]).then_inc(meta_kept[x], 1)
                    m, r = n - 1, (u - 1) % NSLOT
                    if exists(m, NBLK[x]):
                        pool.wait_ge(meta_kept[x], m + 1)
                        from_one(pool, returned[x][r], 16 * (q - (u == 0)))
                        stand()
                        pool.tensor_copy(dest[:, r:r + 1], meta[:, bass.ds(m, 1), 0:1].rearrange("p a n -> p (a n)")).then_inc(
                            dest_ready[x], 1)
                        pool.wait_ge(dest_ready[x], m + 1)
                        pool.wait_ge(y_ready[x], m + 1)
                        stand()
                        pool.indirect_dma_start(dst, bass.IndirectOffsetOnAxis(ap=dest[:, r:r + 1], axis=0),
                                                blk_y[:, r, :], None).then_inc(returned[x][r], 16)

                skewed(pool, NBLK[x], step)

            first_phase_over(pool)
            pool.wait_ge(ld_slot, 48)
            for k in range(2):
                pool.tensor_copy(sent[k][:, :, 0:D], z_all[:, :, :]).then_inc(sent_ready, 1)
                pool.tensor_copy(sent[k][:, :, D], tok_ids[:, k, :]).then_inc(sent_ready, 1)
            pool.wait_ge(sent_ready, 4)
            scatter("a", (slot1, slot2), rows_a)
            send_back("a", back_a)

            def group(t, g):
                return t[:, 4 * g:4 * g + 4, :]

            pool.wait_ge(ld_cond, 16)
            for g in range(G):
                ins = pool.tensor_tensor(group(cb2, g), group(cb2, g), R["b2"].unsqueeze(1).broadcast_to([P, 4, D]), ALU.add)
            ins.then_inc(filled_rows, 1)
            pool.wait_ge(filled_rows, 1)
            for k in range(2):
                for g in LANES[1]:
                    pool.wait_ge(came_back[g], 16)
                    pool.tensor_tensor(group(x_sb, g), group(x_sb, g), picked[:, 4 * g:4 * g + 4, k, :],
                                       ALU.add).then_inc(x2_by_pool, 1)
                pool.wait_ge(x2_by_pool, 2 * k + 2)
            with pool.Fori(0, SLOT_ITERS) as it:
                for g in range(G):
                    pool.wait_ge(S_ready, it * G + g + 1)
                    pool.tensor_tensor(group(s_rest, g), group(S, g), R["bu"].unsqueeze(1).broadcast_to([P, 4, D]),
                                       ALU.add).then_inc(S_rest, 1)
                for g in range(G):
                    pool.wait_ge(mid_ready, it * G + g + 1)
                    pool.tensor_tensor(group(s_rest, g), group(S, g), group(cb2, g), ALU.add).then_inc(mid_rest, 1)
            pool.wait_ge(scattered["a"], 16 * 2 * B)
            pool.tensor_copy(sent[0][:, :, D], tok_ids[:, 2, :]).then_inc(sent_ready, 1)
            pool.wait_ge(sent_ready, 5)
            pool.wait_ge(z3_ready, G - 1)
            pool.wait_ge(normed_by_dve, SLOT_ITERS + 1)
            scatter("b", (slot1,), rows_b)
            send_back("b", back_b)


def layout(I):
    import numpy as np

    arr = {
        "x": I["x"], "ctx": I["ctx_1024"], "cond_t": I["cond_1024"].T,
        "norm_w": np.stack([I[f"L0_xcond_norm{n}_w"] for n in (1, 2, 3)]),
        "eye": np.eye(P, dtype=np.float32),
        "att_w": np.stack([[I[f"L0_xcond_attn{a}_w{j}"] for j in "qkv"] for a in (1, 2)]),
        "att_wo": np.stack([I[f"L0_xcond_attn{a}_wo"] for a in (1, 2)]),
        "ff_w1": I["L0_xcond_ff_w1"], "ff_w2": I["L0_xcond_ff_w2"],
        "wr_t": I["L0_ffn_wr"].T,
    }
    col_list = [I[f"L0_xcond_norm{n}_b"].reshape(2, D) for n in (1, 2, 3)]
    col_list += [I["L0_xcond_ff_b1"].reshape(2 * FF // P, P)]
    col_list += [I[f"L1_xcond_{n}"].reshape(1, D) for n in ("lnkv_g", "lnkv_b", "lnq_g", "lnq_b", "lnm_g", "lnm_b", "bk", "bq", "b1", "bv")]
    arr["cols"] = np.concatenate(col_list).T
    arr["gate_up"] = np.concatenate([np.concatenate([I["L0_ffn_rg"], I["L0_ffn_ru"]], 1),
                                     np.concatenate([I["L0_ffn_sg"], I["L0_ffn_su"]], 0)[None]]).transpose(2, 0, 1)
    downs = np.concatenate([I["L0_ffn_rd"], I["L0_ffn_sd"][None]]).transpose(0, 2, 1)
    downs = np.concatenate([downs, np.zeros((EA + 1, CA * P - IA, D), np.float32)], 1)
    arr["down"] = downs.reshape(EA + 1, CA, P, D).transpose(2, 0, 1, 3)
    arr["tri"] = np.triu(np.ones((P, P), np.float32), 1)
    arr["wgate"] = I["L1_ffn_w_gate"]
    arr["slot_w"] = np.stack([I["L1_xcond_wk"], I["L1_xcond_wv"], I["L1_xcond_wq"].T, I["L1_xcond_wu"],
                              I["L1_xcond_w1"], I["L1_xcond_w2"]])
    arr["cond"] = I["cond_1024"]
    arr["w1b"], arr["w2b"] = I["L1_ffn_W1"], I["L1_ffn_W2"]
    arr["b12"] = np.concatenate([I["L1_ffn_b1"].reshape(-1), I["L1_ffn_b2"].reshape(-1)])
    token = np.arange(B)[None, :] * P + np.arange(P)[:, None]
    arr["tok_ids"] = np.stack([2 * token, 2 * token + 1, token], 1).astype(np.float32)
    pad = np.arange(NR * P, dtype=np.float32)[:, None]
    arr["pad_a"], arr["pad_b"] = (np.concatenate([n + pad[:m * P], 0 * pad[:m * P]], 1) for n, m in ((2 * TOK, NR), (TOK, NB)))
    shape_rows = {"iota": np.arange(EB), "iota100": np.arange(EB) + 100, "edges": np.arange(B) * P, "blocks": np.arange(NR)}
    rows = [("bo1", "L0_xcond_attn1_bo"), ("bo2", "L0_xcond_attn2_bo"), ("ffb2", "L0_xcond_ff_b2"), ("rb", "L0_ffn_rb")]
    rows += [(n, "L1_xcond_" + n) for n in ("q_mu", "q_logsig", "bu", "b2", "lnp_g", "lnp_b")] + [("b_gate", "L1_ffn_b_gate")]
    arr["rows"] = np.concatenate([I[k].reshape(-1) for _, k in rows] + [v.astype(np.float32) for v in shape_rows.values()])
    names = [(n, I[k].size) for n, k in rows] + [(n, v.size) for n, v in shape_rows.items()]
    return {k: np.ascontiguousarray(v) for k, v in arr.items()}, names


def kernel(**inputs):
    import numpy as np
    import concourse.bacc as bacc
    from concourse.bass_utils import run_bass_kernel_spmd

    arrays, row_names = layout({k: np.asarray(v) for k, v in inputs.items()})
    nc = bacc.Bacc("TRN2", target_bir_lowering=False, num_devices=1)
    args = {k: nc.dram_tensor(k, a.shape, mybir.dt.from_np(a.dtype), kind="ExternalInput").ap() for k, a in arrays.items()}
    out = nc.dram_tensor("out", (B, P, D), F32, kind="ExternalOutput").ap()
    program(nc, args, row_names, out)
    r = run_bass_kernel_spmd(nc, [arrays], core_ids=[0])
    return r.results[0]["out"]
```
